# Optimizing a Trainium2 kernel written in Bass

```python
import numpy as np
import jax
import jax.numpy as jnp

def _softmax(x, axis=-1):
    return jax.nn.softmax(x, axis=axis)

def _gelu(x):
    return jax.nn.gelu(x, approximate=True)

def _silu(x):
    return jax.nn.silu(x)

def _sigmoid(x):
    return jax.nn.sigmoid(x)

def _layernorm(x, axis=-1, eps=1e-05):
    m = jnp.mean(x, axis=axis, keepdims=True)
    v = jnp.var(x, axis=axis, keepdims=True)
    return (x - m) / jnp.sqrt(v + eps)

def _scatter_add(tgt, idx, src, axis=0):
    return tgt.at[idx].add(src)

def _segment_sum(src, seg, n):
    return jax.ops.segment_sum(src, seg, n)
kernel_name = 'mk_gnn_preln_d2_gnn_r16_51bd5f'

def setup_inputs(seed: int=0):
    np.random.seed(seed)
    _w = jnp.asarray

    def _rec_inputs():
        import jax
        import jax.numpy as jnp
        _gk = jax.random.key(seed)
        x = -0.0005121 + 1.001 * jax.random.normal(jax.random.fold_in(_gk, 1), (6250, 128), jnp.float32)
        src = jax.random.randint(jax.random.fold_in(_gk, 2), (100000,), 0, 6250, jnp.int32)
        dst = jnp.minimum((6250 * jax.random.uniform(jax.random.fold_in(_gk, 3), (100000,)) ** 2.0).astype(jnp.int32), 99999)
        _o = jnp.argsort(dst, stable=True)
        src = src[_o]
        dst = dst[_o]
        return (x, src, dst)
    x, src, dst = _rec_inputs()

    def _L0_gnn_setup():
        import jax, jax.numpy as jnp
        import numpy as np
        N = 25000
        E = 25000
        D = 128
        H = 3
        NEG_SLOPE = 0.2
        BN_EPS = 1e-05

        def _gatv2(x, edge_index, Wl, bl, Wr, br, att, bias):
            n = x.shape[0]
            h, d = att.shape
            loops = jnp.arange(n)
            src = jnp.concatenate([edge_index[0], loops])
            dst = jnp.concatenate([edge_index[1], loops])
            xl = (x @ Wl + bl).reshape(n, h, d)
            xr = (x @ Wr + br).reshape(n, h, d)
            e = jax.nn.leaky_relu(xl[src] + xr[dst], NEG_SLOPE)
            score = jnp.einsum('ehd,hd->eh', e, att)
            m = jax.ops.segment_max(score, dst, num_segments=n)
            ex = jnp.exp(score - m[dst])
            denom = jax.ops.segment_sum(ex, dst, num_segments=n)
            alpha = ex / denom[dst]
            out = jax.ops.segment_sum(alpha[:, :, None] * xl[src], dst, num_segments=n)
            return out.reshape(n, h * d) + bias

        def _batchnorm(x, gamma, beta):
            mu = jnp.mean(x, axis=0)
            var = jnp.var(x, axis=0)
            return gamma * (x - mu) * jax.lax.rsqrt(var + BN_EPS) + beta
        key = jax.random.key(seed)
        ks = iter(jax.random.split(key, 32))
        s = 0.1
        p = {}
        p['x'] = jax.random.normal(next(ks), (N, D), jnp.float32)
        p['edge_index'] = jax.random.randint(next(ks), (2, E), 0, N, jnp.int64)
        for i in (1, 2):
            p[f'Wl{i}'] = s * jax.random.normal(next(ks), (D, H * D), jnp.float32)
            p[f'bl{i}'] = jnp.zeros((H * D,), jnp.float32)
            p[f'Wr{i}'] = s * jax.random.normal(next(ks), (D, H * D), jnp.float32)
            p[f'br{i}'] = jnp.zeros((H * D,), jnp.float32)
            p[f'att{i}'] = s * jax.random.normal(next(ks), (H, D), jnp.float32)
            p[f'bc{i}'] = jnp.zeros((H * D,), jnp.float32)
            p[f'g{i}'] = jnp.ones((D,), jnp.float32)
            p[f'be{i}'] = jnp.zeros((D,), jnp.float32)
        p['W1'] = s * jax.random.normal(next(ks), (H * D, D), jnp.float32)
        p['b1'] = jnp.zeros((D,), jnp.float32)
        p['W2'] = s * jax.random.normal(next(ks), (2 * H * D, D), jnp.float32)
        p['b2'] = jnp.zeros((D,), jnp.float32)
        return p
    _L0_gnn_all = _L0_gnn_setup()
    _L0_gnn_in = {k: v for k, v in _L0_gnn_all.items() if k in ('Wl1', 'bl1', 'Wr1', 'br1', 'att1', 'bc1', 'g1', 'be1', 'Wl2', 'bl2', 'Wr2', 'br2', 'att2', 'bc2', 'g2', 'be2', 'W1', 'b1', 'W2', 'b2')}
    del _L0_gnn_all

    def _L1_gnn_setup():
        import jax, jax.numpy as jnp
        import numpy as np
        N_NODES = 3125
        N_EDGES = 50000
        D_MODEL = 128
        N_HEAD = 8
        key = jax.random.key(seed)
        k1, k2, k3, k4, k5 = jax.random.split(key, 5)
        scale = 1.0 / np.sqrt(D_MODEL)
        return {'embeds': jax.random.normal(k1, (N_NODES, D_MODEL), dtype=jnp.float32), 'edge_index': jax.random.randint(k2, (2, N_EDGES), 0, N_NODES, dtype=jnp.int64), 'qTrans': jax.random.normal(k3, (D_MODEL, D_MODEL), dtype=jnp.float32) * scale, 'kTrans': jax.random.normal(k4, (D_MODEL, D_MODEL), dtype=jnp.float32) * scale, 'vTrans': jax.random.normal(k5, (D_MODEL, D_MODEL), dtype=jnp.float32) * scale, 'ln_scale': jnp.ones((D_MODEL,), dtype=jnp.float32), 'ln_bias': jnp.zeros((D_MODEL,), dtype=jnp.float32)}
    _L1_gnn_all = _L1_gnn_setup()
    _L1_gnn_in = {k: v for k, v in _L1_gnn_all.items() if k in ('qTrans', 'kTrans', 'vTrans', 'ln_scale', 'ln_bias')}
    del _L1_gnn_all
    return {'x': x, 'src': src, 'dst': dst, 'L0_gnn_Wl1': _L0_gnn_in['Wl1'], 'L0_gnn_bl1': _L0_gnn_in['bl1'], 'L0_gnn_Wr1': _L0_gnn_in['Wr1'], 'L0_gnn_br1': _L0_gnn_in['br1'], 'L0_gnn_att1': _L0_gnn_in['att1'], 'L0_gnn_bc1': _L0_gnn_in['bc1'], 'L0_gnn_g1': _L0_gnn_in['g1'], 'L0_gnn_be1': _L0_gnn_in['be1'], 'L0_gnn_Wl2': _L0_gnn_in['Wl2'], 'L0_gnn_bl2': _L0_gnn_in['bl2'], 'L0_gnn_Wr2': _L0_gnn_in['Wr2'], 'L0_gnn_br2': _L0_gnn_in['br2'], 'L0_gnn_att2': _L0_gnn_in['att2'], 'L0_gnn_bc2': _L0_gnn_in['bc2'], 'L0_gnn_g2': _L0_gnn_in['g2'], 'L0_gnn_be2': _L0_gnn_in['be2'], 'L0_gnn_W1': _L0_gnn_in['W1'], 'L0_gnn_b1': _L0_gnn_in['b1'], 'L0_gnn_W2': _L0_gnn_in['W2'], 'L0_gnn_b2': _L0_gnn_in['b2'], 'L1_gnn_qTrans': _L1_gnn_in['qTrans'], 'L1_gnn_kTrans': _L1_gnn_in['kTrans'], 'L1_gnn_vTrans': _L1_gnn_in['vTrans'], 'L1_gnn_ln_scale': _L1_gnn_in['ln_scale'], 'L1_gnn_ln_bias': _L1_gnn_in['ln_bias']}

def reference(x, src, dst, L0_gnn_Wl1, L0_gnn_bl1, L0_gnn_Wr1, L0_gnn_br1, L0_gnn_att1, L0_gnn_bc1, L0_gnn_g1, L0_gnn_be1, L0_gnn_Wl2, L0_gnn_bl2, L0_gnn_Wr2, L0_gnn_br2, L0_gnn_att2, L0_gnn_bc2, L0_gnn_g2, L0_gnn_be2, L0_gnn_W1, L0_gnn_b1, L0_gnn_W2, L0_gnn_b2, L1_gnn_qTrans, L1_gnn_kTrans, L1_gnn_vTrans, L1_gnn_ln_scale, L1_gnn_ln_bias):
    import jax
    import jax.numpy as jnp

    def _L0_gnn_ref(x, edge_index, Wl1, bl1, Wr1, br1, att1, bc1, g1, be1, Wl2, bl2, Wr2, br2, att2, bc2, g2, be2, W1, b1, W2, b2):
        import jax, jax.numpy as jnp
        import numpy as np
        N = 25000
        E = 25000
        D = 128
        H = 3
        NEG_SLOPE = 0.2
        BN_EPS = 1e-05

        def _gatv2(x, edge_index, Wl, bl, Wr, br, att, bias):
            n = x.shape[0]
            h, d = att.shape
            loops = jnp.arange(n)
            src = jnp.concatenate([edge_index[0], loops])
            dst = jnp.concatenate([edge_index[1], loops])
            xl = (x @ Wl + bl).reshape(n, h, d)
            xr = (x @ Wr + br).reshape(n, h, d)
            e = jax.nn.leaky_relu(xl[src] + xr[dst], NEG_SLOPE)
            score = jnp.einsum('ehd,hd->eh', e, att)
            m = jax.ops.segment_max(score, dst, num_segments=n)
            ex = jnp.exp(score - m[dst])
            denom = jax.ops.segment_sum(ex, dst, num_segments=n)
            alpha = ex / denom[dst]
            out = jax.ops.segment_sum(alpha[:, :, None] * xl[src], dst, num_segments=n)
            return out.reshape(n, h * d) + bias

        def _batchnorm(x, gamma, beta):
            mu = jnp.mean(x, axis=0)
            var = jnp.var(x, axis=0)
            return gamma * (x - mu) * jax.lax.rsqrt(var + BN_EPS) + beta
        x_in = _gatv2(x, edge_index, Wl1, bl1, Wr1, br1, att1, bc1)
        h = _batchnorm(x_in @ W1 + b1, g1, be1)
        h = jax.nn.relu(h)
        h2 = _gatv2(h, edge_index, Wl2, bl2, Wr2, br2, att2, bc2)
        out = jnp.concatenate([h2, x_in], axis=1) @ W2 + b2
        out = _batchnorm(out, g2, be2)
        return jax.nn.relu(out)

    def _L1_gnn_ref(embeds, edge_index, qTrans, kTrans, vTrans, ln_scale, ln_bias):
        import jax, jax.numpy as jnp
        import numpy as np
        N_NODES = 3125
        N_EDGES = 50000
        D_MODEL = 128
        N_HEAD = 8
        rows = edge_index[0]
        cols = edge_index[1]
        n, d = embeds.shape
        e = rows.shape[0]
        h = N_HEAD
        hd = d // h
        rowEmbeds = embeds[rows]
        colEmbeds = embeds[cols]
        q = (rowEmbeds @ qTrans).reshape(e, h, hd)
        k = (colEmbeds @ kTrans).reshape(e, h, hd)
        v = (colEmbeds @ vTrans).reshape(e, h, hd)
        att = jnp.einsum('ehd,ehd->eh', q, k)
        att = jnp.clip(att, -10.0, 10.0)
        expAtt = jnp.exp(att)
        attNorm = jax.ops.segment_sum(expAtt, rows, num_segments=n)[rows]
        att = expAtt / (attNorm + 1e-08)
        resEdges = (att[:, :, None] * v).reshape(e, d)
        res = jax.ops.segment_sum(resEdges, rows, num_segments=n)
        res = res + embeds
        mu = jnp.mean(res, axis=-1, keepdims=True)
        var = jnp.var(res, axis=-1, keepdims=True)
        out = (res - mu) * jax.lax.rsqrt(var + 1e-06) * ln_scale + ln_bias
        return out
    edge_index = jnp.stack([src, dst])
    h = jnp.maximum(_layernorm(x, axis=-1), 0.0)
    x = x + _L0_gnn_ref(h, edge_index, L0_gnn_Wl1, L0_gnn_bl1, L0_gnn_Wr1, L0_gnn_br1, L0_gnn_att1, L0_gnn_bc1, L0_gnn_g1, L0_gnn_be1, L0_gnn_Wl2, L0_gnn_bl2, L0_gnn_Wr2, L0_gnn_br2, L0_gnn_att2, L0_gnn_bc2, L0_gnn_g2, L0_gnn_be2, L0_gnn_W1, L0_gnn_b1, L0_gnn_W2, L0_gnn_b2)
    h = jnp.maximum(_layernorm(x, axis=-1), 0.0)
    x = x + _L1_gnn_ref(h, edge_index, L1_gnn_qTrans, L1_gnn_kTrans, L1_gnn_vTrans, L1_gnn_ln_scale, L1_gnn_ln_bias)
    return x

_drawn_inputs = setup_inputs


def setup_inputs(seed=0):
    import zlib

    import numpy as np

    out = dict(_drawn_inputs(seed))
    spreads = {'L0_gnn_bl1': (0.0, 0.39),
     'L0_gnn_br1': (0.0, 0.342),
     'L0_gnn_bc1': (0.0, 0.8),
     'L0_gnn_g1': (1.0, 0.2),
     'L0_gnn_be1': (0.0, 0.1),
     'L0_gnn_bl2': (0.0, 0.581),
     'L0_gnn_br2': (0.0, 0.531),
     'L0_gnn_bc2': (0.0, 0.8),
     'L0_gnn_g2': (1.0, 0.2),
     'L0_gnn_be2': (0.0, 0.1),
     'L0_gnn_b1': (0.0, 0.8),
     'L0_gnn_b2': (0.0, 0.8),
     'L1_gnn_ln_scale': (1.0, 0.2),
     'L1_gnn_ln_bias': (0.0, 0.1)}
    factors = {}
    for name, (base, spread) in spreads.items():
        noise = np.random.default_rng([zlib.crc32(name.encode()), seed]).standard_normal(out[name].shape)
        drawn = base * np.exp(spread * noise) if base else spread * noise
        out[name] = jnp.asarray(drawn.astype(out[name].dtype))
    for name, factor in factors.items():
        out[name] = (out[name] * factor).astype(out[name].dtype)
    return out
```

```python
from contextlib import ExitStack

import concourse.bass as bass
from concourse import mybir

F32 = mybir.dt.float32
BF16 = mybir.dt.bfloat16
I32 = mybir.dt.int32
ALU = mybir.AluOpType
ACT = mybir.ActivationFunctionType
AX_X = mybir.AxisListType.X
ds = bass.ds

P = 128
N, D = 6250, 128
E = 100000
H = 3
HD = H * D
HE = HD + H
NB = -(-N // P)
NPAD = NB * P
TAIL = N - (NB - 1) * P

EC = 125
COLS = E // EC
CU = 8
RROWS = COLS // CU

PAD_KEY = 16384
SLOTROW = 896
TG = SLOTROW // P
TILES = P * TG
SLOTS = TILES * P
G = 4
T_DST = -(-((E + N + NB * (P - 1)) // P) // (2 * G)) * 2 * G
T_SRC = -(-((E + NB * (P - 1)) // P) // (2 * G)) * 2 * G
assert max(T_DST, T_SRC) <= TILES

LH = 8
KV = 2 * D
VW = D + LH
BIG = 3.0e38
SLOPE = 0.2

NODE_W = max(NB * HE, 2 * NPAD + NB * VW)
WORK_W = 5000


class Order:

    def __init__(self, eng, sem):
        self.eng, self.sem, self.n = eng, sem, 0

    def __call__(self, ins):
        ins.then_inc(self.sem, 1)
        self.n += 1
        self.eng.wait_ge(self.sem, self.n)
        return self.n


class Carver:

    def __init__(self, area):
        self.area, self.at = area, 0

    def __call__(self, words, dtype=F32, parts=P):
        assert self.at + words <= self.area.shape[1], (self.at, words, self.area.shape)
        v = self.area[0:parts, self.at:self.at + words]
        self.at += words
        return v if dtype == F32 else v.bitcast(dtype)


class Core:

    def __init__(self, nc, ctx):
        self.nc, self.ctx = nc, ctx

        def sb(name, shape, dt):
            return ctx.enter_context(nc.sbuf_tensor(name, shape, dt))

        self.node = sb("node_area", [P, NODE_W], F32)
        self.feat = sb("feat_area", [P, 2 * NPAD + WORK_W], F32)
        self.y2 = self.feat[:, 0:NPAD]
        self.hT = self.feat[:, NPAD:2 * NPAD]
        self.work = self.feat[:, 2 * NPAD:2 * NPAD + WORK_W]
        self.wide = self.feat[:, NPAD:2 * NPAD + WORK_W]

        self.iota_f = sb("iota_f", [P, P], F32)
        self.iota_b = sb("iota_b", [P, P], BF16)
        self.part_f = sb("part_f", [P, 1], F32)
        self.tile_f = sb("tile_f", [P, TG], F32)
        self.node_i = sb("node_i", [P, NB], I32)
        self.valid = sb("valid", [P, NB], F32)
        self.ident = sb("ident", [P, P], F32)
        self.ones = sb("ones", [P, P], F32)
        self.upper = sb("upper", [P, P], F32)
        self.lower = sb("lower", [P, P], F32)

        self.pay = sb("pay", [EC, COLS, 2], I32)
        self.pos_s = sb("pos_s", [EC, COLS], I32)
        self.gather_col = sb("gather_col", [P, TILES], I32)
        self.lo_col = sb("lo_col", [P, TILES], F32)
        self.block_row = sb("block_row", [1, TILES], I32)
        self.keep_fwd = sb("keep_fwd", [P, SLOTROW], F32)
        self.keep_bwd = sb("keep_bwd", [P, SLOTROW], F32)
        self.wcol = sb("wcol", [P, TILES * H], F32)

        self.bank = [ctx.enter_context(nc.psum_tensor(f"bank{i}", [P, 512], F32)) for i in range(8)]

        def dram(name, shape, dt):
            return nc.dram_tensor(name, shape, dt, kind="Internal").ap()

        self.rec_d = dram("rec_by_dst", [SLOTS, 2], I32)
        self.rec_s = dram("rec_by_src", [SLOTS, 2], I32)
        self.lo_edge = dram("lo_edge", [E], BF16)
        self.lo_slot = dram("lo_slot", [SLOTS], BF16)
        self.block_d = dram("block_d", [TILES], I32)
        self.block_s = dram("block_s", [TILES], I32)
        self.xl = dram("xl_table", [NPAD, HE], F32)
        self.kv = dram("kv_table", [NPAD, KV], F32)
        self.spill = dram("spill", [T_DST // G, P, G * HD], F32)

        self.passing = []

    def sem(self, name):
        s = self.nc.alloc_semaphore(name)
        self.passing.append(s)
        return s

    def gather_sem(self, name):
        return self.ctx.enter_context(self.nc.semaphore(name))

    def recycle(self):
        with self.nc.Block() as block:
            @block.sync
            def _(sp):
                for s in self.passing:
                    sp.sem_clear(s)
        for s in self.passing:
            self.nc.release_semaphore(s)
        self.passing = []


def constants(k, io):
    nc = k.nc
    cut = Carver(k.node)
    row_i, part_i, tile_i = cut(P, I32), cut(1, I32), cut(TG, I32)
    fill_d, fill_s = cut(2 * SLOTROW, I32), cut(2 * SLOTROW, I32)
    node_f = cut(NB)
    made, filled, order, stored = k.sem("c_iota"), k.sem("c_fill"), k.sem("c_order"), k.sem("c_stored")
    with nc.Block() as block:
        @block.gpsimd
        def _(pool):
            nc.gpsimd.iota(row_i, pattern=[[1, P]], base=0, channel_multiplier=0).then_inc(made, 1)
            nc.gpsimd.iota(part_i, pattern=[[1, 1]], base=0, channel_multiplier=1).then_inc(made, 1)
            nc.gpsimd.iota(tile_i, pattern=[[1, TG]], base=0, channel_multiplier=TG).then_inc(made, 1)
            nc.gpsimd.iota(k.node_i[:, :], pattern=[[P, NB]], base=0, channel_multiplier=1).then_inc(made, 1)

        @block.vector
        def _(dve):
            do = Order(dve, order)
            do(nc.vector.memset(fill_d, 0))
            do(nc.vector.memset(fill_s, 0))
            nc.vector.memset(fill_d.rearrange("p (s f) -> p s f", f=2)[:, :, 1:2], PAD_KEY).then_inc(filled, 1)
            nc.vector.memset(fill_s.rearrange("p (s f) -> p s f", f=2)[:, :, 0:1], PAD_KEY).then_inc(filled, 1)
            dve.wait_ge(made, 4)
            do(nc.vector.tensor_copy(k.iota_f[:, :], row_i))
            do(nc.vector.tensor_copy(k.iota_b[:, :], row_i))
            do(nc.vector.tensor_copy(k.part_f[:, :], part_i))
            do(nc.vector.tensor_copy(k.tile_f[:, :], tile_i))
            do(nc.vector.tensor_copy(node_f, k.node_i[:, :]))
            do(nc.vector.tensor_scalar(k.valid[:, :], node_f, float(N), None, ALU.is_lt))
            do(nc.vector.tensor_scalar(k.ident[:, :], k.iota_f[:, :], k.part_f[:, 0:1], None, ALU.is_equal))
            do(nc.vector.tensor_scalar(k.upper[:, :], k.iota_f[:, :], k.part_f[:, 0:1], None, ALU.is_gt))
            do(nc.vector.tensor_scalar(k.lower[:, :], k.iota_f[:, :], k.part_f[:, 0:1], None, ALU.is_lt))
            do(nc.vector.memset(k.ones[:, :], 1.0))

        @block.sync
        def _(sp):
            sp.wait_ge(filled, 2)
            for rec, fill in ((k.rec_d, fill_d), (k.rec_s, fill_s)):
                sp.dma_start(rec.rearrange("(p s) f -> p (s f)", p=P), fill).then_inc(stored, 16)
            sp.wait_ge(stored, 32)


def sort_by_dst(k, io):
    nc = k.nc
    cut = Carver(k.node)
    raw = {"src": cut(CU * EC, I32, RROWS), "dst": cut(CU * EC, I32, RROWS)}
    rows = {"src": cut(CU * EC, F32, RROWS), "dst": cut(CU * EC, F32, RROWS)}
    lo_i = cut(CU * EC, I32, RROWS)
    lo_b = cut(CU * EC // 2, BF16, RROWS)
    key = {"src": cut(COLS, F32, EC), "dst": cut(COLS, F32, EC)}
    key_i = cut(COLS, I32, EC)
    part_i = cut(COLS, I32, EC)
    lo, hi = cut(COLS, F32, EC), cut(COLS, F32, EC)
    cnt, start, table0 = cut(NB), cut(NB), cut(NB)
    tot_i, tiles_f, tend, tbase = cut(NB, I32), cut(NB), cut(NB), cut(NB)
    self_pos = cut(NB, I32)
    self_rec = cut(2 * NB, I32).rearrange("p (b f) -> p b f", f=2)
    blk_f, blk_i = cut(TG), cut(TG, I32)
    junk = cut(NB)
    HALF = CU // 2
    oh_lo = [cut(HALF * P // 2, BF16, EC).rearrange("p (u m) -> p u m", u=HALF) for _ in range(2)]
    oh_hi = [cut(HALF * 25, BF16, EC).rearrange("p (u m) -> p u m", u=HALF) for _ in range(2)]
    key_bc = [cut(HALF * EC, I32) for _ in range(2)]
    lo_bc = [cut(HALF * EC // 2, BF16) for _ in range(2)]
    oh_loT = [cut(HALF * EC) for _ in range(2)]
    table = [cut(NB) for _ in range(2)]
    before = [cut(HALF, F32, EC) for _ in range(2)]
    peers = [cut(HALF, F32, EC) for _ in range(2)]
    slot = [cut(HALF, I32, EC) for _ in range(2)]
    rec = [cut(2 * HALF, I32, EC).rearrange("p (u f) -> p u f", f=2) for _ in range(2)]
    junk_e = [[cut(EC, F32, EC) for _ in range(HALF)] for _ in range(2)]
    junk_m = [cut(NB, F32, EC) for _ in range(HALF)]

    loaded, order, lo_ready = k.sem("k_loaded"), k.sem("k_order"), k.sem("k_lo_ready")
    rows_ready, turned, stored, keys_done = k.sem("k_rows"), k.sem("k_turned"), k.sem("k_stored"), k.sem("k_copied")
    with nc.Block() as block:
        @block.sync
        def _(sp):
            for name in ("dst", "src"):
                sp.dma_start(raw[name], io[name].rearrange("(r e) -> r e", r=RROWS)).then_inc(loaded, 16)
            sp.wait_ge(lo_ready, 1)
            sp.dma_start(k.lo_edge.rearrange("(r e) -> r e", r=RROWS), lo_b).then_inc(stored, 16)
            sp.wait_ge(stored, 16)

        @block.vector
        def _(dve):
            do = Order(dve, order)
            dve.wait_ge(loaded, 32)
            nc.vector.tensor_copy(rows["dst"], raw["dst"]).then_inc(rows_ready, 1)
            nc.vector.tensor_copy(rows["src"], raw["src"]).then_inc(rows_ready, 1)
            do(nc.vector.tensor_scalar(lo_i, raw["dst"], P - 1, None, ALU.bitwise_and))
            nc.vector.tensor_copy(lo_b, lo_i).then_inc(lo_ready, 1)
            for n, name in enumerate(("dst", "src")):
                for half in range(2):
                    dve.wait_ge(turned, 2 * n + half + 1)
                    dst = key[name].rearrange("p (r g) -> p g r", g=CU)[:, 4 * half:4 * half + 4, :]
                    do(nc.vector.tensor_copy(dst, k.bank[2 * n + half][0:EC, 0:4 * RROWS].rearrange("p (g r) -> p g r", g=4)))
            do(nc.vector.tensor_copy(k.pay[:, :, 0], key["src"]))
            do(nc.vector.tensor_copy(k.pay[:, :, 1], key["dst"]))
            do(nc.vector.tensor_copy(key_i, key["dst"]))
            do(nc.vector.tensor_scalar(part_i, key_i, P - 1, None, ALU.bitwise_and))
            do(nc.vector.tensor_copy(lo, part_i))
            do(nc.vector.tensor_scalar(part_i, key_i, 7, None, ALU.logical_shift_right))
            do(nc.vector.tensor_copy(hi, part_i))

        @block.tensor
        def _(pe):
            for n, name in enumerate(("dst", "src")):
                pe.wait_ge(rows_ready, n + 1)
                for half in range(2):
                    for g in range(4):
                        c = (4 * half + g) * EC
                        last = nc.tensor.transpose(k.bank[2 * n + half][0:EC, g * RROWS:(g + 1) * RROWS],
                                                   rows[name][:, c:c + EC], k.ident[0:RROWS, 0:RROWS])
                    last.then_inc(turned, 1)

    oh_ready = [k.sem(f"h_ready{s}") for s in range(2)]
    oh_free = [k.sem(f"h_free{s}") for s in range(2)]
    counts = k.bank[0][:, 0:NB]
    with nc.Block() as block:
        @block.vector
        def _(dve):
            with dve.Fori(0, COLS // CU) as i:
                for s in range(2):
                    dve.wait_ge(oh_free[s], i + 1)
                    for u in range(HALF):
                        c = CU * i + s * HALF + u
                        nc.vector.tensor_scalar(oh_lo[s][:, u, :], k.iota_b[0:EC, :], lo[:, ds(c, 1)], None, ALU.is_equal)
                        last = nc.vector.tensor_scalar(oh_hi[s][:, u, 0:NB], k.iota_b[0:EC, 0:NB], hi[:, ds(c, 1)],
                                                       None, ALU.is_equal)
                    last.then_inc(oh_ready[s], 1)

        @block.tensor
        def _(pe):
            nc.tensor.matmul(counts, k.ident[:, :], k.valid[:, :], start=True, stop=True)
            for s in range(2):
                pe.sem_inc(oh_free[s], 1)
            with pe.Fori(0, COLS // CU) as i:
                for s in range(2):
                    pe.wait_ge(oh_ready[s], i + 1)
                    for u in range(HALF):
                        last = nc.tensor.matmul(counts, oh_lo[s][:, u, :], oh_hi[s][:, u, 0:NB], start=False, stop=True,
                                                skip_group_check=True)
                    last.then_inc(oh_free[s], 1)

    order, cnt_ready, summed = k.sem("t_order"), k.sem("t_cnt"), k.sem("t_summed")
    blk_ready, stored, self_ready, scattered = k.sem("t_blk"), k.sem("t_stored"), k.sem("t_self"), k.gather_sem("t_scat")
    with nc.Block() as block:
        @block.vector
        def _(dve):
            do = Order(dve, order)
            nc.vector.tensor_copy(cnt, counts).then_inc(cnt_ready, 1)
            dve.wait_ge(summed, 1)
            block_tiles(k, do, k.bank[1][:, 0:NB], tot_i, tiles_f, tend, tbase, blk_f, blk_i, junk)
            nc.vector.tensor_copy(blk_i, blk_f).then_inc(blk_ready, 1)
            do(nc.vector.scalar_tensor_tensor(out=start, in0=tbase, scalar=float(P), in1=k.bank[2][:, 0:NB],
                                              op0=ALU.mult, op1=ALU.add))
            do(nc.vector.tensor_tensor(table0, start, k.valid[:, :], ALU.add))
            do(nc.vector.tensor_copy(self_rec[:, :, 0], k.node_i[:, :]))
            do(nc.vector.tensor_copy(self_rec[:, :, 1], k.node_i[:, :]))
            nc.vector.tensor_copy(self_pos, start).then_inc(self_ready, 1)

        @block.tensor
        def _(pe):
            pe.wait_ge(cnt_ready, 1)
            nc.tensor.matmul(k.bank[1][:, 0:NB], k.ones[:, :], cnt, start=True, stop=True)
            nc.tensor.matmul(k.bank[2][:, 0:NB], k.upper[:, :], cnt, start=True, stop=True).then_inc(summed, 1)

        @block.sync
        def _(sp):
            sp.wait_ge(blk_ready, 1)
            sp.dma_start(k.block_d.rearrange("(p g) -> p g", p=P), blk_i).then_inc(stored, 16)
            sp.wait_ge(stored, 16)

        @block.gpsimd
        def _(pool):
            pool.wait_ge(self_ready, 1)
            for b in range(NB):
                n = P if b < NB - 1 else TAIL
                pool.indirect_dma_start(k.rec_d, bass.IndirectOffsetOnAxis(ap=self_pos[0:n, b:b + 1], axis=0),
                                        self_rec[0:n, b, :], None).then_inc(scattered, 16)
            pool.wait_ge(scattered, 16 * NB)

    bc_ready = [k.sem(f"r_bc{s}") for s in range(2)]
    ohT_ready = [k.sem(f"r_readyT{s}") for s in range(2)]
    cols_free = [k.sem(f"r_free{s}") for s in range(2)]
    copied, looked, updated, ranked = k.sem("r_copied"), k.sem("r_looked"), k.sem("r_updated"), k.sem("r_ranked")
    slot_ready = [k.sem(f"r_slot{s}") for s in range(2)]
    written = [k.gather_sem(f"r_written{s}") for s in range(2)]
    inited, halves = k.sem("r_init"), k.sem("r_halves")
    run = k.bank[3][:, 0:NB]
    look = [k.bank[4 + u][0:EC, 0:NB] for u in range(HALF)]
    with nc.Block() as block:
        @block.sync
        def _(sp):
            with sp.Fori(0, COLS // CU) as i:
                for s in range(2):
                    sp.wait_ge(cols_free[s], i + 1)
                    at = (CU * i + s * HALF) * EC
                    sp.dma_start(key_bc[s], io["dst"][ds(at, HALF * EC)].partition_broadcast(P)).then_inc(bc_ready[s], 16)
                    sp.dma_start(lo_bc[s], k.lo_edge[ds(at, HALF * EC)].partition_broadcast(P)).then_inc(bc_ready[s], 16)

        @block.scalar
        def _(act):
            act.wait_ge(inited, 1)
            act.sem_inc(copied, 1)
            with act.Fori(0, COLS // 2) as i:
                for t in range(2):
                    c = 2 * i + t
                    act.wait_ge(updated, c + CU)
                    nc.scalar.copy(table[t], run).then_inc(copied, 1)

        @block.tensor
        def _(pe):
            nc.tensor.matmul(run, k.ident[:, :], table0, start=True, stop=True).then_inc(inited, 1)
            pe.wait_ge(inited, 1)
            pe.sem_inc(updated, CU)
            with pe.Fori(0, COLS // CU) as i:
                for s in range(2):
                    pe.wait_ge(ohT_ready[s], i + 1)
                    for u in range(HALF):
                        c = CU * i + s * HALF + u
                        pe.wait_ge(copied, c + 2)
                        pe.wait_ge(halves, c + 1)
                        nc.tensor.matmul(look[u], oh_loT[s][:, u * EC:(u + 1) * EC], table[u % 2],
                                         start=True, stop=True).then_inc(looked, 1)
                        nc.tensor.matmul(run, oh_lo[s][:, u, :], oh_hi[s][:, u, 0:NB], start=False, stop=True,
                                         skip_group_check=True).then_inc(updated, 1)

        @block.vector
        def _(dve):
            for s in range(2):
                dve.sem_inc(cols_free[s], 1)
            dve.sem_inc(halves, HALF)
            for s in range(2):
                dve.sem_inc(slot_ready[s], 1)

            def one_hots(i, s):
                dve.wait_ge(updated, CU * i + s * HALF + HALF)
                for u in range(HALF):
                    c = CU * i + s * HALF + u
                    nc.vector.tensor_scalar(oh_lo[s][:, u, :], k.iota_b[0:EC, :], lo[:, ds(c, 1)], None, ALU.is_equal)
                    nc.vector.tensor_scalar(oh_hi[s][:, u, 0:NB], k.iota_b[0:EC, 0:NB], hi[:, ds(c, 1)], None, ALU.is_equal)
                dve.wait_ge(bc_ready[s], 32 * i + 32)
                nc.vector.tensor_scalar(oh_loT[s], lo_bc[s], k.part_f[:, 0:1], None, ALU.is_equal).then_inc(ohT_ready[s], 1)
                dve.wait_ge(slot_ready[s], i + 1)
                dve.wait_ge(cols_free[s], i + 1)
                for u in range(HALF):
                    c = CU * i + s * HALF + u
                    last = nc.vector.scalar_tensor_tensor(out=junk_e[s][u], in0=key_bc[s][0:EC, u * EC:(u + 1) * EC],
                                                          scalar=key["dst"][:, ds(c, 1)], in1=k.lower[0:EC, 0:EC],
                                                          op0=ALU.is_equal, op1=ALU.mult, accum_out=peers[s][:, u:u + 1])
                last.then_inc(cols_free[s], 1)

            def slots(i, s, first=False):
                for u in range(HALF):
                    c = CU * i + s * HALF + u
                    dve.wait_ge(looked, c + 1)
                    last = nc.vector.scalar_tensor_tensor(out=junk_m[u], in0=look[u], scalar=1.0, in1=oh_hi[s][:, u, 0:NB],
                                                          op0=ALU.mult, op1=ALU.mult, accum_out=before[s][:, u:u + 1])
                    last.then_inc(halves, 1)
                dve.wait_ge(halves, CU * i + s * HALF + 2 * HALF)
                if not first:
                    dve.wait_ge(written[s], 64 * i)
                nc.vector.tensor_copy(rec[s], k.pay[:, ds(CU * i + s * HALF, HALF), :])
                nc.vector.tensor_tensor(slot[s], before[s], peers[s], ALU.add).then_inc(slot_ready[s], 1)

            one_hots(0, 0)
            one_hots(0, 1)
            slots(0, 0, first=True)
            one_hots(1, 0)
            slots(0, 1, first=True)
            with dve.Fori(1, COLS // CU - 1) as i:
                one_hots(i, 1)
                slots(i, 0)
                one_hots(i + 1, 0)
                slots(i, 1)
            one_hots(COLS // CU - 1, 1)
            slots(COLS // CU - 1, 0)
            slots(COLS // CU - 1, 1)

        @block.gpsimd
        def _(pool):
            with pool.Fori(0, COLS // CU) as i:
                for s in range(2):
                    pool.wait_ge(slot_ready[s], i + 2)
                    pool.nop(nofuse=True)
                    for u in range(HALF):
                        pool.indirect_dma_start(k.rec_d, bass.IndirectOffsetOnAxis(ap=slot[s][:, u:u + 1], axis=0),
                                                rec[s][:, u, :], None).then_inc(written[s], 16)
            for s in range(2):
                pool.wait_ge(written[s], 64 * (COLS // CU))
    return key["src"]


def block_tiles(k, do, total, tot_i, tiles_f, tend, tbase, blk_f, blk_i, junk):
    nc = k.nc
    do(nc.vector.tensor_scalar(tot_i, total, float(P - 1), None, ALU.add))
    do(nc.vector.tensor_scalar(tot_i, tot_i, 7, None, ALU.logical_shift_right))
    do(nc.vector.tensor_copy(tiles_f, tot_i))
    do(nc.vector.tensor_tensor_scan(tend, k.ones[:, 0:NB], tiles_f, 0.0, ALU.mult, ALU.add))
    do(nc.vector.tensor_tensor(tbase, tend, tiles_f, ALU.subtract))
    for g in range(TG):
        do(nc.vector.tensor_scalar(junk, tend, k.tile_f[:, g:g + 1], None, ALU.is_le, ALU.add,
                                   accum_out=blk_f[:, g:g + 1]))
    do(nc.vector.tensor_scalar(blk_f, blk_f, float(NB - 1), None, ALU.min))


def sort_by_src(k, io, src_key):
    nc = k.nc
    cut = Carver(k.feat)
    key_i, hi = cut(COLS, I32, EC), cut(COLS, F32, EC)
    oh = cut(COLS, F32, EC)
    rank = cut(COLS, F32, EC)
    acc = [cut(COLS, F32, EC) for _ in range(2)]
    lane = cut(NB, F32, EC)
    first = cut(NB, F32, EC)
    tot_i, tiles_f, tend, tbase = cut(NB, I32), cut(NB), cut(NB), cut(NB)
    blk_f, blk_i, junk = cut(TG), cut(TG, I32), cut(NB)
    order, lanes, summed, blk_ready, stored = (k.sem("s_order"), k.sem("s_lanes"), k.sem("s_summed"), k.sem("s_blk"),
                                               k.sem("s_stored"))
    scanned = k.sem("s_scanned")
    with nc.Block() as block:
        @block.vector
        def _(dve):
            do = Order(dve, order)
            do(nc.vector.tensor_copy(key_i, src_key))
            do(nc.vector.tensor_scalar(key_i, key_i, 7, None, ALU.logical_shift_right))
            do(nc.vector.tensor_copy(hi, key_i))
            for b in range(NB):
                do(nc.vector.tensor_scalar(oh, hi, float(b), None, ALU.is_equal, ALU.add, accum_out=lane[:, b:b + 1]))
            dve.sem_inc(lanes, 1)
            dve.wait_ge(summed, 1)
            block_tiles(k, do, k.bank[0][:, 0:NB], tot_i, tiles_f, tend, tbase, blk_f, blk_i, junk)
            nc.vector.tensor_copy(blk_i, blk_f).then_inc(blk_ready, 1)
            do(nc.vector.scalar_tensor_tensor(out=first, in0=tbase[0:EC, :], scalar=float(P),
                                              in1=k.bank[1][0:EC, 0:NB], op0=ALU.mult, op1=ALU.add))
            do(nc.vector.tensor_scalar(first, first, -1.0, None, ALU.add))
            do(nc.vector.memset(acc[0], 0.0))
            for b in range(NB):
                do(nc.vector.tensor_scalar(oh, hi, float(b), None, ALU.is_equal))
                do(nc.vector.tensor_tensor_scan(rank, oh, oh, first[:, b:b + 1], ALU.add, ALU.bypass))
                do(nc.vector.tensor_tensor(rank, rank, oh, ALU.mult))
                do(nc.vector.tensor_tensor(acc[(b + 1) % 2], acc[b % 2], rank, ALU.add))
            do(nc.vector.tensor_copy(k.pos_s[:, :], acc[NB % 2]))

        @block.tensor
        def _(pe):
            pe.wait_ge(lanes, 1)
            nc.tensor.matmul(k.bank[0][:, 0:NB], k.ones[0:EC, :], lane, start=True, stop=True)
            nc.tensor.matmul(k.bank[1][0:EC, 0:NB], k.upper[0:EC, 0:EC], lane, start=True, stop=True).then_inc(summed, 1)

        @block.sync
        def _(sp):
            sp.wait_ge(blk_ready, 1)
            sp.dma_start(k.block_s.rearrange("(p g) -> p g", p=P), blk_i).then_inc(stored, 16)
            sp.wait_ge(stored, 16)


def reused(j):
    return not (isinstance(j, int) and j == 0)


def pipeline(eng, groups, stages):
    ahead, behind = max(lead for lead, _ in stages), min(lead for lead, _ in stages)

    def at(half, s):
        for lead, fn in stages:
            q = s + lead
            if isinstance(half, int) and not 0 <= 2 * half + q < groups:
                continue
            fn(half + q // 2, q % 2)

    first = -(-(2 - behind) // 2)
    last = (groups - ahead) // 2
    for t in range(-ahead, 2 * first):
        at(t // 2, t % 2)
    with eng.Fori(first, last) as i:
        at(i, 0)
        at(i, 1)
    for t in range(2 * last, groups - behind):
        at(t // 2, t % 2)


def slot_tables(k, rec, block_dram, gathered, key, ends, tag):
    nc = k.nc
    cut = Carver(k.wide)
    raw = cut(2 * SLOTROW, I32)
    pair = raw.rearrange("p (s f) -> p s f", f=2)
    node_f, key_f = cut(SLOTROW), cut(SLOTROW)
    lo_i, lo_f, lo_b = cut(SLOTROW, I32), cut(SLOTROW), cut(SLOTROW // 2, BF16)
    edge_i, edge_f = cut(4, I32), cut(4)
    loaded, order, rows_ready, turned = (k.sem(f"l{tag}_loaded"), k.sem(f"l{tag}_order"), k.sem(f"l{tag}_rows"),
                                         k.sem(f"l{tag}_turned"))
    lo_ready, stored, edges_set = k.sem(f"l{tag}_lo"), k.sem(f"l{tag}_stored"), k.sem(f"l{tag}_edges")
    rec_rows = rec.rearrange("(p s) f -> p s f", p=P)
    with nc.Block() as block:
        @block.sync
        def _(sp):
            sp.dma_start(raw, rec.rearrange("(p s) f -> p (s f)", p=P)).then_inc(loaded, 16)
            sp.dma_start(k.block_row[:, :], block_dram.rearrange("(o t) -> o t", o=1)).then_inc(loaded, 16)
            if ends:
                sp.wait_ge(edges_set, 1)
                sp.dma_start(edge_i[1:P, 0:2], rec_rows[0:P - 1, SLOTROW - 1, :]).then_inc(loaded, 16)
                sp.dma_start(edge_i[0:P - 1, 2:4], rec_rows[1:P, 0, :]).then_inc(loaded, 16)
            sp.wait_ge(lo_ready, 1)
            sp.dma_start(k.lo_slot.rearrange("(p s) -> p s", p=P), lo_b).then_inc(stored, 16)
            sp.wait_ge(stored, 16)

        @block.vector
        def _(dve):
            do = Order(dve, order)
            if ends:
                nc.vector.memset(edge_i, -1).then_inc(edges_set, 1)
            dve.wait_ge(loaded, 64 if ends else 32)
            do(nc.vector.tensor_copy(node_f, pair[:, :, gathered]))
            do(nc.vector.tensor_scalar(lo_i, pair[:, :, key], PAD_KEY | (P - 1), None, ALU.bitwise_and))
            nc.vector.tensor_copy(lo_f, lo_i).then_inc(rows_ready, 1)
            nc.vector.tensor_copy(lo_b, lo_i).then_inc(lo_ready, 1)
            if ends:
                do(nc.vector.tensor_copy(key_f, pair[:, :, key]))
                do(nc.vector.tensor_copy(edge_f, edge_i))
                here, there = key_f[:, 1:SLOTROW], key_f[:, 0:SLOTROW - 1]
                do(nc.vector.tensor_tensor(k.keep_fwd[:, 1:SLOTROW], here, there, ALU.is_equal))
                do(nc.vector.tensor_tensor(k.keep_bwd[:, 0:SLOTROW - 1], here, there, ALU.is_equal))
                do(nc.vector.tensor_tensor(k.keep_fwd[:, 0:1], key_f[:, 0:1], edge_f[:, key:key + 1], ALU.is_equal))
                do(nc.vector.tensor_tensor(k.keep_bwd[:, SLOTROW - 1:SLOTROW], key_f[:, SLOTROW - 1:SLOTROW],
                                           edge_f[:, 2 + key:3 + key], ALU.is_equal))
            for n, col in enumerate((k.gather_col, k.lo_col)):
                for half, (g0, g1) in enumerate(((0, 4), (4, TG))):
                    dve.wait_ge(turned, 2 * n + half + 1)
                    out = col[:, :].rearrange("p (t g) -> p g t", g=TG)[:, g0:g1, :]
                    ps = k.bank[2 * n + half][:, 0:(g1 - g0) * P].rearrange("p (g t) -> p g t", t=P)
                    do(nc.vector.tensor_copy(out, ps))

        @block.tensor
        def _(pe):
            pe.wait_ge(rows_ready, 1)
            for n, rows in enumerate((node_f, lo_f)):
                for half, (g0, g1) in enumerate(((0, 4), (4, TG))):
                    for g in range(g0, g1):
                        last = nc.tensor.transpose(k.bank[2 * n + half][:, (g - g0) * P:(g - g0 + 1) * P],
                                                   rows[:, g * P:(g + 1) * P], k.ident[:, :])
                    last.then_inc(turned, 1)


def load_nodes(sp, x, area, loaded):
    whole = (NB - 1) * P
    sp.dma_start(area[:, 0:(NB - 1) * D].rearrange("p (b d) -> p b d", d=D),
                 x[0:whole, :].rearrange("(b p) d -> p b d", p=P)).then_inc(loaded, 16)
    sp.dma_start(area[0:TAIL, (NB - 1) * D:NB * D], x[whole:N, :]).then_inc(loaded, 16)


def center(k, do, dve, x, xc, square, mean, rstd, eps, sq_ready, squared, var_ready, rooted):
    nc = k.nc
    x3 = x.rearrange("p (b d) -> p b d", d=D)
    xc3 = xc.rearrange("p (b d) -> p b d", d=D)
    do(nc.vector.tensor_reduce(mean, x3, AX_X, ALU.add))
    do(nc.vector.tensor_scalar(mean, mean, 1.0 / D, None, ALU.mult))
    nc.vector.tensor_tensor(xc3, x3, mean.unsqueeze(2).to_broadcast([P, NB, D]), ALU.subtract).then_inc(sq_ready, 1)
    dve.wait_ge(squared, 1)
    do(nc.vector.tensor_reduce(rstd, square.rearrange("p (b d) -> p b d", d=D), AX_X, ALU.add))
    nc.vector.tensor_scalar(rstd, rstd, 1.0 / D, eps, ALU.mult, ALU.add).then_inc(var_ready, 1)
    dve.wait_ge(rooted, 1)
    do(nc.vector.reciprocal(rstd, rstd))


def scale_rows(k, rows, by):
    rows3 = rows.rearrange("p (b d) -> p b d", d=D)
    return k.nc.vector.tensor_tensor(rows3, rows3, by.unsqueeze(2).to_broadcast([P, NB, D]), ALU.mult)


def norm_to_features(k, x, rows, scratch, load, tag):
    nc = k.nc
    cut = Carver(k.work)
    mean, rstd = cut(NB), cut(NB)
    stage = [cut(P) for _ in range(2)]
    names = ("loaded", "order", "sq_ready", "squared", "var", "rooted", "ready", "cleared")
    loaded, order, sq_ready, squared, var_ready, rooted, ready, cleared = (k.sem(f"n{tag}_{n}") for n in names)
    staged = [k.sem(f"n{tag}_staged{s}") for s in range(2)]
    turned = [k.sem(f"n{tag}_turned{s}") for s in range(2)]
    kept = [k.sem(f"n{tag}_kept{s}") for s in range(2)]
    with nc.Block() as block:
        if load is not None:
            @block.sync
            def _(sp):
                sp.wait_ge(cleared, 1)
                load_nodes(sp, load, x, loaded)

        @block.scalar
        def _(act):
            act.wait_ge(sq_ready, 1)
            nc.scalar.activation(scratch, rows, ACT.Square).then_inc(squared, 1)
            act.wait_ge(var_ready, 1)
            nc.scalar.activation(rstd, rstd, ACT.Sqrt).then_inc(rooted, 1)
            act.wait_ge(ready, 1)

            def relu(j, s):
                if reused(j):
                    act.wait_ge(turned[s], j)
                nc.scalar.activation(stage[s], rows[:, ds((2 * j + s) * P, P)], ACT.Relu).then_inc(staged[s], 1)

            pipeline(act, NB, [(0, relu)])

        @block.tensor
        def _(pe):
            def turn(j, s):
                pe.wait_ge(staged[s], j + 1)
                if reused(j):
                    pe.wait_ge(kept[s], j)
                nc.tensor.transpose(k.bank[s][:, 0:P], stage[s], k.ident[:, :]).then_inc(turned[s], 1)

            pipeline(pe, NB, [(0, turn)])

        @block.vector
        def _(dve):
            do = Order(dve, order)
            if load is not None:
                nc.vector.memset(x[:, (NB - 1) * D:NB * D], 0.0).then_inc(cleared, 1)
                dve.wait_ge(loaded, 32)
            center(k, do, dve, x, rows, scratch, mean, rstd, 1e-5, sq_ready, squared, var_ready, rooted)
            scale_rows(k, rows, rstd).then_inc(ready, 1)

            def keep(j, s):
                dve.wait_ge(turned[s], j + 1)
                nc.vector.tensor_copy(k.hT[:, ds((2 * j + s) * P, P)], k.bank[s][:, 0:P]).then_inc(kept[s], 1)

            pipeline(dve, NB, [(0, keep)])
            do(nc.vector.tensor_scalar(rows, rows, 0.0, None, ALU.max)) if load is None else None


def node_tables(k, gathered_w, local_ws, gather_w, local_w, table, local, bias_rows, att, tag):
    nc = k.nc
    cut = Carver(k.work)
    w = cut(gather_w + local_w)
    bias = [cut(local_w) for _ in bias_rows]
    stage = [cut(P) for _ in range(2)]
    out = [cut(gather_w) for _ in range(2)]
    att_bc = cut(HD) if att is not None else None
    loaded, order, weights_set = k.sem(f"w{tag}_loaded"), k.sem(f"w{tag}_order"), k.sem(f"w{tag}_weights")
    names = ("staged", "done", "copied", "kept", "stored")
    staged, done, copied, kept, stored = ([k.sem(f"w{tag}_{n}{s}") for s in range(2)] for n in names)
    table3 = table.rearrange("(b p) d -> b p d", p=P)
    n_loads = len(gathered_w) + len(local_ws) + len(bias_rows) + (att is not None)
    with nc.Block() as block:
        @block.sync
        def _(sp):
            for at, group in ((0, gathered_w), (gather_w, local_ws)):
                for v in group:
                    sp.dma_start(w[:, at:at + v.shape[1]], v).then_inc(loaded, 16)
                    at += v.shape[1]
            for b, v in zip(bias, bias_rows):
                sp.dma_start(b[:, 0:v.shape[0]], v.partition_broadcast(P)).then_inc(loaded, 16)
            if att is not None:
                sp.dma_start(att_bc, att.rearrange("h d -> (h d)").partition_broadcast(P)).then_inc(loaded, 16)

            def store(j, s):
                sp.wait_ge(copied[s], j + 1)
                sp.dma_start(table3[ds(2 * j + s, 1), :, :].rearrange("o p d -> (o p) d"), out[s]).then_inc(stored[s], 16)

            pipeline(sp, NB, [(0, store)])
            for s in range(2):
                sp.wait_ge(stored[s], 16 * ((NB + 1 - s) // 2))

        @block.gpsimd
        def _(pool):
            def take(j, s):
                if reused(j):
                    pool.wait_ge(done[s], j)
                    pool.nop(nofuse=True)
                nc.gpsimd.tensor_copy(stage[s], k.hT[:, ds((2 * j + s) * P, P)]).then_inc(staged[s], 1)

            pipeline(pool, NB, [(0, take)])

        @block.tensor
        def _(pe):
            pe.wait_ge(weights_set, 1)

            def products(j, s):
                pe.wait_ge(staged[s], j + 1)
                if reused(j):
                    pe.wait_ge(copied[s], j)
                    pe.wait_ge(kept[s], j)
                nc.tensor.matmul(k.bank[s][:, 0:gather_w], stage[s], w[:, 0:gather_w], start=True, stop=True)
                nc.tensor.matmul(k.bank[2 + s][:, 0:local_w], stage[s], w[:, gather_w:gather_w + local_w],
                                 start=True, stop=True).then_inc(done[s], 1)

            pipeline(pe, NB, [(0, products)])

        @block.scalar
        def _(act):
            def copy(j, s):
                act.wait_ge(done[s], j + 1)
                if reused(j):
                    act.wait_ge(stored[s], 16 * j)
                nc.scalar.copy(out[s], k.bank[s][:, 0:gather_w]).then_inc(copied[s], 1)

            pipeline(act, NB, [(0, copy)])

        @block.vector
        def _(dve):
            do = Order(dve, order)
            dve.wait_ge(loaded, 16 * n_loads)
            if bias_rows:
                do(nc.vector.tensor_tensor(bias[0][:, 0:HD], bias[0][:, 0:HD], bias[1][:, 0:HD], ALU.add))
            if att is not None:
                for v in (w[:, 0:HE], w[:, HE:2 * HE], bias[0]):
                    do(nc.vector.tensor_tensor(out[0][:, 0:HD], v[:, 0:HD], att_bc, ALU.mult))
                    do(nc.vector.tensor_reduce(v[:, HD:HE], out[0][:, 0:HD].rearrange("p (h d) -> p h d", h=H), AX_X,
                                               ALU.add))
            dve.sem_inc(weights_set, 1)

            def keep(j, s):
                dve.wait_ge(done[s], j + 1)
                to = local[:, ds((2 * j + s) * local_w, local_w)]
                if bias_rows:
                    nc.vector.tensor_tensor(to, k.bank[2 + s][:, 0:local_w], bias[0], ALU.add).then_inc(kept[s], 1)
                else:
                    nc.vector.tensor_copy(to, k.bank[2 + s][:, 0:local_w]).then_inc(kept[s], 1)

            pipeline(dve, NB, [(0, keep)])


def edge_scores(k, att, tag):
    nc = k.nc
    groups = T_DST // G
    cut = Carver(k.wide)
    xg = [cut(G * HE) for _ in range(2)]
    z = [cut(G * HE) for _ in range(2)]
    z3 = [v.rearrange("p (u e) -> p u e", u=G) for v in z]
    pick = [cut(G * P) for _ in range(2)]
    lo_bc = [cut(G * P // 2, BF16) for _ in range(2)]
    att_bc = cut(HD)
    part = [cut(G * H) for _ in range(2)]
    index = [cut(G, I32) for _ in range(2)]
    names = ("index", "spilled", "lo", "picked", "added", "rect", "scored", "weighed")
    gathered = [k.gather_sem(f"a{tag}_gathered{s}") for s in range(2)]
    index_set, spilled, lo_ready, pick_ready, added, rect, scored, weighed = (
        [k.sem(f"a{tag}_{n}{s}") for s in range(2)] for n in names)
    loaded, looked, tile_added, cleared = (k.sem(f"a{tag}_loaded"), k.sem(f"a{tag}_looked"), k.sem(f"a{tag}_tile"),
                                           k.sem(f"a{tag}_cleared"))
    with nc.Block() as block:
        @block.gpsimd
        def _(pool):
            def gather(j, s):
                if reused(j):
                    pool.wait_ge(added[s], j)
                    pool.wait_ge(spilled[s], 16 * j)
                    pool.nop(nofuse=True)
                nc.gpsimd.tensor_copy(index[s], k.gather_col[:, ds((2 * j + s) * G, G)]).then_inc(index_set[s], 1)
                pool.wait_ge(index_set[s], j + 1)
                pool.nop(nofuse=True)
                for u in range(G):
                    pool.indirect_dma_start(xg[s][:, u * HE:(u + 1) * HE], None, k.xl,
                                            bass.IndirectOffsetOnAxis(ap=index[s][:, u:u + 1], axis=0)).then_inc(gathered[s], 16)

            pipeline(pool, groups, [(0, gather)])

        @block.sync
        def _(sp):
            sp.dma_start(att_bc, att.rearrange("h d -> (h d)").partition_broadcast(P)).then_inc(loaded, 16)

            def load_lo(j, s):
                if reused(j):
                    sp.wait_ge(pick_ready[s], j)
                sp.dma_start(lo_bc[s], k.lo_slot[ds((2 * j + s) * (G * P), G * P)].partition_broadcast(P)).then_inc(lo_ready[s], 16)

            def spill(j, s):
                sp.wait_ge(gathered[s], 16 * G * j + 16 * G)
                sp.dma_start(k.spill[ds(2 * j + s, 1), :, :].rearrange("o p (u d) -> (o p) u d", u=G),
                             xg[s].rearrange("p (u e) -> p u e", u=G)[:, :, 0:HD]).then_inc(spilled[s], 16)

            pipeline(sp, groups, [(2, load_lo), (0, spill)])
            for s in range(2):
                sp.wait_ge(spilled[s], 16 * (groups // 2))

        @block.tensor
        def _(pe):
            def look(j, s):
                pe.wait_ge(pick_ready[s], j + 1)
                g = 2 * j + s
                for u in range(G):
                    b = pe.value_load(k.block_row[0:1, ds(g * G + u, 1)], min_val=0, max_val=NB - 1)
                    if reused(g):
                        pe.wait_ge(tile_added, G * g + u - G + 1)
                    nc.tensor.matmul(k.bank[u][:, 0:HE], pick[s][:, u * P:(u + 1) * P], k.node[:, ds(b * HE, HE)],
                                     start=True, stop=True).then_inc(looked, 1)

            pipeline(pe, groups, [(0, look)])

        @block.scalar
        def _(act):
            def rectify(j, s):
                act.wait_ge(added[s], j + 1)
                nc.scalar.activation(z3[s][:, :, 0:HD], z3[s][:, :, 0:HD], ACT.Relu, scale=1.0 - SLOPE).then_inc(rect[s], 1)

            pipeline(act, groups, [(0, rectify)])

        @block.vector
        def _(dve):
            nc.vector.memset(k.wcol[:, T_DST * H:TILES * H], 0.0).then_inc(cleared, 1)
            dve.wait_ge(loaded, 16)

            def picks(j, s):
                dve.wait_ge(lo_ready[s], 16 * j + 16)
                g = 2 * j + s
                if reused(j):
                    dve.wait_ge(looked, G * g - G)
                nc.vector.tensor_scalar(pick[s], lo_bc[s], k.part_f[:, 0:1], None, ALU.is_equal).then_inc(pick_ready[s], 1)

            def add(j, s):
                g = 2 * j + s
                dve.wait_ge(gathered[s], 16 * G * j + 16 * G)
                if reused(j):
                    dve.wait_ge(scored[s], j)
                for u in range(G):
                    dve.wait_ge(looked, G * g + u + 1)
                    nc.vector.tensor_tensor(z[s][:, u * HE:(u + 1) * HE], k.bank[u][:, 0:HE],
                                            xg[s][:, u * HE:(u + 1) * HE], ALU.add).then_inc(tile_added, 1)
                dve.wait_ge(tile_added, G * g + G)
                dve.sem_inc(added[s], 1)

            def score(j, s):
                dve.wait_ge(rect[s], j + 1)
                zd = z3[s][:, :, 0:HD]
                nc.vector.tensor_tensor(zd, zd, att_bc.unsqueeze(1).to_broadcast([P, G, HD]), ALU.mult).then_inc(weighed[s], 1)
                dve.wait_ge(weighed[s], 2 * j + 1)
                nc.vector.tensor_reduce(part[s].rearrange("p (u h) -> p u h", u=G),
                                        zd.rearrange("p u (h d) -> p u h d", h=H), AX_X, ALU.add).then_inc(weighed[s], 1)
                dve.wait_ge(weighed[s], 2 * j + 2)
                nc.vector.scalar_tensor_tensor(
                    out=k.wcol[:, ds((2 * j + s) * (G * H), G * H)].rearrange("p (u h) -> p u h", u=G),
                    in0=z3[s][:, :, HD:HE], scalar=SLOPE, in1=part[s].rearrange("p (u h) -> p u h", u=G),
                    op0=ALU.mult, op1=ALU.add).then_inc(scored[s], 1)

            pipeline(dve, groups, [(2, picks), (1, add), (0, score)])


def segment_softmax(k, tag):
    nc = k.nc
    W = SLOTROW
    cut = Carver(k.wide)
    s_row, fwd, bwd = cut(H * W), cut(H * W), cut(H * W)
    whole = cut(1)
    rowkeep = [cut(H) for _ in range(2)]
    ends = [cut(H) for _ in range(2)]
    init = [cut(H) for _ in range(2)]
    keepT = [cut(P, F32, H) for _ in range(2)]
    endT = [cut(P, F32, H) for _ in range(2)]
    carry = [cut(P + 1, F32, H) for _ in range(2)]
    no = [cut(W) for _ in range(2)]
    keep = [k.keep_fwd[:, :], k.keep_bwd[:, :]]
    NBLK = H * TG
    names = ("order", "turned", "in", "ends", "endsT", "carry", "carryT", "shifted", "exp", "weights", "back")
    order, turned, taken, ends_set, endsT, carry_set, carryT, shifted, exped, weights_set, back = (
        k.sem(f"b{tag}_{n}") for n in names)
    by_slot = k.wcol[:, :].rearrange("p (t g h) -> p h g t", g=TG, h=H)
    quads = [range(q, min(q + 4, NBLK)) for q in range(0, NBLK, 4)]
    along = [lambda v: v, lambda v: v[:, ::-1]]
    with nc.Block() as block:
        @block.tensor
        def _(pe):
            for q, quad in enumerate(quads):
                for n in quad:
                    last = nc.tensor.transpose(k.bank[q][:, (n - quad[0]) * P:(n - quad[0] + 1) * P],
                                               by_slot[:, n // TG, n % TG, :], k.ident[:, :])
                last.then_inc(turned, 1)
            pe.wait_ge(taken, len(quads))
            for r in range(2):
                pe.wait_ge(ends_set, r + 1)
                for d in range(2):
                    nc.tensor.transpose(k.bank[0][0:H, d * P:(d + 1) * P], ends[d], k.ident[:, :])
                    last = nc.tensor.transpose(k.bank[0][0:H, (2 + d) * P:(3 + d) * P], rowkeep[d], k.ident[:, :])
                last.then_inc(endsT, 1)
                pe.wait_ge(carry_set, r + 1)
                for d in range(2):
                    last = nc.tensor.transpose(k.bank[1][:, d * H:(d + 1) * H], carry[d][:, d:d + P], k.ident[0:H, 0:H])
                last.then_inc(carryT, 1)
            pe.wait_ge(weights_set, 1)
            for q, quad in enumerate(quads):
                for n in quad:
                    last = nc.tensor.transpose(k.bank[2 + q][:, (n - quad[0]) * P:(n - quad[0] + 1) * P],
                                               s_row[:, n * P:(n + 1) * P], k.ident[:, :])
                last.then_inc(back, 1)

        @block.scalar
        def _(act):
            act.wait_ge(shifted, 1)
            nc.scalar.activation(s_row, s_row, ACT.Exp).then_inc(exped, 1)

        @block.vector
        def _(dve):
            do = Order(dve, order)
            for q, quad in enumerate(quads):
                dve.wait_ge(turned, q + 1)
                w = len(quad) * P
                nc.vector.tensor_copy(s_row[:, quad[0] * P:quad[0] * P + w], k.bank[q][:, 0:w]).then_inc(taken, 1)
            dve.wait_ge(taken, len(quads))
            for d in range(2):
                do(nc.vector.tensor_scalar(no[d], keep[d], -1.0, BIG, ALU.add, ALU.mult))
                do(nc.vector.tensor_reduce(whole, keep[d], AX_X, ALU.min))
                do(nc.vector.tensor_copy(rowkeep[d], whole.to_broadcast([P, H])))

            def both_ways(r, gate, empty, op0, op1):
                out = (fwd, bwd)
                for d in range(2):
                    for h in range(H):
                        row = slice(h * W, (h + 1) * W)
                        nc_scan = nc.vector.tensor_tensor_scan(along[d](out[d][:, row]), along[d](gate[d]),
                                                               along[d](s_row[:, row]), empty, op0, op1)
                        do(nc_scan)
                        end = h * W + (W - 1 if d == 0 else 0)
                        do(nc.vector.tensor_copy(ends[d][:, h:h + 1], out[d][:, end:end + 1]))
                dve.sem_inc(ends_set, 1)
                dve.wait_ge(endsT, r + 1)
                for d in range(2):
                    do(nc.vector.tensor_copy(endT[d], k.bank[0][0:H, d * P:(d + 1) * P]))
                    do(nc.vector.tensor_copy(keepT[d], k.bank[0][0:H, (2 + d) * P:(3 + d) * P]))
                    if r == 0:
                        do(nc.vector.tensor_scalar(keepT[d], keepT[d], -1.0, BIG, ALU.add, ALU.mult))
                    do(nc.vector.memset(carry[d], empty))
                    do(nc.vector.tensor_tensor_scan(along[d](carry[d][:, 1 - d:1 - d + P]), along[d](keepT[d]),
                                                    along[d](endT[d]), empty, op0, op1))
                dve.sem_inc(carry_set, 1)
                dve.wait_ge(carryT, r + 1)
                for d in range(2):
                    do(nc.vector.tensor_copy(init[d], k.bank[1][:, d * H:(d + 1) * H]))
                    for h in range(H):
                        row = slice(h * W, (h + 1) * W)
                        do(nc.vector.tensor_tensor_scan(along[d](out[d][:, row]), along[d](gate[d]),
                                                        along[d](s_row[:, row]), init[d][:, h:h + 1], op0, op1))

            both_ways(0, no, -BIG, ALU.add, ALU.max)
            do(nc.vector.tensor_tensor(fwd, fwd, bwd, ALU.max))
            nc.vector.tensor_tensor(s_row, s_row, fwd, ALU.subtract).then_inc(shifted, 1)
            dve.wait_ge(exped, 1)
            both_ways(1, keep, 0.0, ALU.mult, ALU.add)
            do(nc.vector.tensor_tensor(bwd, bwd, s_row, ALU.subtract))
            do(nc.vector.tensor_tensor(fwd, fwd, bwd, ALU.add))
            do(nc.vector.reciprocal(fwd, fwd))
            nc.vector.tensor_tensor(s_row, s_row, fwd, ALU.mult).then_inc(weights_set, 1)
            for q, quad in enumerate(quads):
                dve.wait_ge(back, q + 1)
                for n in quad:
                    last = nc.vector.tensor_copy(by_slot[:, n // TG, n % TG, :],
                                                 k.bank[2 + q][:, (n - quad[0]) * P:(n - quad[0] + 1) * P])
            do(last)


def aggregate(k, scatter_src, tag):
    nc = k.nc
    groups = T_DST // G
    cut = Carver(k.wide)
    xg = [cut(G * HD) for _ in range(2)]
    wpick = [cut(G * HD) for _ in range(2)]
    rec = [cut(2 * CU, I32, EC).rearrange("p (u f) -> p u f", f=2) for _ in range(2)]
    slot = [cut(CU, I32, EC) for _ in range(2)]
    written = [k.gather_sem(f"g{tag}_written{s}") for s in range(2)]
    names = ("loaded", "picked", "used", "rec")
    loaded, pick_ready, used, rec_set = ([k.sem(f"g{tag}_{n}{s}") for s in range(2)] for n in names)
    cleared, summed, added = k.sem(f"g{tag}_cleared"), k.sem(f"g{tag}_summed"), k.sem(f"g{tag}_added")
    with nc.Block() as block:
        if scatter_src:
            @block.gpsimd
            def _(pool):
                def scatter(j, s):
                    if reused(j):
                        pool.wait_ge(written[s], 16 * CU * j)
                        pool.nop(nofuse=True)
                    at = (2 * j + s) * CU
                    nc.gpsimd.tensor_copy(rec[s], k.pay[:, ds(at, CU), :]).then_inc(rec_set[s], 1)
                    nc.gpsimd.tensor_copy(slot[s], k.pos_s[:, ds(at, CU)]).then_inc(rec_set[s], 1)
                    pool.wait_ge(rec_set[s], 2 * j + 2)
                    pool.nop(nofuse=True)
                    for u in range(CU):
                        pool.indirect_dma_start(k.rec_s, bass.IndirectOffsetOnAxis(ap=slot[s][:, u:u + 1], axis=0),
                                                rec[s][:, u, :], None).then_inc(written[s], 16)

                pipeline(pool, COLS // CU, [(0, scatter)])
                for s in range(2):
                    pool.wait_ge(written[s], 16 * CU * (COLS // CU // 2))

        @block.sync
        def _(sp):
            def load(j, s):
                if reused(j):
                    sp.wait_ge(used[s], j)
                sp.dma_start(xg[s], k.spill[ds(2 * j + s, 1), :, :].rearrange("o p d -> (o p) d")).then_inc(loaded[s], 16)

            pipeline(sp, groups, [(0, load)])

        @block.tensor
        def _(pe):
            def sums(j, s):
                g = 2 * j + s
                pe.wait_ge(loaded[s], 16 * j + 16)
                pe.wait_ge(pick_ready[s], j + 1)
                for u in range(G):
                    if reused(g):
                        pe.wait_ge(added, G * g + u - G + 1)
                    for h in range(H):
                        at = (u * H + h) * P
                        last = nc.tensor.matmul(k.bank[u][:, h * D:(h + 1) * D], wpick[s][:, at:at + P], xg[s][:, at:at + P],
                                                start=True, stop=True)
                    last.then_inc(summed, 1)
                pe.wait_ge(summed, G * g + G)
                pe.sem_inc(used[s], 1)

            pipeline(pe, groups, [(0, sums)])

        @block.vector
        def _(dve):
            nc.vector.memset(k.node[:, 0:NB * HD], 0.0).then_inc(cleared, 1)
            dve.wait_ge(cleared, 1)

            def picks(j, s):
                if reused(j):
                    dve.wait_ge(used[s], j)
                for u in range(G):
                    t = (2 * j + s) * G + u
                    for h in range(H):
                        at = (u * H + h) * P
                        last = nc.vector.tensor_scalar(wpick[s][:, at:at + P], k.iota_f[:, :], k.lo_col[:, ds(t, 1)],
                                                       k.wcol[:, ds(t * H + h, 1)], ALU.is_equal, ALU.mult)
                last.then_inc(pick_ready[s], 1)

            def add(j, s):
                g = 2 * j + s
                for u in range(G):
                    b = dve.value_load(k.block_row[0:1, ds(g * G + u, 1)], min_val=0, max_val=NB - 1)
                    dve.wait_ge(summed, G * g + u + 1)
                    if not (u == 0 and not reused(g)):
                        dve.wait_ge(added, G * g + u)
                    acc = k.node[:, ds(b * HD, HD)]
                    nc.vector.tensor_tensor(acc, acc, k.bank[u][:, 0:HD], ALU.add).then_inc(added, 1)

            pipeline(dve, groups, [(1, picks), (0, add)])


def load_cols(nc, sp, cols, sources, loaded):
    with nc.allow_non_contiguous_dma(reason="one word per partition"):
        for n, v in enumerate(sources):
            sp.dma_start(cols[:, n:n + 1], v.rearrange("(p o) -> p o", o=1)).then_inc(loaded, 16)


def node_layer(k, row_biases, mats, outs, tag):
    nc = k.nc
    cut = Carver(k.work)
    M = len(mats)
    bias = [cut(HD) for _ in row_biases]
    w = cut(M * HD)
    col = cut(M)
    rows = [cut(HD) for _ in range(2)]
    turned_rows = [cut(HD) for _ in range(2)]
    loaded, order = k.sem(f"m{tag}_loaded"), k.sem(f"m{tag}_order")
    names = ("rows", "turned", "copied", "done", "kept")
    rows_set, turned, copied, done, kept = ([k.sem(f"m{tag}_{n}{s}") for s in range(2)] for n in names)
    col_biases = [v for _, v, _ in outs if v is not None]
    n_loads = M + len(row_biases) + len(col_biases)
    with nc.Block() as block:
        @block.sync
        def _(sp):
            for b, v in zip(bias, row_biases):
                sp.dma_start(b, v.partition_broadcast(P)).then_inc(loaded, 16)
            for m, v in enumerate(mats):
                sp.dma_start(w[:, m * HD:(m + 1) * HD].rearrange("p (h n) -> p h n", h=H),
                             v.rearrange("(h p) n -> p h n", p=P)).then_inc(loaded, 16)
            load_cols(nc, sp, col, col_biases, loaded)

        @block.tensor
        def _(pe):
            pe.wait_ge(loaded, 16 * n_loads)

            def turn(j, s):
                pe.wait_ge(rows_set[s], j + 1)
                if reused(j):
                    pe.wait_ge(copied[s], j)
                for h in range(H):
                    last = nc.tensor.transpose(k.bank[s][:, h * P:(h + 1) * P], rows[s][:, h * P:(h + 1) * P], k.ident[:, :])
                last.then_inc(turned[s], 1)

            def products(j, s):
                pe.wait_ge(copied[s], j + 1)
                if reused(j):
                    pe.wait_ge(kept[s], j)
                for m in range(M):
                    for h in range(H):
                        last = nc.tensor.matmul(k.bank[2 + s][:, m * P:(m + 1) * P], w[:, (m * H + h) * P:(m * H + h + 1) * P],
                                                turned_rows[s][:, h * P:(h + 1) * P], start=(h == 0), stop=(h == H - 1))
                last.then_inc(done[s], 1)

            pipeline(pe, NB, [(1, turn), (0, products)])

        @block.scalar
        def _(act):
            def copy(j, s):
                act.wait_ge(turned[s], j + 1)
                if reused(j):
                    act.wait_ge(done[s], j)
                nc.scalar.copy(turned_rows[s], k.bank[s][:, 0:HD]).then_inc(copied[s], 1)

            pipeline(act, NB, [(0, copy)])

        @block.vector
        def _(dve):
            do = Order(dve, order)
            dve.wait_ge(loaded, 16 * n_loads)
            do(nc.vector.tensor_tensor(bias[0], bias[0], bias[1], ALU.add))

            def biased(j, s):
                if reused(j):
                    dve.wait_ge(turned[s], j)
                nc.vector.tensor_tensor(rows[s], k.node[:, ds((2 * j + s) * HD, HD)], bias[0], ALU.add).then_inc(rows_set[s], 1)

            def keep(j, s):
                dve.wait_ge(done[s], j + 1)
                c = 0
                for m, (area, v, adds) in enumerate(outs):
                    to = area[:, ds((2 * j + s) * P, P)]
                    ps = k.bank[2 + s][:, m * P:(m + 1) * P]
                    if adds:
                        last = nc.vector.tensor_tensor(to, to, ps, ALU.add)
                    else:
                        last = nc.vector.tensor_scalar(to, ps, col[:, c:c + 1], None, ALU.add)
                        c += 1
                last.then_inc(kept[s], 1)

            pipeline(dve, NB, [(2, biased), (0, keep)])


def batch_norm(k, y, gamma, beta, scale, shift, tag):
    nc = k.nc
    cut = Carver(k.work[:, 0:400])
    CH = 250
    stats, agg, cols = cut(N // CH * 6), cut(2), cut(2)
    assert N % CH == 0
    loaded, order, rooted, var_set = (k.sem(f"v{tag}_{n}") for n in ("loaded", "order", "rooted", "var"))
    with nc.Block() as block:
        @block.sync
        def _(sp):
            load_cols(nc, sp, cols, (gamma, beta), loaded)

        @block.scalar
        def _(act):
            act.wait_ge(var_set, 1)
            nc.scalar.activation(scale, scale, ACT.Sqrt).then_inc(rooted, 1)

        @block.vector
        def _(dve):
            do = Order(dve, order)
            for c in range(N // CH):
                last = nc.vector.bn_stats(stats[:, 6 * c:6 * c + 6], y[:, c * CH:(c + 1) * CH])
            do(last)
            do(nc.vector.bn_aggr(agg, stats))
            nc.vector.tensor_scalar(scale, agg[:, 1:2], 1e-5, None, ALU.add).then_inc(var_set, 1)
            dve.wait_ge(rooted, 1)
            do(nc.vector.reciprocal(scale, scale))
            dve.wait_ge(loaded, 32)
            do(nc.vector.tensor_tensor(scale, scale, cols[:, 0:1], ALU.mult))
            do(nc.vector.tensor_tensor(shift, agg[:, 0:1], scale, ALU.mult))
            do(nc.vector.tensor_tensor(shift, cols[:, 1:2], shift, ALU.subtract))


def gat_layer(k, io, n):
    w = {m: io[f"L0_gnn_{m}{n}"] for m in ("Wl", "Wr", "bl", "br", "att")}
    node_tables(k, (w["Wl"],), (w["Wr"],), HE, HE, k.xl, k.node, (w["bl"], w["br"]), w["att"], f"{n}")
    edge_scores(k, w["att"], n)
    segment_softmax(k, n)
    aggregate(k, n == 1, n)


def relu_in_place(k, scale, shift, tag):
    nc = k.nc
    done = k.sem(f"u{tag}_done")
    with nc.Block() as block:
        @block.scalar
        def _(act):
            nc.scalar.activation(k.hT, k.hT, ACT.Relu, bias=shift, scale=scale).then_inc(done, 1)
            act.wait_ge(done, 1)


def residual_rows(k, io, scale, shift):
    nc = k.nc
    cut = Carver(k.work)
    stage = [cut(P) for _ in range(2)]
    xr = k.hT
    loaded, cleared = k.sem("e_loaded"), k.sem("e_cleared")
    staged, turned, kept = ([k.sem(f"e_{n}{s}") for s in range(2)] for n in ("staged", "turned", "kept"))
    with nc.Block() as block:
        @block.sync
        def _(sp):
            sp.wait_ge(cleared, 1)
            load_nodes(sp, io["x"], xr, loaded)

        @block.scalar
        def _(act):
            def relu(j, s):
                if reused(j):
                    act.wait_ge(turned[s], j)
                nc.scalar.activation(stage[s], k.y2[:, ds((2 * j + s) * P, P)], ACT.Relu, bias=shift,
                                     scale=scale).then_inc(staged[s], 1)

            pipeline(act, NB, [(0, relu)])

        @block.tensor
        def _(pe):
            def turn(j, s):
                pe.wait_ge(staged[s], j + 1)
                if reused(j):
                    pe.wait_ge(kept[s], j)
                nc.tensor.transpose(k.bank[s][:, 0:P], stage[s], k.ident[:, :]).then_inc(turned[s], 1)

            pipeline(pe, NB, [(0, turn)])

        @block.vector
        def _(dve):
            nc.vector.memset(xr[:, (NB - 1) * D:NB * D], 0.0).then_inc(cleared, 1)
            dve.wait_ge(loaded, 32)

            def add(j, s):
                at = ds((2 * j + s) * P, P)
                dve.wait_ge(turned[s], j + 1)
                nc.vector.tensor_tensor(k.y2[:, at], k.bank[s][:, 0:P], xr[:, at], ALU.add).then_inc(kept[s], 1)

            pipeline(dve, NB, [(0, add)])


def edge_attention(k, q_area, acc):
    nc = k.nc
    groups = T_SRC // G
    cut = Carver(k.wide)
    kv = [cut(G * KV) for _ in range(2)]
    prod = [cut(G * D) for _ in range(2)]
    pick = [cut(G * P) for _ in range(2)]
    place = [cut(G * P) for _ in range(2)]
    lo_bc = [cut(G * P // 2, BF16) for _ in range(2)]
    att = [cut(G * LH) for _ in range(2)]
    wv = [cut(G * VW) for _ in range(2)]
    index = [cut(G, I32) for _ in range(2)]
    gathered = [k.gather_sem(f"f_gathered{s}") for s in range(2)]
    names = ("index", "lo", "picked", "looked", "mult", "att", "clip", "exp", "weighed", "placed")
    index_set, lo_ready, pick_ready, looked, multiplied, att_set, clipped, exped, weighed, placed = (
        [k.sem(f"f_{n}{s}") for s in range(2)] for n in names)
    cleared, summed, added = k.sem("f_cleared"), k.sem("f_summed"), k.sem("f_added")
    with nc.Block() as block:
        @block.gpsimd
        def _(pool):
            def gather(j, s):
                if reused(j):
                    pool.wait_ge(weighed[s], j)
                    pool.nop(nofuse=True)
                nc.gpsimd.tensor_copy(index[s], k.gather_col[:, ds((2 * j + s) * G, G)]).then_inc(index_set[s], 1)
                pool.wait_ge(index_set[s], j + 1)
                pool.nop(nofuse=True)
                for u in range(G):
                    pool.indirect_dma_start(kv[s][:, u * KV:(u + 1) * KV], None, k.kv,
                                            bass.IndirectOffsetOnAxis(ap=index[s][:, u:u + 1], axis=0)).then_inc(gathered[s], 16)

            pipeline(pool, groups, [(0, gather)])

        @block.sync
        def _(sp):
            def load_lo(j, s):
                if reused(j):
                    sp.wait_ge(pick_ready[s], j)
                sp.dma_start(lo_bc[s], k.lo_slot[ds((2 * j + s) * (G * P), G * P)].partition_broadcast(P)).then_inc(lo_ready[s], 16)

            pipeline(sp, groups, [(0, load_lo)])

        @block.tensor
        def _(pe):
            def look(j, s):
                g = 2 * j + s
                pe.wait_ge(pick_ready[s], j + 1)
                if reused(j):
                    pe.wait_ge(multiplied[s], j)
                for u in range(G):
                    b = pe.value_load(k.block_row[0:1, ds(g * G + u, 1)], min_val=0, max_val=NB - 1)
                    last = nc.tensor.matmul(k.bank[s][:, u * P:(u + 1) * P], pick[s][:, u * P:(u + 1) * P],
                                            q_area[:, ds(b * D, D)], start=True, stop=True)
                last.then_inc(looked[s], 1)

            def sums(j, s):
                g = 2 * j + s
                pe.wait_ge(placed[s], j + 1)
                for u in range(G):
                    if reused(g):
                        pe.wait_ge(added, G * g + u - G + 1)
                    nc.tensor.matmul(k.bank[2 + u][:, 0:VW], place[s][:, u * P:(u + 1) * P], wv[s][:, u * VW:(u + 1) * VW],
                                     start=True, stop=True).then_inc(summed, 1)

            pipeline(pe, groups, [(2, look), (0, sums)])

        @block.scalar
        def _(act):
            def weights(j, s):
                act.wait_ge(clipped[s], j + 1)
                if reused(j):
                    act.wait_ge(summed, G * (2 * j + s) - G)
                nc.scalar.activation(wv[s].rearrange("p (u w) -> p u w", u=G)[:, :, D:VW],
                                     att[s].rearrange("p (u h) -> p u h", u=G), ACT.Exp).then_inc(exped[s], 1)

            pipeline(act, groups, [(0, weights)])

        @block.vector
        def _(dve):
            nc.vector.memset(acc, 0.0).then_inc(cleared, 1)
            dve.wait_ge(cleared, 1)

            def picks(j, s):
                dve.wait_ge(lo_ready[s], 16 * j + 16)
                if reused(j):
                    dve.wait_ge(looked[s], j)
                nc.vector.tensor_scalar(pick[s], lo_bc[s], k.part_f[:, 0:1], None, ALU.is_equal).then_inc(pick_ready[s], 1)

            def score(j, s):
                dve.wait_ge(gathered[s], 16 * G * j + 16 * G)
                dve.wait_ge(looked[s], j + 1)
                keys = kv[s].rearrange("p (u d) -> p u d", u=G)[:, :, 0:D]
                nc.vector.tensor_tensor(prod[s].rearrange("p (u d) -> p u d", u=G), keys,
                                        k.bank[s][:, 0:G * D].rearrange("p (u d) -> p u d", u=G),
                                        ALU.mult).then_inc(multiplied[s], 1)
                dve.wait_ge(multiplied[s], j + 1)
                if reused(j):
                    dve.wait_ge(exped[s], j)
                nc.vector.tensor_reduce(att[s], prod[s].rearrange("p (q d) -> p q d", d=D // LH), AX_X,
                                        ALU.add).then_inc(att_set[s], 1)
                dve.wait_ge(att_set[s], j + 1)
                nc.vector.tensor_scalar(att[s], att[s], -10.0, 10.0, ALU.max, ALU.min).then_inc(clipped[s], 1)

            def weigh(j, s):
                g = 2 * j + s
                if reused(j):
                    dve.wait_ge(summed, G * g - G)
                for u in range(G):
                    nc.vector.tensor_scalar(place[s][:, u * P:(u + 1) * P], k.iota_f[:, :],
                                            k.lo_col[:, ds(g * G + u, 1)], None, ALU.is_equal)
                dve.wait_ge(exped[s], j + 1)
                w4 = wv[s].rearrange("p (u w) -> p u w", u=G)
                ex = w4[:, :, D:VW].unsqueeze(3).to_broadcast([P, G, LH, D // LH])
                v4 = kv[s].rearrange("p (u d) -> p u d", u=G)[:, :, D:KV].rearrange("p u (h d) -> p u h d", h=LH)
                nc.vector.tensor_tensor(w4[:, :, 0:D].rearrange("p u (h d) -> p u h d", h=LH), v4, ex,
                                        ALU.mult).then_inc(placed[s], 1)
                dve.wait_ge(placed[s], j + 1)
                dve.sem_inc(weighed[s], 1)

            def add(j, s):
                g = 2 * j + s
                for u in range(G):
                    b = dve.value_load(k.block_row[0:1, ds(g * G + u, 1)], min_val=0, max_val=NB - 1)
                    dve.wait_ge(summed, G * g + u + 1)
                    if not (u == 0 and not reused(g)):
                        dve.wait_ge(added, G * g + u)
                    to = acc[:, ds(b * VW, VW)]
                    nc.vector.tensor_tensor(to, to, k.bank[2 + u][:, 0:VW], ALU.add).then_inc(added, 1)

            pipeline(dve, groups, [(2, picks), (1, score), (0, weigh), (-1, add)])


def finish(k, io, acc, h, x, scratch, square):
    nc = k.nc
    cut = Carver(k.work)
    mean, rstd, recip = cut(NB), cut(NB), cut(NB * LH)
    gain, bias = cut(D), cut(D)
    names = ("loaded", "order", "sq_ready", "squared", "var", "rooted", "ready", "stored")
    loaded, order, sq_ready, squared, var_ready, rooted, ready, stored = (k.sem(f"z_{n}") for n in names)
    acc3 = acc.rearrange("p (b w) -> p b w", w=VW)
    rows = scratch
    rows3 = rows.rearrange("p (b d) -> p b d", d=D)
    with nc.Block() as block:
        @block.sync
        def _(sp):
            sp.dma_start(gain, io["L1_gnn_ln_scale"].partition_broadcast(P)).then_inc(loaded, 16)
            sp.dma_start(bias, io["L1_gnn_ln_bias"].partition_broadcast(P)).then_inc(loaded, 16)
            sp.wait_ge(ready, 1)
            whole = (NB - 1) * P
            sp.dma_start(io["out"][0:whole, :].rearrange("(b p) d -> p b d", p=P),
                         rows[:, 0:(NB - 1) * D].rearrange("p (b d) -> p b d", d=D)).then_inc(stored, 16)
            sp.dma_start(io["out"][whole:N, :], rows[0:TAIL, (NB - 1) * D:NB * D]).then_inc(stored, 16)
            sp.wait_ge(stored, 32)

        @block.scalar
        def _(act):
            act.wait_ge(sq_ready, 1)
            nc.scalar.activation(square, rows, ACT.Square).then_inc(squared, 1)
            act.wait_ge(var_ready, 1)
            nc.scalar.activation(rstd, rstd, ACT.Sqrt).then_inc(rooted, 1)

        @block.vector
        def _(dve):
            do = Order(dve, order)
            r3 = recip.rearrange("p (b h) -> p b h", h=LH)
            do(nc.vector.tensor_scalar(r3, acc3[:, :, D:VW], 1e-8, None, ALU.add))
            do(nc.vector.reciprocal(recip, recip))
            do(nc.vector.tensor_tensor(rows3.rearrange("p b (h d) -> p b h d", h=LH),
                                       acc3[:, :, 0:D].rearrange("p b (h d) -> p b h d", h=LH),
                                       r3.unsqueeze(3).to_broadcast([P, NB, LH, D // LH]), ALU.mult))
            do(nc.vector.tensor_tensor(rows, rows, h, ALU.add))
            center(k, do, dve, rows, rows, square, mean, rstd, 1e-6, sq_ready, squared, var_ready, rooted)
            do(scale_rows(k, rows, rstd))
            dve.wait_ge(loaded, 32)
            do(nc.vector.tensor_tensor(rows3, rows3, gain.unsqueeze(1).to_broadcast([P, NB, D]), ALU.mult))
            do(nc.vector.tensor_tensor(rows3, rows3, bias.unsqueeze(1).to_broadcast([P, NB, D]), ALU.add))
            nc.vector.tensor_tensor(rows, rows, x, ALU.add).then_inc(ready, 1)


def program(nc, io):
    with ExitStack() as ctx:
        k = Core(nc, ctx)
        g = {n: io[f"L0_gnn_{n}"] for n in ("bl1", "bc1", "g1", "be1", "bl2", "bc2", "g2", "be2", "W1", "b1", "W2", "b2")}
        scale = ctx.enter_context(nc.sbuf_tensor("bn_scale", [P, 1], F32))
        shift = ctx.enter_context(nc.sbuf_tensor("bn_shift", [P, 1], F32))
        constants(k, io)
        src_key = sort_by_dst(k, io)
        sort_by_src(k, io, src_key)
        slot_tables(k, k.rec_d, k.block_d, 0, 1, True, "d")

        k.recycle()

        norm_to_features(k, k.y2, k.node[:, 0:NPAD], k.node[:, NPAD:2 * NPAD], io["x"], "0")
        gat_layer(k, io, 1)
        node_layer(k, (g["bl1"], g["bc1"]), (g["W1"], g["W2"][HD:2 * HD, :]),
                   ((k.hT, g["b1"], False), (k.y2, g["b2"], False)), "1")
        batch_norm(k, k.hT, g["g1"], g["be1"], scale[:, :], shift[:, :], "1")
        relu_in_place(k, scale[:, 0:1], shift[:, 0:1], "1")

        k.recycle()

        gat_layer(k, io, 2)
        node_layer(k, (g["bl2"], g["bc2"]), (g["W2"][0:HD, :],), ((k.y2, None, True),), "2")
        batch_norm(k, k.y2, g["g2"], g["be2"], scale[:, :], shift[:, :], "2")
        residual_rows(k, io, scale[:, 0:1], shift[:, 0:1])

        k.recycle()

        q_area, acc, h = k.node[:, 0:NPAD], k.node[:, NPAD:NPAD + NB * VW], k.node[:, NPAD + NB * VW:2 * NPAD + NB * VW]
        norm_to_features(k, k.y2, h, q_area, None, "3")
        node_tables(k, (io["L1_gnn_kTrans"], io["L1_gnn_vTrans"]), (io["L1_gnn_qTrans"],), KV, D, k.kv, q_area, (), None, "3")
        slot_tables(k, k.rec_s, k.block_s, 1, 0, False, "s")
        edge_attention(k, q_area, acc)
        finish(k, io, acc, h, k.y2, q_area, k.hT)


_INS = ["x", "src", "dst"] + [f"L0_gnn_{n}" for n in (
    "Wl1", "bl1", "Wr1", "br1", "att1", "bc1", "g1", "be1", "Wl2", "bl2", "Wr2", "br2", "att2", "bc2", "g2", "be2",
    "W1", "b1", "W2", "b2")] + [f"L1_gnn_{n}" for n in ("qTrans", "kTrans", "vTrans", "ln_scale", "ln_bias")]


def kernel(**inputs):
    import numpy as np
    import concourse.bacc as bacc
    from concourse.bass_utils import run_bass_kernel_spmd

    nc = bacc.Bacc("TRN2", target_bir_lowering=False, num_devices=1)
    arrays, io = {}, {}
    for name in _INS:
        a = np.ascontiguousarray(inputs[name])
        arrays[f"in_{name}"] = a
        io[name] = nc.dram_tensor(f"in_{name}", a.shape, mybir.dt.from_np(a.dtype), kind="ExternalInput").ap()
    io["out"] = nc.dram_tensor("out_0", (N, D), F32, kind="ExternalOutput").ap()
    program(nc, io)
    r = run_bass_kernel_spmd(nc, [arrays], core_ids=[0])
    return r.results[0]["out_0"]
```

```python
from contextlib import ExitStack

import concourse.bass as bass
from concourse import mybir

F32 = mybir.dt.float32
BF16 = mybir.dt.bfloat16
I32 = mybir.dt.int32
ALU = mybir.AluOpType
ACT = mybir.ActivationFunctionType
AX_X = mybir.AxisListType.X
PE, DVE = mybir.EngineType.PE, mybir.EngineType.DVE
ds = bass.ds

P = 128
N, D = 6250, 128
E = 100000
H = 3
HD = H * D
HE = HD + H
NB = -(-N // P)
NPAD = NB * P
TAIL = N - (NB - 1) * P

EC = 125
COLS = E // EC
CU = 8
RROWS = COLS // CU

PAD_KEY = 16384
SLOTROW = 896
TG = SLOTROW // P
TILES = P * TG
SLOTS = TILES * P
G = 4
GS = 2
T_DST = -(-((E + N + NB * (P - 1)) // P) // (2 * G)) * 2 * G
T_SRC = -(-((E + NB * (P - 1)) // P) // (2 * G)) * 2 * G
assert max(T_DST, T_SRC) <= TILES

LH = 8
KV = 2 * D
VW = D + LH
BIG = 3.0e38
SLOPE = 0.2

NODE_W = max(NB * HE, 2 * NPAD + NB * VW)
WORK_W = 5000


class Order:

    def __init__(self, eng, sem):
        self.eng, self.sem, self.n = eng, sem, 0

    def __call__(self, ins):
        ins.then_inc(self.sem, 1)
        self.n += 1
        self.eng.wait_ge(self.sem, self.n)
        return self.n


def later(g, n=1):
    return not isinstance(g, int) or g >= n


def reused(j):
    return later(j)


def pipeline(eng, groups, stages, unroll=2):
    ahead, behind = max(lead for lead, _ in stages), min(lead for lead, _ in stages)

    def at(turn, s):
        for lead, fn in stages:
            q = s + lead
            if isinstance(turn, int) and not 0 <= unroll * turn + q < groups:
                continue
            fn(turn + q // unroll, q % unroll)

    first = -(-(unroll - behind) // unroll)
    last = (groups - ahead) // unroll
    for t in range(-ahead, unroll * first):
        at(t // unroll, t % unroll)
    with eng.Fori(first, last) as i:
        for s in range(unroll):
            at(i, s)
    for t in range(unroll * last, groups - behind):
        at(t // unroll, t % unroll)


class Carver:

    def __init__(self, area):
        self.area, self.at = area, 0

    def __call__(self, words, dtype=F32, parts=P):
        assert self.at + words <= self.area.shape[1], (self.at, words, self.area.shape)
        v = self.area[0:parts, self.at:self.at + words]
        self.at += words
        return v if dtype == F32 else v.bitcast(dtype)


class Core:

    def __init__(self, nc, ctx):
        self.nc, self.ctx = nc, ctx

        def sb(name, shape, dt):
            return ctx.enter_context(nc.sbuf_tensor(name, shape, dt))

        self.node = sb("node_area", [P, NODE_W], F32)
        self.feat = sb("feat_area", [P, 2 * NPAD + WORK_W], F32)
        self.y2 = self.feat[:, 0:NPAD]
        self.hT = self.feat[:, NPAD:2 * NPAD]
        self.work = self.feat[:, 2 * NPAD:2 * NPAD + WORK_W]
        self.wide = self.feat[:, NPAD:2 * NPAD + WORK_W]

        self.iota_f = sb("iota_f", [P, P], F32)
        self.iota_b = sb("iota_b", [P, P], BF16)
        self.part_f = sb("part_f", [P, 1], F32)
        self.tile_f = sb("tile_f", [P, TG], F32)
        self.node_i = sb("node_i", [P, NB], I32)
        self.valid = sb("valid", [P, NB], F32)
        self.ident = sb("ident", [P, P], F32)
        self.ones = sb("ones", [P, P], F32)
        self.upper = sb("upper", [P, P], F32)
        self.lower = sb("lower", [P, P], F32)

        self.pay = sb("pay", [EC, COLS, 2], I32)
        self.pos_s = sb("pos_s", [EC, COLS], I32)
        self.gather_col = sb("gather_col", [P, TILES], I32)
        self.lo_col = sb("lo_col", [P, TILES], F32)
        self.block_row = sb("block_row", [1, TILES], I32)
        self.keep_fwd = sb("keep_fwd", [P, SLOTROW], F32)
        self.keep_bwd = sb("keep_bwd", [P, SLOTROW], F32)
        self.wcol = sb("wcol", [P, TILES * H], F32)

        self.bank = [ctx.enter_context(nc.psum_tensor(f"bank{i}", [P, 512], F32)) for i in range(8)]

        def dram(name, shape, dt):
            return nc.dram_tensor(name, shape, dt, kind="Internal").ap()

        self.rec_d = dram("rec_by_dst", [SLOTS, 2], I32)
        self.rec_s = dram("rec_by_src", [SLOTS, 2], I32)
        self.lo_edge = dram("lo_edge", [E], BF16)
        self.lo_slot = dram("lo_slot", [SLOTS], BF16)
        self.block_d = dram("block_d", [TILES], I32)
        self.block_s = dram("block_s", [TILES], I32)
        self.xl = dram("xl_table", [NPAD, HE], F32)
        self.kv = dram("kv_table", [NPAD, KV], F32)
        self.spill = dram("spill", [T_DST, P, HD], F32)

        self.passing = []

    def sem(self, name):
        s = self.nc.alloc_semaphore(name)
        self.passing.append(s)
        return s

    def gather_sem(self, name):
        return self.ctx.enter_context(self.nc.semaphore(name))

    def recycle(self):
        with self.nc.Block() as block:
            @block.sync
            def _(sp):
                for s in self.passing:
                    sp.sem_clear(s)
        for s in self.passing:
            self.nc.release_semaphore(s)
        self.passing = []


def constants(k, io):
    nc = k.nc
    cut = Carver(k.node)
    row_i, part_i, tile_i = cut(P, I32), cut(1, I32), cut(TG, I32)
    fill_d, fill_s = cut(2 * SLOTROW, I32), cut(2 * SLOTROW, I32)
    node_f = cut(NB)
    made, filled, order, stored = k.sem("c_iota"), k.sem("c_fill"), k.sem("c_order"), k.sem("c_stored")
    with nc.Block() as block:
        @block.gpsimd
        def _(pool):
            nc.gpsimd.iota(row_i, pattern=[[1, P]], base=0, channel_multiplier=0).then_inc(made, 1)
            nc.gpsimd.iota(part_i, pattern=[[1, 1]], base=0, channel_multiplier=1).then_inc(made, 1)
            nc.gpsimd.iota(tile_i, pattern=[[1, TG]], base=0, channel_multiplier=TG).then_inc(made, 1)
            nc.gpsimd.iota(k.node_i[:, :], pattern=[[P, NB]], base=0, channel_multiplier=1).then_inc(made, 1)

        @block.vector
        def _(dve):
            do = Order(dve, order)
            do(nc.vector.memset(fill_d, 0))
            do(nc.vector.memset(fill_s, 0))
            nc.vector.memset(fill_d.rearrange("p (s f) -> p s f", f=2)[:, :, 1:2], PAD_KEY).then_inc(filled, 1)
            nc.vector.memset(fill_s.rearrange("p (s f) -> p s f", f=2)[:, :, 0:1], PAD_KEY).then_inc(filled, 1)
            dve.wait_ge(made, 4)
            do(nc.vector.tensor_copy(k.iota_f[:, :], row_i))
            do(nc.vector.tensor_copy(k.iota_b[:, :], row_i))
            do(nc.vector.tensor_copy(k.part_f[:, :], part_i))
            do(nc.vector.tensor_copy(k.tile_f[:, :], tile_i))
            do(nc.vector.tensor_copy(node_f, k.node_i[:, :]))
            do(nc.vector.tensor_scalar(k.valid[:, :], node_f, float(N), None, ALU.is_lt))
            do(nc.vector.tensor_scalar(k.ident[:, :], k.iota_f[:, :], k.part_f[:, 0:1], None, ALU.is_equal))
            do(nc.vector.tensor_scalar(k.upper[:, :], k.iota_f[:, :], k.part_f[:, 0:1], None, ALU.is_gt))
            do(nc.vector.tensor_scalar(k.lower[:, :], k.iota_f[:, :], k.part_f[:, 0:1], None, ALU.is_lt))
            do(nc.vector.memset(k.ones[:, :], 1.0))

        @block.sync
        def _(sp):
            sp.wait_ge(filled, 2)
            for rec, fill in ((k.rec_d, fill_d), (k.rec_s, fill_s)):
                sp.dma_start(rec.rearrange("(p s) f -> p (s f)", p=P), fill).then_inc(stored, 16)
            sp.wait_ge(stored, 32)


def sort_by_dst(k, io, beside):
    nc = k.nc
    cut = Carver(k.node)
    raw = {"src": cut(CU * EC, I32, RROWS), "dst": cut(CU * EC, I32, RROWS)}
    rows = {"src": cut(CU * EC, F32, RROWS), "dst": cut(CU * EC, F32, RROWS)}
    lo_i = cut(CU * EC, I32, RROWS)
    lo_b = cut(CU * EC // 2, BF16, RROWS)
    key = {"src": cut(COLS, F32, EC), "dst": cut(COLS, F32, EC)}
    key_i = cut(COLS, I32, EC)
    part_i = cut(COLS, I32, EC)
    lo, hi = cut(COLS, F32, EC), cut(COLS, F32, EC)
    cnt, start, table0 = cut(NB), cut(NB), cut(NB)
    tot_i, tiles_f, tend, tbase = cut(NB, I32), cut(NB), cut(NB), cut(NB)
    self_pos = cut(NB, I32)
    self_rec = cut(2 * NB, I32).rearrange("p (b f) -> p b f", f=2)
    blk_f, blk_i = cut(TG), cut(TG, I32)
    junk = cut(NB)
    HALF = CU // 2
    oh_lo = [cut(HALF * P // 2, BF16, EC).rearrange("p (u m) -> p u m", u=HALF) for _ in range(2)]
    oh_hi = [cut(HALF * 25, BF16, EC).rearrange("p (u m) -> p u m", u=HALF) for _ in range(2)]
    key_bc = [cut(HALF * EC, I32) for _ in range(2)]
    lo_bc = [cut(HALF * EC // 2, BF16) for _ in range(2)]
    oh_loT = [cut(HALF * EC) for _ in range(2)]
    table = [cut(NB) for _ in range(2)]
    before = [cut(HALF, F32, EC) for _ in range(2)]
    peers = [cut(HALF, F32, EC) for _ in range(2)]
    pos_d = cut(COLS, I32, EC)
    slot = [cut(CU, I32, EC) for _ in range(2)]
    rec = [cut(2 * CU, I32, EC).rearrange("p (u f) -> p u f", f=2) for _ in range(2)]
    junk_e = [[cut(EC, F32, EC) for _ in range(HALF)] for _ in range(2)]
    junk_m = [cut(NB, F32, EC) for _ in range(HALF)]

    loaded, order, lo_ready = k.sem("k_loaded"), k.sem("k_order"), k.sem("k_lo_ready")
    rows_ready, turned, stored, keys_done = k.sem("k_rows"), k.sem("k_turned"), k.sem("k_stored"), k.sem("k_copied")
    with nc.Block() as block:
        @block.sync
        def _(sp):
            for name in ("dst", "src"):
                sp.dma_start(raw[name], io[name].rearrange("(r e) -> r e", r=RROWS)).then_inc(loaded, 16)
            sp.wait_ge(lo_ready, 1)
            sp.dma_start(k.lo_edge.rearrange("(r e) -> r e", r=RROWS), lo_b).then_inc(stored, 16)
            sp.wait_ge(stored, 16)

        @block.vector
        def _(dve):
            do = Order(dve, order)
            dve.wait_ge(loaded, 32)
            nc.vector.tensor_copy(rows["dst"], raw["dst"]).then_inc(rows_ready, 1)
            nc.vector.tensor_copy(rows["src"], raw["src"]).then_inc(rows_ready, 1)
            do(nc.vector.tensor_scalar(lo_i, raw["dst"], P - 1, None, ALU.bitwise_and))
            nc.vector.tensor_copy(lo_b, lo_i).then_inc(lo_ready, 1)
            for n, name in enumerate(("dst", "src")):
                for half in range(2):
                    dve.wait_ge(turned, 2 * n + half + 1)
                    dst = key[name].rearrange("p (r g) -> p g r", g=CU)[:, 4 * half:4 * half + 4, :]
                    do(nc.vector.tensor_copy(dst, k.bank[2 * n + half][0:EC, 0:4 * RROWS].rearrange("p (g r) -> p g r", g=4)))
            do(nc.vector.tensor_copy(k.pay[:, :, 0], key["src"]))
            do(nc.vector.tensor_copy(k.pay[:, :, 1], key["dst"]))
            do(nc.vector.tensor_copy(key_i, key["dst"]))
            do(nc.vector.tensor_scalar(part_i, key_i, P - 1, None, ALU.bitwise_and))
            do(nc.vector.tensor_copy(lo, part_i))
            do(nc.vector.tensor_scalar(part_i, key_i, 7, None, ALU.logical_shift_right))
            do(nc.vector.tensor_copy(hi, part_i))
            beside.src_key = key["src"]

        @block.tensor
        def _(pe):
            for n, name in enumerate(("dst", "src")):
                pe.wait_ge(rows_ready, n + 1)
                for half in range(2):
                    for g in range(4):
                        c = (4 * half + g) * EC
                        last = nc.tensor.transpose(k.bank[2 * n + half][0:EC, g * RROWS:(g + 1) * RROWS],
                                                   rows[name][:, c:c + EC], k.ident[0:RROWS, 0:RROWS])
                    last.then_inc(turned, 1)

    oh_ready = [k.sem(f"h_ready{s}") for s in range(2)]
    oh_free = [k.sem(f"h_free{s}") for s in range(2)]
    counts = k.bank[0][:, 0:NB]
    halves = COLS // HALF
    HU = 8
    with nc.Block() as block:
        @block.vector
        def _(dve):
            with dve.Fori(0, halves // HU) as i:
                for n in range(HU):
                    s = n % 2
                    dve.wait_ge(oh_free[s], HU // 2 * i + n // 2 + 1)
                    for u in range(HALF):
                        c = HU * HALF * i + n * HALF + u
                        nc.vector.tensor_scalar(oh_lo[s][:, u, :], k.iota_b[0:EC, :], lo[:, ds(c, 1)], None, ALU.is_equal)
                        last = nc.vector.tensor_scalar(oh_hi[s][:, u, 0:NB], k.iota_b[0:EC, 0:NB], hi[:, ds(c, 1)],
                                                       None, ALU.is_equal)
                    last.then_inc(oh_ready[s], 1)

        @block.tensor
        def _(pe):
            nc.tensor.matmul(counts, k.ident[:, :], k.valid[:, :], start=True, stop=True)
            for s in range(2):
                pe.sem_inc(oh_free[s], 1)
            with pe.Fori(0, halves // HU) as i:
                for n in range(HU):
                    s = n % 2
                    pe.wait_ge(oh_ready[s], HU // 2 * i + n // 2 + 1)
                    for u in range(HALF):
                        last = nc.tensor.matmul(counts, oh_lo[s][:, u, :], oh_hi[s][:, u, 0:NB], start=False, stop=True,
                                                skip_group_check=True)
                    last.then_inc(oh_free[s], 1)

    order, cnt_ready, summed = k.sem("t_order"), k.sem("t_cnt"), k.sem("t_summed")
    blk_ready, stored, self_ready, scattered = k.sem("t_blk"), k.sem("t_stored"), k.sem("t_self"), k.gather_sem("t_scat")
    with nc.Block() as block:
        @block.vector
        def _(dve):
            do = Order(dve, order)
            nc.vector.tensor_copy(cnt, counts).then_inc(cnt_ready, 1)
            dve.wait_ge(summed, 1)
            block_tiles(k, do, k.bank[1][:, 0:NB], tot_i, tiles_f, tend, tbase, blk_f, blk_i, junk)
            nc.vector.tensor_copy(blk_i, blk_f).then_inc(blk_ready, 1)
            do(nc.vector.scalar_tensor_tensor(out=start, in0=tbase, scalar=float(P), in1=k.bank[2][:, 0:NB],
                                              op0=ALU.mult, op1=ALU.add))
            do(nc.vector.tensor_tensor(table0, start, k.valid[:, :], ALU.add))
            do(nc.vector.tensor_copy(self_rec[:, :, 0], k.node_i[:, :]))
            do(nc.vector.tensor_copy(self_rec[:, :, 1], k.node_i[:, :]))
            nc.vector.tensor_copy(self_pos, start).then_inc(self_ready, 1)

        @block.tensor
        def _(pe):
            pe.wait_ge(cnt_ready, 1)
            nc.tensor.matmul(k.bank[1][:, 0:NB], k.ones[:, :], cnt, start=True, stop=True)
            nc.tensor.matmul(k.bank[2][:, 0:NB], k.upper[:, :], cnt, start=True, stop=True).then_inc(summed, 1)

        @block.sync
        def _(sp):
            sp.wait_ge(blk_ready, 1)
            sp.dma_start(k.block_d.rearrange("(p g) -> p g", p=P), blk_i).then_inc(stored, 16)
            sp.wait_ge(stored, 16)

        @block.gpsimd
        def _(pool):
            pool.wait_ge(self_ready, 1)
            for b in range(NB):
                n = P if b < NB - 1 else TAIL
                pool.indirect_dma_start(k.rec_d, bass.IndirectOffsetOnAxis(ap=self_pos[0:n, b:b + 1], axis=0),
                                        self_rec[0:n, b, :], None).then_inc(scattered, 16)
            pool.wait_ge(scattered, 16 * NB)

    bc_ready = [k.sem(f"r_bc{s}") for s in range(2)]
    written = [k.gather_sem(f"r_written{s}") for s in range(2)]
    names = ("init", "copied", "looked", "updated", "onehot", "peers", "sums", "ranked", "staged")
    inited, copied, looked, updated, ohT_ready, peered, summed, ranked, staged = (k.sem(f"r_{n}") for n in names)
    run = k.bank[3][:, 0:NB]
    look = [k.bank[4 + u][0:EC, 0:NB] for u in range(HALF)]
    with nc.Block() as block:
        @block.sync
        def _(sp):
            def load_keys(j, s):
                h = 2 * j + s
                if reused(j):
                    sp.wait_ge(peered, h - 1)
                at = h * (HALF * EC)
                sp.dma_start(key_bc[s], io["dst"][ds(at, HALF * EC)].partition_broadcast(P)).then_inc(bc_ready[s], 16)
                sp.dma_start(lo_bc[s], k.lo_edge[ds(at, HALF * EC)].partition_broadcast(P)).then_inc(bc_ready[s], 16)

            pipeline(sp, halves, [(0, load_keys)])
            beside.on_sync(sp)

        @block.scalar
        def _(act):
            def copy_table(j, s):
                c = 2 * j + s
                if later(c):
                    act.wait_ge(updated, c)
                else:
                    act.wait_ge(inited, 1)
                if later(c, 2):
                    act.wait_ge(looked, c - 1)
                nc.scalar.copy(table[s], run).then_inc(copied, 1)

            pipeline(act, COLS, [(0, copy_table)])

        @block.tensor
        def _(pe):
            nc.tensor.matmul(run, k.ident[:, :], table0, start=True, stop=True).then_inc(inited, 1)
            pe.wait_ge(inited, 1)

            def look_up(j, s):
                h = 2 * j + s
                pe.wait_ge(ohT_ready, h + 1)
                for u in range(HALF):
                    c = HALF * h + u
                    pe.wait_ge(copied, c + 1)
                    if later(h):
                        pe.wait_ge(summed, c - HALF + 1)
                    nc.tensor.matmul(run, oh_lo[s][:, u, :], oh_hi[s][:, u, 0:NB], start=False, stop=True,
                                     skip_group_check=True).then_inc(updated, 1)
                    nc.tensor.matmul(look[u], oh_loT[s][:, u * EC:(u + 1) * EC], table[u % 2],
                                     start=True, stop=True).then_inc(looked, 1)

            pipeline(pe, halves, [(0, look_up)])
            beside.on_tensor(pe)

        @block.vector
        def _(dve):
            def one_hots(u):
                def fn(j, s):
                    h = 2 * j + s
                    c = HALF * h + u
                    if u == 0 and reused(j):
                        dve.wait_ge(updated, HALF * h - HALF)
                        dve.wait_ge(summed, HALF * h - HALF)
                    nc.vector.tensor_scalar(oh_lo[s][:, u, :], k.iota_b[0:EC, :], lo[:, ds(c, 1)], None, ALU.is_equal)
                    nc.vector.tensor_scalar(oh_hi[s][:, u, 0:NB], k.iota_b[0:EC, 0:NB], hi[:, ds(c, 1)], None, ALU.is_equal)
                return fn

            def key_columns(j, s):
                h = 2 * j + s
                if reused(j):
                    dve.wait_ge(looked, HALF * h - HALF)
                dve.wait_ge(bc_ready[s], 32 * j + 32)
                nc.vector.tensor_scalar(oh_loT[s], lo_bc[s], k.part_f[:, 0:1], None, ALU.is_equal).then_inc(ohT_ready, 1)

            def count_peers(j, s):
                h = 2 * j + s
                if reused(j):
                    dve.wait_ge(ranked, h - 1)
                for u in range(HALF):
                    c = HALF * h + u
                    last = nc.vector.scalar_tensor_tensor(out=junk_e[s][u], in0=key_bc[s][0:EC, u * EC:(u + 1) * EC],
                                                          scalar=key["dst"][:, ds(c, 1)], in1=k.lower[0:EC, 0:EC],
                                                          op0=ALU.is_equal, op1=ALU.mult, accum_out=peers[s][:, u:u + 1])
                last.then_inc(peered, 1)

            def read_table(u):
                def fn(j, s):
                    h = 2 * j + s
                    if u == 0 and later(h):
                        dve.wait_ge(summed, HALF * h)
                    if u == 0 and later(h, 2):
                        dve.wait_ge(ranked, h - 1)
                    dve.wait_ge(looked, HALF * h + u + 1)
                    nc.vector.scalar_tensor_tensor(out=junk_m[u], in0=look[u], scalar=1.0, in1=oh_hi[s][:, u, 0:NB],
                                                   op0=ALU.mult, op1=ALU.mult, accum_out=before[s][:, u:u + 1]
                                                   ).then_inc(summed, 1)
                return fn

            def slots(j, s):
                h = 2 * j + s
                dve.wait_ge(summed, HALF * h + HALF)
                dve.wait_ge(peered, h + 1)
                nc.vector.tensor_tensor(pos_d[:, ds(HALF * h, HALF)], before[s], peers[s], ALU.add).then_inc(ranked, 1)

            pipeline(dve, halves, [(1, one_hots(0)), (1, one_hots(1)), (0, read_table(0)), (1, one_hots(2)),
                                   (0, read_table(1)), (1, one_hots(3)), (0, read_table(2)), (1, key_columns),
                                   (0, read_table(3)), (1, count_peers), (0, slots)])
            beside.on_vector(dve)

        @block.gpsimd
        def _(pool):
            def scatter(j, s):
                pool.wait_ge(ranked, 4 * j + 2 * s + 2)
                pool.nop(nofuse=True)
                scatter_columns(k, pool, pos_d, k.rec_d, rec[s], slot[s], staged, written[s], j, s)

            pipeline(pool, COLS // CU, [(0, scatter)])
            for s in range(2):
                pool.wait_ge(written[s], 16 * CU * (COLS // CU // 2))


def scatter_columns(k, pool, pos, table, rec, slot, staged, written, j, s, n=CU, first=0):
    nc = k.nc
    step = 2 * j + s
    if reused(j):
        pool.wait_ge(written, 16 * n * j)
        pool.nop(nofuse=True)
    nc.gpsimd.tensor_copy(rec, k.pay[:, ds(step * n + first, n), :]).then_inc(staged, 1)
    nc.gpsimd.tensor_copy(slot, pos[:, ds(step * n + first, n)]).then_inc(staged, 1)
    pool.wait_ge(staged, 2 * step + 2)
    pool.nop(nofuse=True)
    for u in range(n):
        pool.indirect_dma_start(table, bass.IndirectOffsetOnAxis(ap=slot[:, u:u + 1], axis=0),
                                rec[:, u, :], None).then_inc(written, 16)


def block_tiles(k, do, total, tot_i, tiles_f, tend, tbase, blk_f, blk_i, junk):
    nc = k.nc
    do(nc.vector.tensor_scalar(tot_i, total, float(P - 1), None, ALU.add))
    do(nc.vector.tensor_scalar(tot_i, tot_i, 7, None, ALU.logical_shift_right))
    do(nc.vector.tensor_copy(tiles_f, tot_i))
    do(nc.vector.tensor_tensor_scan(tend, k.ones[:, 0:NB], tiles_f, 0.0, ALU.mult, ALU.add))
    do(nc.vector.tensor_tensor(tbase, tend, tiles_f, ALU.subtract))
    for g in range(TG):
        do(nc.vector.tensor_scalar(junk, tend, k.tile_f[:, g:g + 1], None, ALU.is_le, ALU.add,
                                   accum_out=blk_f[:, g:g + 1]))
    do(nc.vector.tensor_scalar(blk_f, blk_f, float(NB - 1), None, ALU.min))


class SortBySrc:

    def __init__(self, k):
        self.k = k
        cut = Carver(k.feat)
        self.key_i, self.hi = cut(COLS, I32, EC), cut(COLS, F32, EC)
        self.oh, self.rank = cut(COLS, F32, EC), cut(COLS, F32, EC)
        self.acc = [cut(COLS, F32, EC) for _ in range(2)]
        self.lane, self.first = cut(NB, F32, EC), cut(NB, F32, EC)
        self.tot_i, self.tiles_f, self.tend, self.tbase = cut(NB, I32), cut(NB), cut(NB), cut(NB)
        self.blk_f, self.blk_i, self.junk = cut(TG), cut(TG, I32), cut(NB)
        names = ("order", "lanes", "summed", "blk", "stored")
        self.order, self.lanes, self.summed, self.blk_ready, self.stored = (k.sem(f"s_{n}") for n in names)

    def on_vector(self, dve):
        k, nc, oh, rank, hi, acc = self.k, self.k.nc, self.oh, self.rank, self.hi, self.acc
        do = Order(dve, self.order)
        do(nc.vector.tensor_copy(self.key_i, self.src_key))
        do(nc.vector.tensor_scalar(self.key_i, self.key_i, 7, None, ALU.logical_shift_right))
        do(nc.vector.tensor_copy(hi, self.key_i))
        for b in range(NB):
            do(nc.vector.tensor_scalar(oh, hi, float(b), None, ALU.is_equal, ALU.add, accum_out=self.lane[:, b:b + 1]))
        dve.sem_inc(self.lanes, 1)
        dve.wait_ge(self.summed, 1)
        block_tiles(k, do, k.bank[0][:, 0:NB], self.tot_i, self.tiles_f, self.tend, self.tbase, self.blk_f, self.blk_i,
                    self.junk)
        nc.vector.tensor_copy(self.blk_i, self.blk_f).then_inc(self.blk_ready, 1)
        do(nc.vector.scalar_tensor_tensor(out=self.first, in0=self.tbase[0:EC, :], scalar=float(P),
                                          in1=k.bank[1][0:EC, 0:NB], op0=ALU.mult, op1=ALU.add))
        do(nc.vector.tensor_scalar(self.first, self.first, -1.0, None, ALU.add))
        do(nc.vector.memset(acc[0], 0.0))
        for b in range(NB):
            do(nc.vector.tensor_scalar(oh, hi, float(b), None, ALU.is_equal))
            do(nc.vector.tensor_tensor_scan(rank, oh, oh, self.first[:, b:b + 1], ALU.add, ALU.bypass))
            do(nc.vector.tensor_tensor(rank, rank, oh, ALU.mult))
            do(nc.vector.tensor_tensor(acc[(b + 1) % 2], acc[b % 2], rank, ALU.add))
        do(nc.vector.tensor_copy(k.pos_s[:, :], acc[NB % 2]))

    def on_tensor(self, pe):
        k, nc = self.k, self.k.nc
        pe.wait_ge(self.lanes, 1)
        nc.tensor.matmul(k.bank[0][:, 0:NB], k.ones[0:EC, :], self.lane, start=True, stop=True)
        nc.tensor.matmul(k.bank[1][0:EC, 0:NB], k.upper[0:EC, 0:EC], self.lane, start=True,
                         stop=True).then_inc(self.summed, 1)

    def on_sync(self, sp):
        k = self.k
        sp.wait_ge(self.blk_ready, 1)
        sp.dma_start(k.block_s.rearrange("(p g) -> p g", p=P), self.blk_i).then_inc(self.stored, 16)
        sp.wait_ge(self.stored, 16)


def slot_tables(k, rec, block_dram, gathered, key, ends, tag):
    nc = k.nc
    cut = Carver(k.wide)
    raw = cut(2 * SLOTROW, I32)
    pair = raw.rearrange("p (s f) -> p s f", f=2)
    node_f, key_f = cut(SLOTROW), cut(SLOTROW)
    lo_i, lo_f, lo_b = cut(SLOTROW, I32), cut(SLOTROW), cut(SLOTROW // 2, BF16)
    edge_i, edge_f = cut(4, I32), cut(4)
    loaded, order, rows_ready, turned = (k.sem(f"l{tag}_loaded"), k.sem(f"l{tag}_order"), k.sem(f"l{tag}_rows"),
                                         k.sem(f"l{tag}_turned"))
    lo_ready, stored, edges_set = k.sem(f"l{tag}_lo"), k.sem(f"l{tag}_stored"), k.sem(f"l{tag}_edges")
    rec_rows = rec.rearrange("(p s) f -> p s f", p=P)
    with nc.Block() as block:
        @block.sync
        def _(sp):
            sp.dma_start(raw, rec.rearrange("(p s) f -> p (s f)", p=P)).then_inc(loaded, 16)
            sp.dma_start(k.block_row[:, :], block_dram.rearrange("(o t) -> o t", o=1)).then_inc(loaded, 16)
            if ends:
                sp.wait_ge(edges_set, 1)
                sp.dma_start(edge_i[1:P, 0:2], rec_rows[0:P - 1, SLOTROW - 1, :]).then_inc(loaded, 16)
                sp.dma_start(edge_i[0:P - 1, 2:4], rec_rows[1:P, 0, :]).then_inc(loaded, 16)
            sp.wait_ge(lo_ready, 1)
            sp.dma_start(k.lo_slot.rearrange("(p s) -> p s", p=P), lo_b).then_inc(stored, 16)
            sp.wait_ge(stored, 16)

        @block.vector
        def _(dve):
            do = Order(dve, order)
            if ends:
                nc.vector.memset(edge_i, -1).then_inc(edges_set, 1)
            dve.wait_ge(loaded, 64 if ends else 32)
            do(nc.vector.tensor_copy(node_f, pair[:, :, gathered]))
            do(nc.vector.tensor_scalar(lo_i, pair[:, :, key], PAD_KEY | (P - 1), None, ALU.bitwise_and))
            nc.vector.tensor_copy(lo_f, lo_i).then_inc(rows_ready, 1)
            nc.vector.tensor_copy(lo_b, lo_i).then_inc(lo_ready, 1)
            if ends:
                do(nc.vector.tensor_copy(key_f, pair[:, :, key]))
                do(nc.vector.tensor_copy(edge_f, edge_i))
                here, there = key_f[:, 1:SLOTROW], key_f[:, 0:SLOTROW - 1]
                do(nc.vector.tensor_tensor(k.keep_fwd[:, 1:SLOTROW], here, there, ALU.is_equal))
                do(nc.vector.tensor_tensor(k.keep_bwd[:, 0:SLOTROW - 1], here, there, ALU.is_equal))
                do(nc.vector.tensor_tensor(k.keep_fwd[:, 0:1], key_f[:, 0:1], edge_f[:, key:key + 1], ALU.is_equal))
                do(nc.vector.tensor_tensor(k.keep_bwd[:, SLOTROW - 1:SLOTROW], key_f[:, SLOTROW - 1:SLOTROW],
                                           edge_f[:, 2 + key:3 + key], ALU.is_equal))
            for n, col in enumerate((k.gather_col, k.lo_col)):
                for half, (g0, g1) in enumerate(((0, 4), (4, TG))):
                    dve.wait_ge(turned, 2 * n + half + 1)
                    out = col[:, :].rearrange("p (t g) -> p g t", g=TG)[:, g0:g1, :]
                    ps = k.bank[2 * n + half][:, 0:(g1 - g0) * P].rearrange("p (g t) -> p g t", t=P)
                    do(nc.vector.tensor_copy(out, ps))

        @block.tensor
        def _(pe):
            pe.wait_ge(rows_ready, 1)
            for n, rows in enumerate((node_f, lo_f)):
                for half, (g0, g1) in enumerate(((0, 4), (4, TG))):
                    for g in range(g0, g1):
                        last = nc.tensor.transpose(k.bank[2 * n + half][:, (g - g0) * P:(g - g0 + 1) * P],
                                                   rows[:, g * P:(g + 1) * P], k.ident[:, :])
                    last.then_inc(turned, 1)


def node_blocks(k, engine, tile, n):
    return k.nc.values_load_multi_w_load_instructions(k.block_row[0:1, ds(tile, n)], engines=(engine,), min_val=0,
                                                      max_val=NB - 1)[1]


def load_nodes(sp, x, area, loaded):
    whole = (NB - 1) * P
    sp.dma_start(area[:, 0:(NB - 1) * D].rearrange("p (b d) -> p b d", d=D),
                 x[0:whole, :].rearrange("(b p) d -> p b d", p=P)).then_inc(loaded, 16)
    sp.dma_start(area[0:TAIL, (NB - 1) * D:NB * D], x[whole:N, :]).then_inc(loaded, 16)


def center(k, do, dve, x, xc, square, mean, rstd, eps, sq_ready, squared, var_ready, rooted):
    nc = k.nc
    x3 = x.rearrange("p (b d) -> p b d", d=D)
    xc3 = xc.rearrange("p (b d) -> p b d", d=D)
    do(nc.vector.tensor_reduce(mean, x3, AX_X, ALU.add))
    do(nc.vector.tensor_scalar(mean, mean, 1.0 / D, None, ALU.mult))
    nc.vector.tensor_tensor(xc3, x3, mean.unsqueeze(2).to_broadcast([P, NB, D]), ALU.subtract).then_inc(sq_ready, 1)
    dve.wait_ge(squared, 1)
    do(nc.vector.tensor_reduce(rstd, square.rearrange("p (b d) -> p b d", d=D), AX_X, ALU.add))
    nc.vector.tensor_scalar(rstd, rstd, 1.0 / D, eps, ALU.mult, ALU.add).then_inc(var_ready, 1)
    dve.wait_ge(rooted, 1)
    do(nc.vector.reciprocal(rstd, rstd))


def scale_rows(k, rows, by):
    rows3 = rows.rearrange("p (b d) -> p b d", d=D)
    return k.nc.vector.tensor_tensor(rows3, rows3, by.unsqueeze(2).to_broadcast([P, NB, D]), ALU.mult)


def norm_to_features(k, x, rows, scratch, load, tag):
    nc = k.nc
    cut = Carver(k.work)
    mean, rstd = cut(NB), cut(NB)
    stage = [cut(P) for _ in range(2)]
    names = ("loaded", "order", "sq_ready", "squared", "var", "rooted", "ready", "cleared")
    loaded, order, sq_ready, squared, var_ready, rooted, ready, cleared = (k.sem(f"n{tag}_{n}") for n in names)
    staged = [k.sem(f"n{tag}_staged{s}") for s in range(2)]
    turned = [k.sem(f"n{tag}_turned{s}") for s in range(2)]
    kept = [k.sem(f"n{tag}_kept{s}") for s in range(2)]
    with nc.Block() as block:
        if load is not None:
            @block.sync
            def _(sp):
                sp.wait_ge(cleared, 1)
                load_nodes(sp, load, x, loaded)

        @block.scalar
        def _(act):
            act.wait_ge(sq_ready, 1)
            nc.scalar.activation(scratch, rows, ACT.Square).then_inc(squared, 1)
            act.wait_ge(var_ready, 1)
            nc.scalar.activation(rstd, rstd, ACT.Sqrt).then_inc(rooted, 1)
            act.wait_ge(ready, 1)

            def relu(j, s):
                if reused(j):
                    act.wait_ge(turned[s], j)
                nc.scalar.activation(stage[s], rows[:, ds((2 * j + s) * P, P)], ACT.Relu).then_inc(staged[s], 1)

            pipeline(act, NB, [(0, relu)])

        @block.tensor
        def _(pe):
            def turn(j, s):
                pe.wait_ge(staged[s], j + 1)
                if reused(j):
                    pe.wait_ge(kept[s], j)
                nc.tensor.transpose(k.bank[s][:, 0:P], stage[s], k.ident[:, :]).then_inc(turned[s], 1)

            pipeline(pe, NB, [(0, turn)])

        @block.vector
        def _(dve):
            do = Order(dve, order)
            if load is not None:
                nc.vector.memset(x[:, (NB - 1) * D:NB * D], 0.0).then_inc(cleared, 1)
                dve.wait_ge(loaded, 32)
            center(k, do, dve, x, rows, scratch, mean, rstd, 1e-5, sq_ready, squared, var_ready, rooted)
            scale_rows(k, rows, rstd).then_inc(ready, 1)

            def keep(j, s):
                dve.wait_ge(turned[s], j + 1)
                nc.vector.tensor_copy(k.hT[:, ds((2 * j + s) * P, P)], k.bank[s][:, 0:P]).then_inc(kept[s], 1)

            pipeline(dve, NB, [(0, keep)])
            do(nc.vector.tensor_scalar(rows, rows, 0.0, None, ALU.max)) if load is None else None


def node_tables(k, gathered_w, local_ws, gather_w, local_w, table, local, bias_rows, att, tag):
    nc = k.nc
    cut = Carver(k.work)
    w = cut(gather_w + local_w)
    bias = [cut(local_w) for _ in bias_rows]
    stage = [cut(P) for _ in range(2)]
    out = [cut(gather_w) for _ in range(2)]
    att_bc = cut(HD) if att is not None else None
    loaded, order, weights_set = k.sem(f"w{tag}_loaded"), k.sem(f"w{tag}_order"), k.sem(f"w{tag}_weights")
    names = ("staged", "done", "copied", "kept", "stored")
    staged, done, copied, kept, stored = ([k.sem(f"w{tag}_{n}{s}") for s in range(2)] for n in names)
    table3 = table.rearrange("(b p) d -> b p d", p=P)
    n_loads = len(gathered_w) + len(local_ws) + len(bias_rows) + (att is not None)
    with nc.Block() as block:
        @block.sync
        def _(sp):
            for at, group in ((0, gathered_w), (gather_w, local_ws)):
                for v in group:
                    sp.dma_start(w[:, at:at + v.shape[1]], v).then_inc(loaded, 16)
                    at += v.shape[1]
            for b, v in zip(bias, bias_rows):
                sp.dma_start(b[:, 0:v.shape[0]], v.partition_broadcast(P)).then_inc(loaded, 16)
            if att is not None:
                sp.dma_start(att_bc, att.rearrange("h d -> (h d)").partition_broadcast(P)).then_inc(loaded, 16)

            def store(j, s):
                sp.wait_ge(copied[s], j + 1)
                sp.dma_start(table3[ds(2 * j + s, 1), :, :].rearrange("o p d -> (o p) d"), out[s]).then_inc(stored[s], 16)

            pipeline(sp, NB, [(0, store)])
            for s in range(2):
                sp.wait_ge(stored[s], 16 * ((NB + 1 - s) // 2))

        @block.gpsimd
        def _(pool):
            def take(j, s):
                if reused(j):
                    pool.wait_ge(done[s], j)
                    pool.nop(nofuse=True)
                nc.gpsimd.tensor_copy(stage[s], k.hT[:, ds((2 * j + s) * P, P)]).then_inc(staged[s], 1)

            pipeline(pool, NB, [(0, take)])

        @block.tensor
        def _(pe):
            pe.wait_ge(weights_set, 1)

            def products(j, s):
                pe.wait_ge(staged[s], j + 1)
                if reused(j):
                    pe.wait_ge(copied[s], j)
                    pe.wait_ge(kept[s], j)
                nc.tensor.matmul(k.bank[s][:, 0:gather_w], stage[s], w[:, 0:gather_w], start=True, stop=True)
                nc.tensor.matmul(k.bank[2 + s][:, 0:local_w], stage[s], w[:, gather_w:gather_w + local_w],
                                 start=True, stop=True).then_inc(done[s], 1)

            pipeline(pe, NB, [(0, products)])

        @block.scalar
        def _(act):
            def copy(j, s):
                act.wait_ge(done[s], j + 1)
                if reused(j):
                    act.wait_ge(stored[s], 16 * j)
                nc.scalar.copy(out[s], k.bank[s][:, 0:gather_w]).then_inc(copied[s], 1)

            pipeline(act, NB, [(0, copy)])

        @block.vector
        def _(dve):
            do = Order(dve, order)
            dve.wait_ge(loaded, 16 * n_loads)
            if bias_rows:
                do(nc.vector.tensor_tensor(bias[0][:, 0:HD], bias[0][:, 0:HD], bias[1][:, 0:HD], ALU.add))
            if att is not None:
                for v in (w[:, 0:HE], w[:, HE:2 * HE], bias[0]):
                    do(nc.vector.tensor_tensor(out[0][:, 0:HD], v[:, 0:HD], att_bc, ALU.mult))
                    do(nc.vector.tensor_reduce(v[:, HD:HE], out[0][:, 0:HD].rearrange("p (h d) -> p h d", h=H), AX_X,
                                               ALU.add))
            dve.sem_inc(weights_set, 1)

            def keep(j, s):
                dve.wait_ge(done[s], j + 1)
                to = local[:, ds((2 * j + s) * local_w, local_w)]
                if bias_rows:
                    nc.vector.tensor_tensor(to, k.bank[2 + s][:, 0:local_w], bias[0], ALU.add).then_inc(kept[s], 1)
                else:
                    nc.vector.tensor_copy(to, k.bank[2 + s][:, 0:local_w]).then_inc(kept[s], 1)

            pipeline(dve, NB, [(0, keep)])


def edge_scores(k, att, tag):
    nc = k.nc
    groups = T_DST // GS
    U = 4
    cut = Carver(k.wide)
    xg = [cut(GS * HE) for _ in range(U)]
    z = [cut(GS * HE) for _ in range(U)]
    z3 = [v.rearrange("p (u e) -> p u e", u=GS) for v in z]
    pick = [cut(GS * P) for _ in range(U)]
    lo_bc = [cut(GS * P // 2, BF16) for _ in range(U)]
    att_bc = cut(HD)
    part = [cut(GS * H) for _ in range(U)]
    index = [cut(GS, I32) for _ in range(U)]
    gathered = [k.gather_sem(f"a{tag}_gathered{s}") for s in range(U)]
    index_set, spilled, lo_ready = ([k.sem(f"a{tag}_{n}{s}") for s in range(U)] for n in ("index", "spilled", "lo"))
    names = ("loaded", "cleared", "order", "picked", "looked", "added", "weighed", "reduced", "scored")
    loaded, cleared, order, picked, looked, added, weighed, reduced, scored = (k.sem(f"a{tag}_{n}") for n in names)
    with nc.Block() as block:
        @block.gpsimd
        def _(pool):
            def gather(j, s):
                g = U * j + s
                pool.wait_ge(index_set[s], 16 * j + 16)
                if reused(j):
                    pool.wait_ge(added, GS * g - GS * U + GS)
                    if s < U - 1:
                        pool.wait_ge(spilled[s], 16 * j)
                pool.nop(nofuse=True)
                for u in range(GS):
                    pool.indirect_dma_start(xg[s][:, u * HE:(u + 1) * HE], None, k.xl,
                                            bass.IndirectOffsetOnAxis(ap=index[s][:, u:u + 1], axis=0)).then_inc(gathered[s], 16)

            pipeline(pool, groups, [(0, gather)], U)

        @block.sync
        def _(sp):
            sp.dma_start(att_bc, att.rearrange("h d -> (h d)").partition_broadcast(P)).then_inc(loaded, 16)

            def load(j, s):
                g = U * j + s
                if reused(j):
                    sp.wait_ge(gathered[s], 16 * GS * j)
                    sp.nop(nofuse=True)
                    sp.wait_ge(picked, g - U + 1)
                    sp.nop(nofuse=True)
                sp.dma_start(lo_bc[s], k.lo_slot[ds(g * (GS * P), GS * P)].partition_broadcast(P)).then_inc(lo_ready[s], 16)
                sp.dma_start(index[s], k.gather_col[:, ds(g * GS, GS)]).then_inc(index_set[s], 16)

            def spill(j, s):
                if s == U - 1:
                    return
                sp.wait_ge(gathered[s], 16 * GS * j + 16 * GS)
                sp.dma_start(k.spill[ds((U * j + s) * GS, GS), :, :].rearrange("u p d -> p u d"),
                             xg[s].rearrange("p (u e) -> p u e", u=GS)[:, :, 0:HD]).then_inc(spilled[s], 16)

            pipeline(sp, groups, [(3, load), (0, spill)], U)
            for s in range(U - 1):
                sp.wait_ge(spilled[s], 16 * (groups // U))

        @block.tensor
        def _(pe):
            def look(j, s):
                g = U * j + s
                pe.wait_ge(picked, g + 1)
                for u, b in enumerate(node_blocks(k, PE, g * GS, GS)):
                    if later(g, U):
                        pe.wait_ge(added, GS * (g - U) + u + 1)
                    nc.tensor.matmul(k.bank[GS * s + u][:, 0:HE], pick[s][:, u * P:(u + 1) * P], k.node[:, ds(b * HE, HE)],
                                     start=True, stop=True).then_inc(looked, 1)

            pipeline(pe, groups, [(0, look)], U)

        @block.scalar
        def _(act):
            def reduce(j, s):
                g = U * j + s
                act.wait_ge(weighed, g + 1)
                if later(g, U):
                    act.wait_ge(scored, g - U + 1)
                for u in range(GS):
                    for h in range(H):
                        at = z[s][:, u * HE + h * D:u * HE + (h + 1) * D]
                        last = nc.scalar.activation(at, at, ACT.Copy, accum_out=part[s][:, u * H + h:u * H + h + 1])
                last.then_inc(reduced, 1)

            pipeline(act, groups, [(0, reduce)], U)

        @block.vector
        def _(dve):
            do = Order(dve, order)
            do(nc.vector.memset(k.wcol[:, T_DST * H:TILES * H], 0.0))
            dve.wait_ge(loaded, 16)
            do(nc.vector.tensor_scalar(att_bc, att_bc, 1.0 - SLOPE, None, ALU.mult))

            def picks(j, s):
                g = U * j + s
                dve.wait_ge(lo_ready[s], 16 * j + 16)
                if later(g, U):
                    dve.wait_ge(looked, GS * (g - U) + GS)
                nc.vector.tensor_scalar(pick[s], lo_bc[s], k.part_f[:, 0:1], None, ALU.is_equal).then_inc(picked, 1)

            def add(j, s):
                g = U * j + s
                dve.wait_ge(gathered[s], 16 * GS * j + 16 * GS)
                if later(g, U):
                    dve.wait_ge(scored, g - U + 1)
                for u in range(GS):
                    dve.wait_ge(looked, GS * g + u + 1)
                    nc.vector.tensor_tensor(z[s][:, u * HE:(u + 1) * HE], k.bank[GS * s + u][:, 0:HE],
                                            xg[s][:, u * HE:(u + 1) * HE], ALU.add).then_inc(added, 1)

            def weigh(j, s):
                g = U * j + s
                dve.wait_ge(added, GS * g + GS)
                zd = z3[s][:, :, 0:HD]
                nc.vector.scalar_tensor_tensor(out=zd, in0=zd, scalar=0.0, in1=att_bc.unsqueeze(1).to_broadcast([P, GS, HD]),
                                               op0=ALU.max, op1=ALU.mult).then_inc(weighed, 1)

            def score(j, s):
                g = U * j + s
                dve.wait_ge(reduced, g + 1)
                nc.vector.scalar_tensor_tensor(
                    out=k.wcol[:, ds(g * (GS * H), GS * H)].rearrange("p (u h) -> p u h", u=GS),
                    in0=z3[s][:, :, HD:HE], scalar=SLOPE, in1=part[s].rearrange("p (u h) -> p u h", u=GS),
                    op0=ALU.mult, op1=ALU.add).then_inc(scored, 1)

            pipeline(dve, groups, [(3, picks), (1, add), (0, weigh), (-2, score)], U)


def segment_softmax(k, tag):
    nc = k.nc
    W = SLOTROW
    cut = Carver(k.wide)
    s_row, fwd, bwd = cut(H * W), cut(H * W), cut(H * W)
    whole = cut(1)
    rowkeep = [cut(H) for _ in range(2)]
    ends = [cut(H) for _ in range(2)]
    init = [cut(H) for _ in range(2)]
    keepT = [cut(P, F32, H) for _ in range(2)]
    endT = [cut(P, F32, H) for _ in range(2)]
    carry = [cut(P + 1, F32, H) for _ in range(2)]
    no = [cut(W) for _ in range(2)]
    keep = [k.keep_fwd[:, :], k.keep_bwd[:, :]]
    NBLK = H * TG
    names = ("order", "turned", "in", "ends", "endsT", "carry", "carryT", "shifted", "exp", "weights", "back")
    order, turned, taken, ends_set, endsT, carry_set, carryT, shifted, exped, weights_set, back = (
        k.sem(f"b{tag}_{n}") for n in names)
    by_slot = k.wcol[:, :].rearrange("p (t g h) -> p h g t", g=TG, h=H)
    quads = [range(q, min(q + 4, NBLK)) for q in range(0, NBLK, 4)]
    along = [lambda v: v, lambda v: v[:, ::-1]]
    with nc.Block() as block:
        @block.tensor
        def _(pe):
            for q, quad in enumerate(quads):
                for n in quad:
                    last = nc.tensor.transpose(k.bank[q][:, (n - quad[0]) * P:(n - quad[0] + 1) * P],
                                               by_slot[:, n // TG, n % TG, :], k.ident[:, :])
                last.then_inc(turned, 1)
            pe.wait_ge(taken, len(quads))
            for r in range(2):
                pe.wait_ge(ends_set, r + 1)
                for d in range(2):
                    nc.tensor.transpose(k.bank[0][0:H, d * P:(d + 1) * P], ends[d], k.ident[:, :])
                    last = nc.tensor.transpose(k.bank[0][0:H, (2 + d) * P:(3 + d) * P], rowkeep[d], k.ident[:, :])
                last.then_inc(endsT, 1)
                pe.wait_ge(carry_set, r + 1)
                for d in range(2):
                    last = nc.tensor.transpose(k.bank[1][:, d * H:(d + 1) * H], carry[d][:, d:d + P], k.ident[0:H, 0:H])
                last.then_inc(carryT, 1)
            pe.wait_ge(weights_set, 1)
            for q, quad in enumerate(quads):
                for n in quad:
                    last = nc.tensor.transpose(k.bank[2 + q][:, (n - quad[0]) * P:(n - quad[0] + 1) * P],
                                               s_row[:, n * P:(n + 1) * P], k.ident[:, :])
                last.then_inc(back, 1)

        @block.scalar
        def _(act):
            act.wait_ge(shifted, 1)
            nc.scalar.activation(s_row, s_row, ACT.Exp).then_inc(exped, 1)

        @block.vector
        def _(dve):
            do = Order(dve, order)
            for q, quad in enumerate(quads):
                dve.wait_ge(turned, q + 1)
                w = len(quad) * P
                nc.vector.tensor_copy(s_row[:, quad[0] * P:quad[0] * P + w], k.bank[q][:, 0:w]).then_inc(taken, 1)
            dve.wait_ge(taken, len(quads))
            for d in range(2):
                do(nc.vector.tensor_scalar(no[d], keep[d], -1.0, BIG, ALU.add, ALU.mult))
                do(nc.vector.tensor_reduce(whole, keep[d], AX_X, ALU.min))
                do(nc.vector.tensor_copy(rowkeep[d], whole.to_broadcast([P, H])))

            def both_ways(r, gate, empty, op0, op1):
                out = (fwd, bwd)
                for d in range(2):
                    for h in range(H):
                        row = slice(h * W, (h + 1) * W)
                        nc_scan = nc.vector.tensor_tensor_scan(along[d](out[d][:, row]), along[d](gate[d]),
                                                               along[d](s_row[:, row]), empty, op0, op1)
                        do(nc_scan)
                        end = h * W + (W - 1 if d == 0 else 0)
                        do(nc.vector.tensor_copy(ends[d][:, h:h + 1], out[d][:, end:end + 1]))
                dve.sem_inc(ends_set, 1)
                dve.wait_ge(endsT, r + 1)
                for d in range(2):
                    do(nc.vector.tensor_copy(endT[d], k.bank[0][0:H, d * P:(d + 1) * P]))
                    do(nc.vector.tensor_copy(keepT[d], k.bank[0][0:H, (2 + d) * P:(3 + d) * P]))
                    if r == 0:
                        do(nc.vector.tensor_scalar(keepT[d], keepT[d], -1.0, BIG, ALU.add, ALU.mult))
                    do(nc.vector.memset(carry[d], empty))
                    do(nc.vector.tensor_tensor_scan(along[d](carry[d][:, 1 - d:1 - d + P]), along[d](keepT[d]),
                                                    along[d](endT[d]), empty, op0, op1))
                dve.sem_inc(carry_set, 1)
                dve.wait_ge(carryT, r + 1)
                for d in range(2):
                    do(nc.vector.tensor_copy(init[d], k.bank[1][:, d * H:(d + 1) * H]))
                    for h in range(H):
                        row = slice(h * W, (h + 1) * W)
                        do(nc.vector.tensor_tensor_scan(along[d](out[d][:, row]), along[d](gate[d]),
                                                        along[d](s_row[:, row]), init[d][:, h:h + 1], op0, op1))

            both_ways(0, no, -BIG, ALU.add, ALU.max)
            do(nc.vector.tensor_tensor(fwd, fwd, bwd, ALU.max))
            nc.vector.tensor_tensor(s_row, s_row, fwd, ALU.subtract).then_inc(shifted, 1)
            dve.wait_ge(exped, 1)
            both_ways(1, keep, 0.0, ALU.mult, ALU.add)
            do(nc.vector.tensor_tensor(bwd, bwd, s_row, ALU.subtract))
            do(nc.vector.tensor_tensor(fwd, fwd, bwd, ALU.add))
            do(nc.vector.reciprocal(fwd, fwd))
            nc.vector.tensor_tensor(s_row, s_row, fwd, ALU.mult).then_inc(weights_set, 1)
            for q, quad in enumerate(quads):
                dve.wait_ge(back, q + 1)
                for n in quad:
                    last = nc.vector.tensor_copy(by_slot[:, n // TG, n % TG, :],
                                                 k.bank[2 + q][:, (n - quad[0]) * P:(n - quad[0] + 1) * P])
            do(last)


def aggregate(k, half, tag):
    nc = k.nc
    groups = T_DST // G
    U = 4
    turns = groups // U
    cut = Carver(k.wide)
    xg = [cut(GS * (HD + HE) if s % 2 else G * HD) for s in range(U)]
    row_at = [[u * HD + (max(u - GS, 0) * H if s % 2 else 0) for u in range(G)] for s in range(U)]
    xw = [cut(G * HD) for _ in range(2)]
    place = [cut(G * P) for _ in range(2)]
    index = [cut(GS, I32) for _ in range(2)]
    rec = [cut(CU, I32, EC).rearrange("p (u f) -> p u f", f=2) for _ in range(2)]
    slot = [cut(CU // 2, I32, EC) for _ in range(2)]
    written = [k.gather_sem(f"g{tag}_written{s}") for s in range(2)]
    gathered = [k.gather_sem(f"g{tag}_gathered{s}") for s in range(2)]
    index_set = [k.sem(f"g{tag}_index{s}") for s in range(2)]
    loaded = [k.sem(f"g{tag}_loaded{s}") for s in range(U)]
    names = ("cleared", "staged", "placed", "weighed", "summed", "added")
    cleared, staged, placed, weighed, summed, added = (k.sem(f"g{tag}_{n}") for n in names)
    by_vector = ((1, 2), (3, 2))
    cols = COLS // 2
    scatter_turns = cols // CU

    def rows_in(eng, j, s, u):
        if u == 0:
            eng.wait_ge(loaded[s], 16 * j + 16)
        if u == GS and s % 2:
            eng.wait_ge(gathered[s // 2], 16 * GS * j + 16 * GS)

    with nc.Block() as block:
        @block.gpsimd
        def _(pool):
            def gather(j, n):
                s = 2 * n + 1
                pool.wait_ge(index_set[n], 16 * j + 16)
                if reused(j):
                    pool.wait_ge(weighed, G * (U * j + s - U) + G)
                    pool.wait_ge(placed, G * (U * j + s - U) + G)
                pool.nop(nofuse=True)
                for u in range(GS):
                    at = row_at[s][GS + u]
                    pool.indirect_dma_start(xg[s][:, at:at + HE], None, k.xl,
                                            bass.IndirectOffsetOnAxis(ap=index[n][:, u:u + 1], axis=0)).then_inc(gathered[n], 16)

            def both(j):
                for n in range(2):
                    gather(j, n)
                    scatter_columns(k, pool, k.pos_s, k.rec_s, rec[n], slot[n], staged, written[n], j, n,
                                    CU // 2, half * cols)

            both(0)
            with pool.Fori(1, scatter_turns) as i:
                both(i)
            with pool.Fori(scatter_turns, turns) as i:
                for n in range(2):
                    gather(i, n)
            for n in range(2):
                pool.wait_ge(written[n], 16 * (CU // 2) * scatter_turns)

        @block.sync
        def _(sp):
            def load(j, s):
                g = U * j + s
                tiles = GS if s % 2 else G
                if later(g, U):
                    sp.wait_ge(weighed, G * (g - U) + G)
                    sp.nop(nofuse=True)
                    sp.wait_ge(placed, G * (g - U) + G)
                    sp.nop(nofuse=True)
                sp.dma_start(xg[s][:, 0:tiles * HD].rearrange("p (u d) -> p u d", u=tiles),
                             k.spill[ds(g * G, tiles), :, :].rearrange("u p d -> p u d")).then_inc(loaded[s], 16)
                if s % 2:
                    sp.dma_start(index[s // 2], k.gather_col[:, ds(g * G + GS, GS)]).then_inc(index_set[s // 2], 16)

            pipeline(sp, groups, [(0, load)], U)

        @block.scalar
        def _(act):
            def weigh(j, s):
                g = U * j + s
                for u in range(G):
                    rows_in(act, j, s, u)
                    if later(g, 2):
                        act.wait_ge(summed, G * (g - 2) + u + 1)
                    for h in range(H):
                        if (u, h) in by_vector:
                            continue
                        at, to = row_at[s][u] + h * D, u * HD + h * D
                        last = nc.scalar.activation(xw[s % 2][:, to:to + D], xg[s][:, at:at + D], ACT.Copy,
                                                    scale=k.wcol[:, ds((g * G + u) * H + h, 1)])
                    last.then_inc(weighed, 1)

            pipeline(act, groups, [(0, weigh)], U)

        @block.tensor
        def _(pe):
            def sums(j, s):
                g = U * j + s
                for u in range(G):
                    pe.wait_ge(weighed, G * g + u + 1)
                    pe.wait_ge(placed, G * g + u + 1)
                    if later(g, 2):
                        pe.wait_ge(added, G * (g - 2) + u + 1)
                    nc.tensor.matmul(k.bank[G * (s % 2) + u][:, 0:HD], place[s % 2][:, u * P:(u + 1) * P],
                                     xw[s % 2][:, u * HD:(u + 1) * HD], start=True, stop=True).then_inc(summed, 1)

            pipeline(pe, groups, [(0, sums)], U)

        @block.vector
        def _(dve):
            nc.vector.memset(k.node[:, 0:NB * HD], 0.0).then_inc(cleared, 1)
            dve.wait_ge(cleared, 1)
            blocks = []

            def get_blocks(j, s):
                blocks[:] = node_blocks(k, DVE, (U * j + s) * G, G)

            def add(u):
                def fn(j, s):
                    g = U * j + s
                    dve.wait_ge(summed, G * g + u + 1)
                    if u > 0 or later(g):
                        dve.wait_ge(added, G * g + u)
                    acc = k.node[:, ds(blocks[u] * HD, HD)]
                    nc.vector.tensor_tensor(acc, acc, k.bank[G * (s % 2) + u][:, 0:HD], ALU.add).then_inc(added, 1)
                return fn

            def places(u):
                def fn(j, s):
                    g = U * j + s
                    if later(g, 2):
                        dve.wait_ge(summed, G * (g - 2) + u + 1)
                    last = nc.vector.tensor_scalar(place[s % 2][:, u * P:(u + 1) * P], k.iota_f[:, :],
                                                   k.lo_col[:, ds(g * G + u, 1)], None, ALU.is_equal)
                    for v, h in by_vector:
                        if v == u:
                            rows_in(dve, j, s, 0)
                            rows_in(dve, j, s, u - u % GS)
                            at, to = row_at[s][u] + h * D, u * HD + h * D
                            last = nc.vector.tensor_scalar(xw[s % 2][:, to:to + D], xg[s][:, at:at + D],
                                                           k.wcol[:, ds((g * G + u) * H + h, 1)], None, ALU.mult)
                    last.then_inc(placed, 1)
                return fn

            stages = [(0, get_blocks)]
            for u in range(G):
                stages += [(0, add(u)), (2, places(u))]
            pipeline(dve, groups, stages, U)


def load_cols(nc, sp, cols, sources, loaded):
    with nc.allow_non_contiguous_dma(reason="one word per partition"):
        for n, v in enumerate(sources):
            sp.dma_start(cols[:, n:n + 1], v.rearrange("(p o) -> p o", o=1)).then_inc(loaded, 16)


def node_layer(k, row_biases, mats, outs, tag):
    nc = k.nc
    cut = Carver(k.work)
    M = len(mats)
    bias = [cut(HD) for _ in row_biases]
    w = cut(M * HD)
    col = cut(M)
    rows = [cut(HD) for _ in range(2)]
    turned_rows = [cut(HD) for _ in range(2)]
    loaded, order = k.sem(f"m{tag}_loaded"), k.sem(f"m{tag}_order")
    names = ("rows", "turned", "copied", "done", "kept")
    rows_set, turned, copied, done, kept = ([k.sem(f"m{tag}_{n}{s}") for s in range(2)] for n in names)
    col_biases = [v for _, v, _ in outs if v is not None]
    n_loads = M + len(row_biases) + len(col_biases)
    with nc.Block() as block:
        @block.sync
        def _(sp):
            for b, v in zip(bias, row_biases):
                sp.dma_start(b, v.partition_broadcast(P)).then_inc(loaded, 16)
            for m, v in enumerate(mats):
                sp.dma_start(w[:, m * HD:(m + 1) * HD].rearrange("p (h n) -> p h n", h=H),
                             v.rearrange("(h p) n -> p h n", p=P)).then_inc(loaded, 16)
            load_cols(nc, sp, col, col_biases, loaded)

        @block.tensor
        def _(pe):
            pe.wait_ge(loaded, 16 * n_loads)

            def turn(j, s):
                pe.wait_ge(rows_set[s], j + 1)
                if reused(j):
                    pe.wait_ge(copied[s], j)
                for h in range(H):
                    last = nc.tensor.transpose(k.bank[s][:, h * P:(h + 1) * P], rows[s][:, h * P:(h + 1) * P], k.ident[:, :])
                last.then_inc(turned[s], 1)

            def products(j, s):
                pe.wait_ge(copied[s], j + 1)
                if reused(j):
                    pe.wait_ge(kept[s], j)
                for m in range(M):
                    for h in range(H):
                        last = nc.tensor.matmul(k.bank[2 + s][:, m * P:(m + 1) * P], w[:, (m * H + h) * P:(m * H + h + 1) * P],
                                                turned_rows[s][:, h * P:(h + 1) * P], start=(h == 0), stop=(h == H - 1))
                last.then_inc(done[s], 1)

            pipeline(pe, NB, [(1, turn), (0, products)])

        @block.scalar
        def _(act):
            def copy(j, s):
                act.wait_ge(turned[s], j + 1)
                if reused(j):
                    act.wait_ge(done[s], j)
                nc.scalar.copy(turned_rows[s], k.bank[s][:, 0:HD]).then_inc(copied[s], 1)

            pipeline(act, NB, [(0, copy)])

        @block.vector
        def _(dve):
            do = Order(dve, order)
            dve.wait_ge(loaded, 16 * n_loads)
            do(nc.vector.tensor_tensor(bias[0], bias[0], bias[1], ALU.add))

            def biased(j, s):
                if reused(j):
                    dve.wait_ge(turned[s], j)
                nc.vector.tensor_tensor(rows[s], k.node[:, ds((2 * j + s) * HD, HD)], bias[0], ALU.add).then_inc(rows_set[s], 1)

            def keep(j, s):
                dve.wait_ge(done[s], j + 1)
                c = 0
                for m, (area, v, adds) in enumerate(outs):
                    to = area[:, ds((2 * j + s) * P, P)]
                    ps = k.bank[2 + s][:, m * P:(m + 1) * P]
                    if adds:
                        last = nc.vector.tensor_tensor(to, to, ps, ALU.add)
                    else:
                        last = nc.vector.tensor_scalar(to, ps, col[:, c:c + 1], None, ALU.add)
                        c += 1
                last.then_inc(kept[s], 1)

            pipeline(dve, NB, [(2, biased), (0, keep)])


def batch_norm(k, y, gamma, beta, scale, shift, tag):
    nc = k.nc
    cut = Carver(k.work[:, 0:400])
    CH = 250
    stats, agg, cols = cut(N // CH * 6), cut(2), cut(2)
    assert N % CH == 0
    loaded, order, rooted, var_set = (k.sem(f"v{tag}_{n}") for n in ("loaded", "order", "rooted", "var"))
    with nc.Block() as block:
        @block.sync
        def _(sp):
            load_cols(nc, sp, cols, (gamma, beta), loaded)

        @block.scalar
        def _(act):
            act.wait_ge(var_set, 1)
            nc.scalar.activation(scale, scale, ACT.Sqrt).then_inc(rooted, 1)

        @block.vector
        def _(dve):
            do = Order(dve, order)
            for c in range(N // CH):
                last = nc.vector.bn_stats(stats[:, 6 * c:6 * c + 6], y[:, c * CH:(c + 1) * CH])
            do(last)
            do(nc.vector.bn_aggr(agg, stats))
            nc.vector.tensor_scalar(scale, agg[:, 1:2], 1e-5, None, ALU.add).then_inc(var_set, 1)
            dve.wait_ge(rooted, 1)
            do(nc.vector.reciprocal(scale, scale))
            dve.wait_ge(loaded, 32)
            do(nc.vector.tensor_tensor(scale, scale, cols[:, 0:1], ALU.mult))
            do(nc.vector.tensor_tensor(shift, agg[:, 0:1], scale, ALU.mult))
            do(nc.vector.tensor_tensor(shift, cols[:, 1:2], shift, ALU.subtract))


def gat_layer(k, io, n):
    w = {m: io[f"L0_gnn_{m}{n}"] for m in ("Wl", "Wr", "bl", "br", "att")}
    node_tables(k, (w["Wl"],), (w["Wr"],), HE, HE, k.xl, k.node, (w["bl"], w["br"]), w["att"], f"{n}")
    edge_scores(k, w["att"], n)
    segment_softmax(k, n)
    aggregate(k, n - 1, n)


def relu_in_place(k, scale, shift, tag):
    nc = k.nc
    done = k.sem(f"u{tag}_done")
    with nc.Block() as block:
        @block.scalar
        def _(act):
            nc.scalar.activation(k.hT, k.hT, ACT.Relu, bias=shift, scale=scale).then_inc(done, 1)
            act.wait_ge(done, 1)


def residual_rows(k, io, scale, shift):
    nc = k.nc
    cut = Carver(k.work)
    stage = [cut(P) for _ in range(2)]
    xr = k.hT
    loaded, cleared = k.sem("e_loaded"), k.sem("e_cleared")
    staged, turned, kept = ([k.sem(f"e_{n}{s}") for s in range(2)] for n in ("staged", "turned", "kept"))
    with nc.Block() as block:
        @block.sync
        def _(sp):
            sp.wait_ge(cleared, 1)
            load_nodes(sp, io["x"], xr, loaded)

        @block.scalar
        def _(act):
            def relu(j, s):
                if reused(j):
                    act.wait_ge(turned[s], j)
                nc.scalar.activation(stage[s], k.y2[:, ds((2 * j + s) * P, P)], ACT.Relu, bias=shift,
                                     scale=scale).then_inc(staged[s], 1)

            pipeline(act, NB, [(0, relu)])

        @block.tensor
        def _(pe):
            def turn(j, s):
                pe.wait_ge(staged[s], j + 1)
                if reused(j):
                    pe.wait_ge(kept[s], j)
                nc.tensor.transpose(k.bank[s][:, 0:P], stage[s], k.ident[:, :]).then_inc(turned[s], 1)

            pipeline(pe, NB, [(0, turn)])

        @block.vector
        def _(dve):
            nc.vector.memset(xr[:, (NB - 1) * D:NB * D], 0.0).then_inc(cleared, 1)
            dve.wait_ge(loaded, 32)

            def add(j, s):
                at = ds((2 * j + s) * P, P)
                dve.wait_ge(turned[s], j + 1)
                nc.vector.tensor_tensor(k.y2[:, at], k.bank[s][:, 0:P], xr[:, at], ALU.add).then_inc(kept[s], 1)

            pipeline(dve, NB, [(0, add)])


def edge_attention(k, q_area, acc):
    nc = k.nc
    groups = T_SRC // G
    U = 4
    cut = Carver(k.wide)
    kv = [cut(G * KV) for _ in range(U)]
    prod = [cut(G * D) for _ in range(2)]
    pick = [cut(G * P) for _ in range(2)]
    place = [cut(G * P) for _ in range(2)]
    lo_bc = [cut(G * P // 2, BF16) for _ in range(U)]
    att = [cut(G * LH) for _ in range(2)]
    wv = [cut(G * VW) for _ in range(2)]
    w4 = [v.rearrange("p (u w) -> p u w", u=G) for v in wv]
    index = [cut(G, I32) for _ in range(U)]
    gathered = [k.gather_sem(f"f_gathered{s}") for s in range(U)]
    index_set, lo_ready = ([k.sem(f"f_{n}{s}") for s in range(U)] for n in ("index", "lo"))
    names = ("cleared", "picked", "looked", "mult", "att", "clip", "exp", "weighed", "summed", "added")
    cleared, picked, looked, multiplied, att_set, clipped, exped, weighed, summed, added = (k.sem(f"f_{n}") for n in names)
    with nc.Block() as block:
        @block.gpsimd
        def _(pool):
            def gather(j, s):
                g = U * j + s
                pool.wait_ge(index_set[s], 16 * j + 16)
                if later(g, U):
                    pool.wait_ge(weighed, g - U + 1)
                pool.nop(nofuse=True)
                for u in range(G):
                    pool.indirect_dma_start(kv[s][:, u * KV:(u + 1) * KV], None, k.kv,
                                            bass.IndirectOffsetOnAxis(ap=index[s][:, u:u + 1], axis=0)).then_inc(gathered[s], 16)

            pipeline(pool, groups, [(0, gather)], U)

        @block.sync
        def _(sp):
            def load(j, s):
                g = U * j + s
                if reused(j):
                    sp.wait_ge(gathered[s], 16 * G * j)
                    sp.nop(nofuse=True)
                    sp.wait_ge(picked, g - U + 1)
                    sp.nop(nofuse=True)
                sp.dma_start(lo_bc[s], k.lo_slot[ds(g * (G * P), G * P)].partition_broadcast(P)).then_inc(lo_ready[s], 16)
                sp.dma_start(index[s], k.gather_col[:, ds(g * G, G)]).then_inc(index_set[s], 16)

            pipeline(sp, groups, [(0, load)], U)

        @block.tensor
        def _(pe):
            def look(j, s):
                g = U * j + s
                pe.wait_ge(picked, g + 1)
                if later(g, 2):
                    pe.wait_ge(multiplied, g - 1)
                for u, b in enumerate(node_blocks(k, PE, g * G, G)):
                    last = nc.tensor.matmul(k.bank[s % 2][:, u * P:(u + 1) * P], pick[s % 2][:, u * P:(u + 1) * P],
                                            q_area[:, ds(b * D, D)], start=True, stop=True)
                last.then_inc(looked, 1)

            def sums(j, s):
                g = U * j + s
                pe.wait_ge(weighed, g + 1)
                for u in range(G):
                    if later(g):
                        pe.wait_ge(added, G * (g - 1) + u + 1)
                    nc.tensor.matmul(k.bank[2 + u][:, 0:VW], place[s % 2][:, u * P:(u + 1) * P],
                                     wv[s % 2][:, u * VW:(u + 1) * VW], start=True, stop=True).then_inc(summed, 1)

            pipeline(pe, groups, [(2, look), (0, sums)], U)

        @block.scalar
        def _(act):
            def weights(j, s):
                g = U * j + s
                act.wait_ge(clipped, g + 1)
                if later(g, 2):
                    act.wait_ge(summed, G * g - G)
                nc.scalar.activation(w4[s % 2][:, :, D:VW], att[s % 2].rearrange("p (u h) -> p u h", u=G),
                                     ACT.Exp).then_inc(exped, 1)

            pipeline(act, groups, [(0, weights)], U)

        @block.vector
        def _(dve):
            nc.vector.memset(acc, 0.0).then_inc(cleared, 1)
            dve.wait_ge(cleared, 1)

            def picks(j, s):
                g = U * j + s
                dve.wait_ge(lo_ready[s], 16 * j + 16)
                if later(g, 2):
                    dve.wait_ge(looked, g - 1)
                nc.vector.tensor_scalar(pick[s % 2], lo_bc[s], k.part_f[:, 0:1], None, ALU.is_equal).then_inc(picked, 1)

            def multiply(j, s):
                g = U * j + s
                dve.wait_ge(gathered[s], 16 * G * j + 16 * G)
                dve.wait_ge(looked, g + 1)
                keys = kv[s].rearrange("p (u d) -> p u d", u=G)[:, :, 0:D]
                if later(g, 2):
                    dve.wait_ge(att_set, g - 1)
                nc.vector.tensor_tensor(prod[s % 2].rearrange("p (u d) -> p u d", u=G), keys,
                                        k.bank[s % 2][:, 0:G * D].rearrange("p (u d) -> p u d", u=G),
                                        ALU.mult).then_inc(multiplied, 1)

            def reduce(j, s):
                g = U * j + s
                dve.wait_ge(multiplied, g + 1)
                if later(g, 2):
                    dve.wait_ge(exped, g - 1)
                nc.vector.tensor_reduce(att[s % 2], prod[s % 2].rearrange("p (q d) -> p q d", d=D // LH), AX_X,
                                        ALU.add).then_inc(att_set, 1)

            def clip(j, s):
                g = U * j + s
                dve.wait_ge(att_set, g + 1)
                nc.vector.tensor_scalar(att[s % 2], att[s % 2], -10.0, 10.0, ALU.max, ALU.min).then_inc(clipped, 1)

            def places(u0):
                def fn(j, s):
                    g = U * j + s
                    if later(g, 2):
                        dve.wait_ge(summed, G * g - G)
                    for u in (u0, u0 + 1):
                        nc.vector.tensor_scalar(place[s % 2][:, u * P:(u + 1) * P], k.iota_f[:, :],
                                                k.lo_col[:, ds(g * G + u, 1)], None, ALU.is_equal)
                return fn

            def weigh(j, s):
                g = U * j + s
                dve.wait_ge(exped, g + 1)
                ex = w4[s % 2][:, :, D:VW].unsqueeze(3).to_broadcast([P, G, LH, D // LH])
                v4 = kv[s].rearrange("p (u d) -> p u d", u=G)[:, :, D:KV].rearrange("p u (h d) -> p u h d", h=LH)
                nc.vector.tensor_tensor(w4[s % 2][:, :, 0:D].rearrange("p u (h d) -> p u h d", h=LH), v4, ex,
                                        ALU.mult).then_inc(weighed, 1)

            blocks = []

            def get_blocks(j, s):
                blocks[:] = node_blocks(k, DVE, (U * j + s) * G, G)

            def add(u):
                def fn(j, s):
                    g = U * j + s
                    dve.wait_ge(summed, G * g + u + 1)
                    if u > 0 or later(g):
                        dve.wait_ge(added, G * g + u)
                    to = acc[:, ds(blocks[u] * VW, VW)]
                    nc.vector.tensor_tensor(to, to, k.bank[2 + u][:, 0:VW], ALU.add).then_inc(added, 1)
                return fn

            pipeline(dve, groups, [(-1, get_blocks), (1, multiply), (-1, add(0)), (1, reduce), (-1, add(1)),
                                   (0, places(0)), (1, clip), (-1, add(2)), (0, places(2)), (-1, add(3)),
                                   (0, weigh), (3, picks)], U)


def finish(k, io, acc, h, x, scratch, square):
    nc = k.nc
    cut = Carver(k.work)
    mean, rstd, recip = cut(NB), cut(NB), cut(NB * LH)
    gain, bias = cut(D), cut(D)
    names = ("loaded", "order", "sq_ready", "squared", "var", "rooted", "ready", "stored")
    loaded, order, sq_ready, squared, var_ready, rooted, ready, stored = (k.sem(f"z_{n}") for n in names)
    acc3 = acc.rearrange("p (b w) -> p b w", w=VW)
    rows = scratch
    rows3 = rows.rearrange("p (b d) -> p b d", d=D)
    with nc.Block() as block:
        @block.sync
        def _(sp):
            sp.dma_start(gain, io["L1_gnn_ln_scale"].partition_broadcast(P)).then_inc(loaded, 16)
            sp.dma_start(bias, io["L1_gnn_ln_bias"].partition_broadcast(P)).then_inc(loaded, 16)
            sp.wait_ge(ready, 1)
            whole = (NB - 1) * P
            sp.dma_start(io["out"][0:whole, :].rearrange("(b p) d -> p b d", p=P),
                         rows[:, 0:(NB - 1) * D].rearrange("p (b d) -> p b d", d=D)).then_inc(stored, 16)
            sp.dma_start(io["out"][whole:N, :], rows[0:TAIL, (NB - 1) * D:NB * D]).then_inc(stored, 16)
            sp.wait_ge(stored, 32)

        @block.scalar
        def _(act):
            act.wait_ge(sq_ready, 1)
            nc.scalar.activation(square, rows, ACT.Square).then_inc(squared, 1)
            act.wait_ge(var_ready, 1)
            nc.scalar.activation(rstd, rstd, ACT.Sqrt).then_inc(rooted, 1)

        @block.vector
        def _(dve):
            do = Order(dve, order)
            r3 = recip.rearrange("p (b h) -> p b h", h=LH)
            do(nc.vector.tensor_scalar(r3, acc3[:, :, D:VW], 1e-8, None, ALU.add))
            do(nc.vector.reciprocal(recip, recip))
            do(nc.vector.tensor_tensor(rows3.rearrange("p b (h d) -> p b h d", h=LH),
                                       acc3[:, :, 0:D].rearrange("p b (h d) -> p b h d", h=LH),
                                       r3.unsqueeze(3).to_broadcast([P, NB, LH, D // LH]), ALU.mult))
            do(nc.vector.tensor_tensor(rows, rows, h, ALU.add))
            center(k, do, dve, rows, rows, square, mean, rstd, 1e-6, sq_ready, squared, var_ready, rooted)
            do(scale_rows(k, rows, rstd))
            dve.wait_ge(loaded, 32)
            do(nc.vector.tensor_tensor(rows3, rows3, gain.unsqueeze(1).to_broadcast([P, NB, D]), ALU.mult))
            do(nc.vector.tensor_tensor(rows3, rows3, bias.unsqueeze(1).to_broadcast([P, NB, D]), ALU.add))
            nc.vector.tensor_tensor(rows, rows, x, ALU.add).then_inc(ready, 1)


def program(nc, io):
    with ExitStack() as ctx:
        k = Core(nc, ctx)
        g = {n: io[f"L0_gnn_{n}"] for n in ("bl1", "bc1", "g1", "be1", "bl2", "bc2", "g2", "be2", "W1", "b1", "W2", "b2")}
        scale = ctx.enter_context(nc.sbuf_tensor("bn_scale", [P, 1], F32))
        shift = ctx.enter_context(nc.sbuf_tensor("bn_shift", [P, 1], F32))
        constants(k, io)
        sort_by_dst(k, io, SortBySrc(k))
        slot_tables(k, k.rec_d, k.block_d, 0, 1, True, "d")

        k.recycle()

        norm_to_features(k, k.y2, k.node[:, 0:NPAD], k.node[:, NPAD:2 * NPAD], io["x"], "0")
        gat_layer(k, io, 1)
        node_layer(k, (g["bl1"], g["bc1"]), (g["W1"], g["W2"][HD:2 * HD, :]),
                   ((k.hT, g["b1"], False), (k.y2, g["b2"], False)), "1")
        batch_norm(k, k.hT, g["g1"], g["be1"], scale[:, :], shift[:, :], "1")
        relu_in_place(k, scale[:, 0:1], shift[:, 0:1], "1")

        k.recycle()

        gat_layer(k, io, 2)
        node_layer(k, (g["bl2"], g["bc2"]), (g["W2"][0:HD, :],), ((k.y2, None, True),), "2")
        batch_norm(k, k.y2, g["g2"], g["be2"], scale[:, :], shift[:, :], "2")
        residual_rows(k, io, scale[:, 0:1], shift[:, 0:1])

        k.recycle()

        q_area, acc, h = k.node[:, 0:NPAD], k.node[:, NPAD:NPAD + NB * VW], k.node[:, NPAD + NB * VW:2 * NPAD + NB * VW]
        norm_to_features(k, k.y2, h, q_area, None, "3")
        node_tables(k, (io["L1_gnn_kTrans"], io["L1_gnn_vTrans"]), (io["L1_gnn_qTrans"],), KV, D, k.kv, q_area, (), None, "3")
        slot_tables(k, k.rec_s, k.block_s, 1, 0, False, "s")
        edge_attention(k, q_area, acc)
        finish(k, io, acc, h, k.y2, q_area, k.hT)


_INS = ["x", "src", "dst"] + [f"L0_gnn_{n}" for n in (
    "Wl1", "bl1", "Wr1", "br1", "att1", "bc1", "g1", "be1", "Wl2", "bl2", "Wr2", "br2", "att2", "bc2", "g2", "be2",
    "W1", "b1", "W2", "b2")] + [f"L1_gnn_{n}" for n in ("qTrans", "kTrans", "vTrans", "ln_scale", "ln_bias")]


def kernel(**inputs):
    import numpy as np
    import concourse.bacc as bacc
    from concourse.bass_utils import run_bass_kernel_spmd

    nc = bacc.Bacc("TRN2", target_bir_lowering=False, num_devices=1)
    arrays, io = {}, {}
    for name in _INS:
        a = np.ascontiguousarray(inputs[name])
        arrays[f"in_{name}"] = a
        io[name] = nc.dram_tensor(f"in_{name}", a.shape, mybir.dt.from_np(a.dtype), kind="ExternalInput").ap()
    io["out"] = nc.dram_tensor("out_0", (N, D), F32, kind="ExternalOutput").ap()
    program(nc, io)
    r = run_bass_kernel_spmd(nc, [arrays], core_ids=[0])
    return r.results[0]["out_0"]
```

```python
from contextlib import ExitStack

import concourse.bass as bass
from concourse import mybir

F32 = mybir.dt.float32
BF16 = mybir.dt.bfloat16
I32 = mybir.dt.int32
ALU = mybir.AluOpType
ACT = mybir.ActivationFunctionType
AX_X = mybir.AxisListType.X
PE, DVE = mybir.EngineType.PE, mybir.EngineType.DVE
ds = bass.ds

P = 128
N, D = 6250, 128
E = 100000
H = 3
HD = H * D
HE = HD + H
NB = -(-N // P)
NPAD = NB * P
TAIL = N - (NB - 1) * P

EC = 125
COLS = E // EC
CU = 8
RROWS = COLS // CU

TURNS = COLS // CU // 2
RANK_TURNS = TURNS * 41 // 50
NORM_TURNS = TURNS * 45 // 50

PAD_KEY = 16384
SLOTROW = 896
TG = SLOTROW // P
TILES = P * TG
SLOTS = TILES * P
G = 4
GS = 2
T_DST = -(-((E + N + NB * (P - 1)) // P) // (2 * G)) * 2 * G
T_SRC = -(-((E + NB * (P - 1)) // P) // (2 * G)) * 2 * G
assert max(T_DST, T_SRC) <= TILES

BLOCK_BITS = 6
assert NB <= 1 << BLOCK_BITS and G * BLOCK_BITS <= 24 and TILES % G == 0

LH = 8
KV = 2 * D
VW = D + LH
BIG = 3.0e38
SLOPE = 0.2

NODE_W = max(NB * HE, 2 * NPAD + NB * VW)
WORK_W = 5000


class Order:

    def __init__(self, eng, sem):
        self.eng, self.sem, self.n = eng, sem, 0

    def __call__(self, ins):
        ins.then_inc(self.sem, 1)
        self.n += 1
        self.eng.wait_ge(self.sem, self.n)
        return self.n


def later(g, n=1):
    return not isinstance(g, int) or g >= n


def reused(j):
    return later(j)


def snapped(eng, value):
    return value if isinstance(value, int) else eng.snap(value)


def pipeline(eng, groups, stages, unroll=2, number=False):
    ahead, behind = max(lead for lead, _ in stages), min(lead for lead, _ in stages)

    def at(turn, s):
        numbers = {}
        for lead, fn in stages:
            q = s + lead
            if isinstance(turn, int) and not 0 <= unroll * turn + q < groups:
                continue
            if not number:
                fn(turn + q // unroll, q % unroll)
                continue
            if q not in numbers:
                numbers[q] = snapped(eng, unroll * turn + q)
            fn(turn + q // unroll, q % unroll, numbers[q])

    first = -(-(unroll - behind) // unroll)
    last = (groups - ahead) // unroll
    for t in range(-ahead, unroll * first):
        at(t // unroll, t % unroll)
    with eng.Fori(first, last) as i:
        for s in range(unroll):
            at(i, s)
    for t in range(unroll * last, groups - behind):
        at(t // unroll, t % unroll)


class Carver:

    def __init__(self, area):
        self.area, self.at = area, 0

    def __call__(self, words, dtype=F32, parts=P):
        assert self.at + words <= self.area.shape[1], (self.at, words, self.area.shape)
        v = self.area[0:parts, self.at:self.at + words]
        self.at += words
        return v if dtype == F32 else v.bitcast(dtype)


class Core:

    def __init__(self, nc, ctx):
        self.nc, self.ctx = nc, ctx

        def sb(name, shape, dt):
            return ctx.enter_context(nc.sbuf_tensor(name, shape, dt))

        self.node = sb("node_area", [P, NODE_W], F32)
        self.feat = sb("feat_area", [P, 2 * NPAD + WORK_W], F32)
        self.y2 = self.feat[:, 0:NPAD]
        self.hT = self.feat[:, NPAD:2 * NPAD]
        self.work = self.feat[:, 2 * NPAD:2 * NPAD + WORK_W]
        self.wide = self.feat[:, NPAD:2 * NPAD + WORK_W]

        self.iota_f = sb("iota_f", [P, P], F32)
        self.iota_b = sb("iota_b", [P, P], BF16)
        self.part_f = sb("part_f", [P, 1], F32)
        self.tile_f = sb("tile_f", [P, TG], F32)
        self.node_i = sb("node_i", [P, NB], I32)
        self.valid = sb("valid", [P, NB], F32)
        self.ident = sb("ident", [P, P], F32)
        self.ones = sb("ones", [P, P], F32)
        self.upper = sb("upper", [P, P], F32)
        self.lower = sb("lower", [P, P], F32)

        self.pay = sb("pay", [EC, COLS, 2], I32)
        self.pos_s = sb("pos_s", [EC, COLS], I32)
        self.gather_col = sb("gather_col", [P, TILES], I32)
        self.lo_col = sb("lo_col", [P, TILES], F32)
        self.block_row = sb("block_row", [1, TILES // G], I32)
        self.keep_fwd = sb("keep_fwd", [P, SLOTROW], F32)
        self.keep_bwd = sb("keep_bwd", [P, SLOTROW], F32)
        self.wcol = sb("wcol", [P, TILES * H], F32)

        self.bank = [ctx.enter_context(nc.psum_tensor(f"bank{i}", [P, 512], F32)) for i in range(8)]

        def dram(name, shape, dt):
            return nc.dram_tensor(name, shape, dt, kind="Internal").ap()

        self.rec_d = dram("rec_by_dst", [SLOTS, 2], I32)
        self.rec_s = dram("rec_by_src", [SLOTS, 2], I32)
        self.lo_edge = dram("lo_edge", [E], BF16)
        self.lo_slot = dram("lo_slot", [SLOTS], BF16)
        self.block_d = dram("block_d", [TILES], I32)
        self.block_s = dram("block_s", [TILES], I32)
        self.xl = dram("xl_table", [NPAD, HE], F32)
        self.kv = dram("kv_table", [NPAD, KV], F32)
        self.spill = dram("spill", [T_DST, P, HD], F32)

        self.passing = []

    def sem(self, name):
        s = self.nc.alloc_semaphore(name)
        self.passing.append(s)
        return s

    def gather_sem(self, name):
        return self.ctx.enter_context(self.nc.semaphore(name))

    def recycle(self):
        with self.nc.Block() as block:
            @block.sync
            def _(sp):
                for s in self.passing:
                    sp.sem_clear(s)
        for s in self.passing:
            self.nc.release_semaphore(s)
        self.passing = []


def constants(k, io):
    nc = k.nc
    cut = Carver(k.node)
    row_i, part_i, tile_i = cut(P, I32), cut(1, I32), cut(TG, I32)
    fill_d, fill_s = cut(2 * SLOTROW, I32), cut(2 * SLOTROW, I32)
    node_f = cut(NB)
    made, filled, order, stored = k.sem("c_iota"), k.sem("c_fill"), k.sem("c_order"), k.sem("c_stored")
    with nc.Block() as block:
        @block.gpsimd
        def _(pool):
            nc.gpsimd.iota(row_i, pattern=[[1, P]], base=0, channel_multiplier=0).then_inc(made, 1)
            nc.gpsimd.iota(part_i, pattern=[[1, 1]], base=0, channel_multiplier=1).then_inc(made, 1)
            nc.gpsimd.iota(tile_i, pattern=[[1, TG]], base=0, channel_multiplier=TG).then_inc(made, 1)
            nc.gpsimd.iota(k.node_i[:, :], pattern=[[P, NB]], base=0, channel_multiplier=1).then_inc(made, 1)

        @block.vector
        def _(dve):
            do = Order(dve, order)
            do(nc.vector.memset(fill_d, 0))
            do(nc.vector.memset(fill_s, 0))
            nc.vector.memset(fill_d.rearrange("p (s f) -> p s f", f=2)[:, :, 1:2], PAD_KEY).then_inc(filled, 1)
            nc.vector.memset(fill_s.rearrange("p (s f) -> p s f", f=2)[:, :, 0:1], PAD_KEY).then_inc(filled, 1)
            dve.wait_ge(made, 4)
            do(nc.vector.tensor_copy(k.iota_f[:, :], row_i))
            do(nc.vector.tensor_copy(k.iota_b[:, :], row_i))
            do(nc.vector.tensor_copy(k.part_f[:, :], part_i))
            do(nc.vector.tensor_copy(k.tile_f[:, :], tile_i))
            do(nc.vector.tensor_copy(node_f, k.node_i[:, :]))
            do(nc.vector.tensor_scalar(k.valid[:, :], node_f, float(N), None, ALU.is_lt))
            do(nc.vector.tensor_scalar(k.ident[:, :], k.iota_f[:, :], k.part_f[:, 0:1], None, ALU.is_equal))
            do(nc.vector.tensor_scalar(k.upper[:, :], k.iota_f[:, :], k.part_f[:, 0:1], None, ALU.is_gt))
            do(nc.vector.tensor_scalar(k.lower[:, :], k.iota_f[:, :], k.part_f[:, 0:1], None, ALU.is_lt))
            do(nc.vector.memset(k.ones[:, :], 1.0))

        @block.sync
        def _(sp):
            sp.wait_ge(filled, 2)
            for rec, fill in ((k.rec_d, fill_d), (k.rec_s, fill_s)):
                sp.dma_start(rec.rearrange("(p s) f -> p (s f)", p=P), fill).then_inc(stored, 16)
            sp.wait_ge(stored, 32)


def sort_by_dst(k, io, beside):
    nc = k.nc
    cut = Carver(k.node)
    raw = {"src": cut(CU * EC, I32, RROWS), "dst": cut(CU * EC, I32, RROWS)}
    rows = {"src": cut(CU * EC, F32, RROWS), "dst": cut(CU * EC, F32, RROWS)}
    lo_i = cut(CU * EC, I32, RROWS)
    lo_b = cut(CU * EC // 2, BF16, RROWS)
    key = {"src": cut(COLS, F32, EC), "dst": cut(COLS, F32, EC)}
    key_i = cut(COLS, I32, EC)
    part_i = cut(COLS, I32, EC)
    lo, hi = cut(COLS // 2, BF16, EC), cut(COLS // 2, BF16, EC)
    cnt, start, table0 = cut(NB), cut(NB), cut(NB)
    tot_i, tiles_f, tend, tbase = cut(NB, I32), cut(NB), cut(NB), cut(NB)
    self_pos = cut(NB, I32)
    self_rec = cut(2 * NB, I32).rearrange("p (b f) -> p b f", f=2)
    blk_f, blk_i = cut(TG), cut(TG, I32)
    junk = cut(NB)
    HALF = CU // 2
    oh_lo = [cut(HALF * P // 2, BF16, EC).rearrange("p (u m) -> p u m", u=HALF) for _ in range(2)]
    oh_hi = [cut(HALF * 25, BF16, EC).rearrange("p (u m) -> p u m", u=HALF) for _ in range(2)]
    key_bc = [cut(HALF * EC, I32) for _ in range(2)]
    lo_bc = [cut(HALF * EC // 2, BF16) for _ in range(2)]
    oh_loT = [cut(HALF * EC) for _ in range(2)]
    table = [cut(NB) for _ in range(2)]
    before = [cut(HALF, F32, EC) for _ in range(2)]
    peers = [cut(HALF, F32, EC) for _ in range(2)]
    records = Records(k)
    pos_d = records.pos
    junk_e = [[cut(EC, F32, EC) for _ in range(HALF)] for _ in range(2)]
    junk_m = [cut(NB, F32, EC) for _ in range(HALF)]

    def one_hot_rows(out, part, col, width):
        shape = [EC, HALF, width]
        return nc.vector.tensor_tensor(out[:, :, 0:width], k.iota_b[0:EC, 0:width].unsqueeze(1).to_broadcast(shape),
                                       part[:, ds(col, HALF)].unsqueeze(2).to_broadcast(shape), ALU.is_equal)

    loaded, order, lo_ready = k.sem("k_loaded"), k.sem("k_order"), k.sem("k_lo_ready")
    rows_ready, turned, stored, keys_done = k.sem("k_rows"), k.sem("k_turned"), k.sem("k_stored"), k.sem("k_copied")
    with nc.Block() as block:
        @block.sync
        def _(sp):
            for name in ("dst", "src"):
                sp.dma_start(raw[name], io[name].rearrange("(r e) -> r e", r=RROWS)).then_inc(loaded, 16)
            sp.wait_ge(lo_ready, 1)
            sp.dma_start(k.lo_edge.rearrange("(r e) -> r e", r=RROWS), lo_b).then_inc(stored, 16)
            sp.wait_ge(stored, 16)

        @block.vector
        def _(dve):
            do = Order(dve, order)
            dve.wait_ge(loaded, 32)
            nc.vector.tensor_copy(rows["dst"], raw["dst"]).then_inc(rows_ready, 1)
            nc.vector.tensor_copy(rows["src"], raw["src"]).then_inc(rows_ready, 1)
            do(nc.vector.tensor_scalar(lo_i, raw["dst"], P - 1, None, ALU.bitwise_and))
            nc.vector.tensor_copy(lo_b, lo_i).then_inc(lo_ready, 1)
            for n, name in enumerate(("dst", "src")):
                for half in range(2):
                    dve.wait_ge(turned, 2 * n + half + 1)
                    dst = key[name].rearrange("p (r g) -> p g r", g=CU)[:, 4 * half:4 * half + 4, :]
                    do(nc.vector.tensor_copy(dst, k.bank[2 * n + half][0:EC, 0:4 * RROWS].rearrange("p (g r) -> p g r", g=4)))
            do(nc.vector.tensor_copy(k.pay[:, :, 0], key["src"]))
            do(nc.vector.tensor_copy(k.pay[:, :, 1], key["dst"]))
            do(nc.vector.tensor_copy(key_i, key["dst"]))
            do(nc.vector.tensor_scalar(part_i, key_i, P - 1, None, ALU.bitwise_and))
            do(nc.vector.tensor_copy(lo, part_i))
            do(nc.vector.tensor_scalar(part_i, key_i, 7, None, ALU.logical_shift_right))
            do(nc.vector.tensor_copy(hi, part_i))
            beside.key_blocks(do, key["src"])

        @block.tensor
        def _(pe):
            for n, name in enumerate(("dst", "src")):
                pe.wait_ge(rows_ready, n + 1)
                for half in range(2):
                    for g in range(4):
                        c = (4 * half + g) * EC
                        last = nc.tensor.transpose(k.bank[2 * n + half][0:EC, g * RROWS:(g + 1) * RROWS],
                                                   rows[name][:, c:c + EC], k.ident[0:RROWS, 0:RROWS])
                    last.then_inc(turned, 1)

    oh_ready = [k.sem(f"h_ready{s}") for s in range(2)]
    oh_free = [k.sem(f"h_free{s}") for s in range(2)]
    counts = k.bank[0][:, 0:NB]
    halves = COLS // HALF
    HU = 8
    with nc.Block() as block:
        @block.vector
        def _(dve):
            with dve.Fori(0, halves // HU) as i:
                for n in range(HU):
                    s = n % 2
                    dve.wait_ge(oh_free[s], HU // 2 * i + n // 2 + 1)
                    c = HU * HALF * i + n * HALF
                    one_hot_rows(oh_lo[s], lo, c, P)
                    one_hot_rows(oh_hi[s], hi, c, NB).then_inc(oh_ready[s], 1)

        @block.scalar
        def _(act):
            beside.count(act)

        @block.tensor
        def _(pe):
            nc.tensor.matmul(counts, k.ident[:, :], k.valid[:, :], start=True, stop=True)
            for s in range(2):
                pe.sem_inc(oh_free[s], 1)
            with pe.Fori(0, halves // HU) as i:
                for n in range(HU):
                    s = n % 2
                    pe.wait_ge(oh_ready[s], HU // 2 * i + n // 2 + 1)
                    for u in range(HALF):
                        last = nc.tensor.matmul(counts, oh_lo[s][:, u, :], oh_hi[s][:, u, 0:NB], start=False, stop=True,
                                                skip_group_check=True)
                    last.then_inc(oh_free[s], 1)

    order, cnt_ready, summed = k.sem("t_order"), k.sem("t_cnt"), k.sem("t_summed")
    blk_ready, stored, scattered = k.sem("t_blk"), k.sem("t_stored"), k.gather_sem("t_scat")
    with nc.Block() as block:
        @block.vector
        def _(dve):
            do = Order(dve, order)
            nc.vector.tensor_copy(cnt, counts).then_inc(cnt_ready, 1)
            dve.wait_ge(summed, 1)
            block_tiles(k, do, k.bank[1][:, 0:NB], tot_i, tiles_f, tend, tbase, blk_f, blk_i, junk)
            nc.vector.tensor_copy(blk_i, blk_f).then_inc(blk_ready, 1)
            do(nc.vector.scalar_tensor_tensor(out=start, in0=tbase, scalar=float(P), in1=k.bank[2][:, 0:NB],
                                              op0=ALU.mult, op1=ALU.add))
            do(nc.vector.tensor_tensor(table0, start, k.valid[:, :], ALU.add))
            do(nc.vector.tensor_copy(self_rec[:, :, 0], k.node_i[:, :]))
            do(nc.vector.tensor_copy(self_rec[:, :, 1], k.node_i[:, :]))
            do(nc.vector.tensor_copy(self_pos, start))

        @block.tensor
        def _(pe):
            pe.wait_ge(cnt_ready, 1)
            nc.tensor.matmul(k.bank[1][:, 0:NB], k.ones[:, :], cnt, start=True, stop=True)
            nc.tensor.matmul(k.bank[2][:, 0:NB], k.upper[:, :], cnt, start=True, stop=True).then_inc(summed, 1)

        @block.sync
        def _(sp):
            sp.wait_ge(blk_ready, 1)
            sp.dma_start(k.block_d.rearrange("(p g) -> p g", p=P), blk_i).then_inc(stored, 16)
            sp.wait_ge(stored, 16)

    bc_ready = [k.sem(f"r_bc{s}") for s in range(2)]
    names = ("init", "copied", "looked", "updated", "onehot", "peers", "sums", "ranked")
    inited, copied, looked, updated, ohT_ready, peered, summed, ranked = (k.sem(f"r_{n}") for n in names)
    run = k.bank[3][:, 0:NB]
    look = [k.bank[4 + u][0:EC, 0:NB] for u in range(HALF)]
    with nc.Block() as block:
        @block.sync
        def _(sp):
            def load_keys(j, s):
                h = 2 * j + s
                if reused(j):
                    sp.wait_ge(peered, h - 1)
                at = h * (HALF * EC)
                sp.dma_start(key_bc[s], io["dst"][ds(at, HALF * EC)].partition_broadcast(P)).then_inc(bc_ready[s], 16)
                sp.dma_start(lo_bc[s], k.lo_edge[ds(at, HALF * EC)].partition_broadcast(P)).then_inc(bc_ready[s], 16)

            pipeline(sp, halves, [(0, load_keys)])
            beside.on_sync(sp)

        @block.scalar
        def _(act):
            def copy_table(j, s):
                c = 2 * j + s
                if later(c):
                    act.wait_ge(updated, c)
                else:
                    act.wait_ge(inited, 1)
                if later(c, 2):
                    act.wait_ge(looked, c - 1)
                nc.scalar.copy(table[s], run).then_inc(copied, 1)

            pipeline(act, COLS, [(0, copy_table)])
            beside.on_scalar(act)

        @block.tensor
        def _(pe):
            nc.tensor.matmul(run, k.ident[:, :], table0, start=True, stop=True).then_inc(inited, 1)
            pe.wait_ge(inited, 1)

            def look_up(j, s):
                h = 2 * j + s
                pe.wait_ge(ohT_ready, h + 1)
                for u in range(HALF):
                    c = HALF * h + u
                    pe.wait_ge(copied, c + 1)
                    if later(h):
                        pe.wait_ge(summed, c - HALF + 1)
                    nc.tensor.matmul(run, oh_lo[s][:, u, :], oh_hi[s][:, u, 0:NB], start=False, stop=True,
                                     skip_group_check=True).then_inc(updated, 1)
                    nc.tensor.matmul(look[u], oh_loT[s][:, u * EC:(u + 1) * EC], table[u % 2],
                                     start=True, stop=True).then_inc(looked, 1)

            pipeline(pe, halves, [(0, look_up)])
            beside.on_tensor(pe)

        @block.vector
        def _(dve):
            ahead, here = [], []

            def columns_of(which):
                def fn(j, s):
                    c = snapped(dve, HALF * (2 * j + s))
                    which[:] = [c] + [snapped(dve, c + u) for u in range(1, HALF + 1)]
                return fn

            def one_hots(j, s):
                h = 2 * j + s
                if reused(j):
                    dve.wait_ge(updated, HALF * h - HALF)
                    dve.wait_ge(summed, HALF * h - HALF)
                one_hot_rows(oh_lo[s], lo, ahead[0], P)
                one_hot_rows(oh_hi[s], hi, ahead[0], NB)

            def key_columns(j, s):
                h = 2 * j + s
                if reused(j):
                    dve.wait_ge(looked, HALF * h - HALF)
                dve.wait_ge(bc_ready[s], 32 * j + 32)
                nc.vector.tensor_scalar(oh_loT[s], lo_bc[s], k.part_f[:, 0:1], None, ALU.is_equal).then_inc(ohT_ready, 1)

            def count_peers(j, s):
                h = 2 * j + s
                if reused(j):
                    dve.wait_ge(ranked, h - 1)
                for u in range(HALF):
                    c = ahead[u]
                    last = nc.vector.scalar_tensor_tensor(out=junk_e[s][u], in0=key_bc[s][0:EC, u * EC:(u + 1) * EC],
                                                          scalar=key["dst"][:, ds(c, 1)], in1=k.lower[0:EC, 0:EC],
                                                          op0=ALU.is_equal, op1=ALU.mult, accum_out=peers[s][:, u:u + 1])
                last.then_inc(peered, 1)

            def read_table(u):
                def fn(j, s):
                    h = 2 * j + s
                    if u == 0 and later(h):
                        dve.wait_ge(summed, here[0])
                    if u == 0 and later(h, 2):
                        dve.wait_ge(ranked, h - 1)
                    dve.wait_ge(looked, here[u + 1])
                    nc.vector.scalar_tensor_tensor(out=junk_m[u], in0=look[u], scalar=1.0, in1=oh_hi[s][:, u, 0:NB],
                                                   op0=ALU.mult, op1=ALU.mult, accum_out=before[s][:, u:u + 1]
                                                   ).then_inc(summed, 1)
                return fn

            def slots(j, s):
                h = 2 * j + s
                dve.wait_ge(summed, here[HALF])
                dve.wait_ge(peered, h + 1)
                nc.vector.tensor_tensor(pos_d[:, ds(here[0], HALF)], before[s], peers[s], ALU.add).then_inc(ranked, 1)

            pipeline(dve, halves, [(1, columns_of(ahead)), (0, columns_of(here)), (1, one_hots), (0, read_table(0)),
                                   (0, read_table(1)), (1, key_columns), (0, read_table(2)), (0, read_table(3)),
                                   (1, count_peers), (0, slots)])
            beside.on_vector(dve)

        @block.gpsimd
        def _(pool):
            for b in range(NB):
                n = P if b < NB - 1 else TAIL
                pool.indirect_dma_start(k.rec_d, bass.IndirectOffsetOnAxis(ap=self_pos[0:n, b:b + 1], axis=0),
                                        self_rec[0:n, b, :], None).then_inc(scattered, 16)

            records.write(pool, 0, RANK_TURNS, ranked)
            pool.wait_ge(scattered, 16 * NB)
    return records


class Records:

    def __init__(self, k):
        self.k = k
        cut = Carver(k.wcol)
        self.pos = cut(COLS, I32, EC)
        self.slot = [cut(CU, I32, EC) for _ in range(2)]
        self.rec = [cut(2 * CU, I32, EC).rearrange("p (u f) -> p u f", f=2) for _ in range(2)]
        self.written = [k.gather_sem(f"r_written{s}") for s in range(2)]
        self.staged = k.sem("r_staged")

    def write(self, pool, first, last, ranked=None):
        def turn(j):
            for s in range(2):
                if ranked is not None:
                    pool.wait_ge(ranked, 4 * j + 2 * s + 2)
                    pool.nop(nofuse=True)
                scatter_columns(self.k, pool, self.pos, self.k.rec_d, self.rec[s], self.slot[s], self.staged,
                                self.written[s], j, s)

        if first == 0:
            turn(0)
        with pool.Fori(max(first, 1), last) as i:
            turn(i)
        if last == TURNS:
            for s in range(2):
                pool.wait_ge(self.written[s], 16 * CU * TURNS)


def scatter_columns(k, pool, pos, table, rec, slot, staged, written, j, s, n=CU, first=0):
    nc = k.nc
    step = 2 * j + s
    if reused(j):
        pool.wait_ge(written, 16 * n * j)
        pool.nop(nofuse=True)
    nc.gpsimd.tensor_copy(rec, k.pay[:, ds(step * n + first, n), :]).then_inc(staged, 1)
    nc.gpsimd.tensor_copy(slot, pos[:, ds(step * n + first, n)]).then_inc(staged, 1)
    pool.wait_ge(staged, 2 * step + 2)
    pool.nop(nofuse=True)
    for u in range(n):
        pool.indirect_dma_start(table, bass.IndirectOffsetOnAxis(ap=slot[:, u:u + 1], axis=0),
                                rec[:, u, :], None).then_inc(written, 16)


def block_tiles(k, do, total, tot_i, tiles_f, tend, tbase, blk_f, blk_i, junk):
    nc = k.nc
    do(nc.vector.tensor_scalar(tot_i, total, float(P - 1), None, ALU.add))
    do(nc.vector.tensor_scalar(tot_i, tot_i, 7, None, ALU.logical_shift_right))
    do(nc.vector.tensor_copy(tiles_f, tot_i))
    do(nc.vector.tensor_tensor_scan(tend, k.ones[:, 0:NB], tiles_f, 0.0, ALU.mult, ALU.add))
    do(nc.vector.tensor_tensor(tbase, tend, tiles_f, ALU.subtract))
    for g in range(TG):
        do(nc.vector.tensor_scalar(junk, tend, k.tile_f[:, g:g + 1], None, ALU.is_le, ALU.add,
                                   accum_out=blk_f[:, g:g + 1]))
    do(nc.vector.tensor_scalar(blk_f, blk_f, float(NB - 1), None, ALU.min))


class SortBySrc:

    def __init__(self, k):
        self.k = k
        cut = Carver(k.feat)
        self.key_i, self.hi = cut(COLS, I32, EC), cut(COLS, F32, EC)
        self.away = [cut(COLS, F32, EC) for _ in range(2)]
        self.oh = [cut(COLS, F32, EC) for _ in range(2)]
        self.rank = cut(COLS, F32, EC)
        self.term = [cut(COLS, F32, EC) for _ in range(2)]
        self.lane, self.first = cut(NB, F32, EC), cut(NB, F32, EC)
        self.tot_i, self.tiles_f, self.tend, self.tbase = cut(NB, I32), cut(NB), cut(NB), cut(NB)
        self.blk_f, self.blk_i, self.junk = cut(TG), cut(TG, I32), cut(NB)
        names = ("order", "away", "counted", "summed", "blk", "stored", "based", "oh", "term", "kept")
        (self.order, self.away_ready, self.counted, self.summed, self.blk_ready, self.stored, self.based, self.oh_ready,
         self.term_ready, self.kept) = (k.sem(f"s_{n}") for n in names)
        self.halves = [slice(0, COLS // 2), slice(COLS // 2, COLS)]
        self.total = [k.bank[0][0:EC, 0:COLS // 2], k.bank[1][0:EC, 0:COLS // 2]]

    def key_blocks(self, do, src_key):
        nc = self.k.nc
        do(nc.vector.tensor_copy(self.key_i, src_key))
        do(nc.vector.tensor_scalar(self.key_i, self.key_i, 7, None, ALU.logical_shift_right))
        do(nc.vector.tensor_copy(self.hi, self.key_i))

    def one_hot(self, act, n, b, out, **sums):
        nc, k, away = self.k.nc, self.k, self.away[n % 2]
        nc.scalar.activation(away, self.hi, ACT.Abs, scale=-1.0, bias=k.iota_f[0:EC, b:b + 1]).then_inc(self.away_ready, 1)
        act.wait_ge(self.away_ready, n + 1)
        return nc.scalar.activation(out, away, ACT.Relu, scale=-1.0, bias=k.ones[0:EC, 0:1], **sums)

    def count(self, act):
        for b in range(NB):
            if b >= 2:
                act.wait_ge(self.counted, b - 1)
            self.one_hot(act, b, b, self.oh[b % 2], accum_out=self.lane[:, b:b + 1]).then_inc(self.counted, 1)

    def on_scalar(self, act):
        for b in range(NB):
            if b >= 2:
                act.wait_ge(self.term_ready, b - 1)
                act.wait_ge(self.oh_ready, b - 1)
            else:
                act.wait_ge(self.counted, NB)
            self.one_hot(act, NB + b, b, self.oh[b % 2]).then_inc(self.oh_ready, 1)

    def on_vector(self, dve):
        k, nc, rank = self.k, self.k.nc, self.rank
        do = Order(dve, self.order)
        dve.wait_ge(self.summed, 1)
        block_tiles(k, do, k.bank[2][:, 0:NB], self.tot_i, self.tiles_f, self.tend, self.tbase, self.blk_f, self.blk_i,
                    self.junk)
        nc.vector.tensor_copy(self.blk_i, self.blk_f).then_inc(self.blk_ready, 1)
        do(nc.vector.scalar_tensor_tensor(out=self.first, in0=self.tbase[0:EC, :], scalar=float(P),
                                          in1=k.bank[2][0:EC, NB:2 * NB], op0=ALU.mult, op1=ALU.add))
        do(nc.vector.tensor_scalar(self.first, self.first, -1.0, None, ALU.add))
        for b in range(NB):
            oh = self.oh[b % 2]
            dve.wait_ge(self.oh_ready, b + 1)
            do(nc.vector.tensor_tensor_scan(rank, oh, oh, self.first[:, b:b + 1], ALU.add, ALU.bypass))
            if b >= 2:
                dve.wait_ge(self.kept, b - 1)
            nc.vector.tensor_tensor(self.term[b % 2], rank, oh, ALU.mult).then_inc(self.term_ready, 1)
            dve.wait_ge(self.term_ready, b + 1)
        dve.wait_ge(self.kept, NB)
        for half, total in zip(self.halves, self.total):
            do(nc.vector.tensor_copy(k.pos_s[:, half], total))

    def on_tensor(self, pe):
        k, nc = self.k, self.k.nc
        pe.wait_ge(self.counted, NB)
        nc.tensor.matmul(k.bank[2][:, 0:NB], k.ones[0:EC, :], self.lane, start=True, stop=True)
        nc.tensor.matmul(k.bank[2][0:EC, NB:2 * NB], k.upper[0:EC, 0:EC], self.lane, start=True,
                         stop=True).then_inc(self.summed, 1)
        for b in range(NB):
            pe.wait_ge(self.term_ready, b + 1)
            for half, total in zip(self.halves, self.total):
                last = nc.tensor.matmul(total, k.ident[0:EC, 0:EC], self.term[b % 2][:, half], start=b == 0, stop=True,
                                        skip_group_check=b > 0)
            last.then_inc(self.kept, 1)

    def on_sync(self, sp):
        k = self.k
        sp.wait_ge(self.blk_ready, 1)
        sp.dma_start(k.block_s.rearrange("(p g) -> p g", p=P), self.blk_i).then_inc(self.stored, 16)
        sp.wait_ge(self.stored, 16)


def slot_tables(k, rec, block_dram, gathered, key, ends, tag, sums=None):
    nc = k.nc
    cut = Carver(k.wide)
    raw = cut(2 * SLOTROW, I32)
    pair = raw.rearrange("p (s f) -> p s f", f=2)
    node_f, key_f = cut(SLOTROW), cut(SLOTROW)
    lo_i, lo_f, lo_b = cut(SLOTROW, I32), cut(SLOTROW), cut(SLOTROW // 2, BF16)
    edge_i, edge_f = cut(4, I32), cut(4)
    block_i, block_f, word = cut(TILES, I32, 1), cut(TILES, F32, 1), cut(TILES // G, F32, 1)
    loaded, order, rows_ready, turned = (k.sem(f"l{tag}_loaded"), k.sem(f"l{tag}_order"), k.sem(f"l{tag}_rows"),
                                         k.sem(f"l{tag}_turned"))
    lo_ready, stored, edges_set = k.sem(f"l{tag}_lo"), k.sem(f"l{tag}_stored"), k.sem(f"l{tag}_edges")
    rec_rows = rec.rearrange("(p s) f -> p s f", p=P)
    with nc.Block() as block:
        if sums is not None:
            @block.gpsimd
            def _(pool):
                nc.gpsimd.memset(sums, 0.0)

        @block.sync
        def _(sp):
            sp.dma_start(raw, rec.rearrange("(p s) f -> p (s f)", p=P)).then_inc(loaded, 16)
            sp.dma_start(block_i, block_dram.rearrange("(o t) -> o t", o=1)).then_inc(loaded, 16)
            if ends:
                sp.wait_ge(edges_set, 1)
                sp.dma_start(edge_i[1:P, 0:2], rec_rows[0:P - 1, SLOTROW - 1, :]).then_inc(loaded, 16)
                sp.dma_start(edge_i[0:P - 1, 2:4], rec_rows[1:P, 0, :]).then_inc(loaded, 16)
            sp.wait_ge(lo_ready, 1)
            sp.dma_start(k.lo_slot.rearrange("(p s) -> p s", p=P), lo_b).then_inc(stored, 16)
            sp.wait_ge(stored, 16)

        @block.vector
        def _(dve):
            do = Order(dve, order)
            if ends:
                nc.vector.memset(edge_i, -1).then_inc(edges_set, 1)
            dve.wait_ge(loaded, 64 if ends else 32)
            do(nc.vector.tensor_copy(node_f, pair[:, :, gathered]))
            do(nc.vector.tensor_copy(block_f, block_i))
            of_tile = block_f.rearrange("o (w u) -> o w u", u=G)
            do(nc.vector.tensor_copy(word, of_tile[:, :, G - 1]))
            for u in range(G - 2, -1, -1):
                do(nc.vector.scalar_tensor_tensor(out=word, in0=word, scalar=float(1 << BLOCK_BITS), in1=of_tile[:, :, u],
                                                  op0=ALU.mult, op1=ALU.add))
            do(nc.vector.tensor_copy(k.block_row[:, :], word))
            do(nc.vector.tensor_scalar(lo_i, pair[:, :, key], PAD_KEY | (P - 1), None, ALU.bitwise_and))
            nc.vector.tensor_copy(lo_f, lo_i).then_inc(rows_ready, 1)
            nc.vector.tensor_copy(lo_b, lo_i).then_inc(lo_ready, 1)
            if ends:
                do(nc.vector.tensor_copy(key_f, pair[:, :, key]))
                do(nc.vector.tensor_copy(edge_f, edge_i))
                here, there = key_f[:, 1:SLOTROW], key_f[:, 0:SLOTROW - 1]
                do(nc.vector.tensor_tensor(k.keep_fwd[:, 1:SLOTROW], here, there, ALU.is_equal))
                do(nc.vector.tensor_tensor(k.keep_bwd[:, 0:SLOTROW - 1], here, there, ALU.is_equal))
                do(nc.vector.tensor_tensor(k.keep_fwd[:, 0:1], key_f[:, 0:1], edge_f[:, key:key + 1], ALU.is_equal))
                do(nc.vector.tensor_tensor(k.keep_bwd[:, SLOTROW - 1:SLOTROW], key_f[:, SLOTROW - 1:SLOTROW],
                                           edge_f[:, 2 + key:3 + key], ALU.is_equal))
            for n, col in enumerate((k.gather_col, k.lo_col)):
                for half, (g0, g1) in enumerate(((0, 4), (4, TG))):
                    dve.wait_ge(turned, 2 * n + half + 1)
                    out = col[:, :].rearrange("p (t g) -> p g t", g=TG)[:, g0:g1, :]
                    ps = k.bank[2 * n + half][:, 0:(g1 - g0) * P].rearrange("p (g t) -> p g t", t=P)
                    do(nc.vector.tensor_copy(out, ps))

        @block.tensor
        def _(pe):
            pe.wait_ge(rows_ready, 1)
            for n, rows in enumerate((node_f, lo_f)):
                for half, (g0, g1) in enumerate(((0, 4), (4, TG))):
                    for g in range(g0, g1):
                        last = nc.tensor.transpose(k.bank[2 * n + half][:, (g - g0) * P:(g - g0 + 1) * P],
                                                   rows[:, g * P:(g + 1) * P], k.ident[:, :])
                    last.then_inc(turned, 1)


def block_words(k, engine, word, n):
    return k.nc.values_load_multi_w_load_instructions(
        k.block_row[0:1, ds(word, n)], engines=(engine,), min_val=0, max_val=(1 << G * BLOCK_BITS) - 1,
        skip_runtime_bounds_check_because="every block was limited to NB - 1 before it was packed")[1]


def block_columns(eng, packed, tiles, width):
    blocks = [((packed >> (BLOCK_BITS * u)) & ((1 << BLOCK_BITS) - 1)).with_bounds(min_val=0, max_val=NB - 1) for u in tiles]
    return [eng.snap(b * width) for b in blocks]


def key_rows(k, out, tile, n):
    shape = [P, n, P]
    return k.nc.vector.tensor_tensor(out.rearrange("p (u m) -> p u m", u=n), k.iota_f[:, :].unsqueeze(1).to_broadcast(shape),
                                     k.lo_col[:, ds(tile, n)].unsqueeze(2).to_broadcast(shape), ALU.is_equal)


def load_nodes(sp, x, area, loaded):
    whole = (NB - 1) * P
    sp.dma_start(area[:, 0:(NB - 1) * D].rearrange("p (b d) -> p b d", d=D),
                 x[0:whole, :].rearrange("(b p) d -> p b d", p=P)).then_inc(loaded, 16)
    sp.dma_start(area[0:TAIL, (NB - 1) * D:NB * D], x[whole:N, :]).then_inc(loaded, 16)


def center(k, do, dve, x, xc, square, mean, rstd, eps, sq_ready, squared, var_ready, rooted):
    nc = k.nc
    x3 = x.rearrange("p (b d) -> p b d", d=D)
    xc3 = xc.rearrange("p (b d) -> p b d", d=D)
    do(nc.vector.tensor_reduce(mean, x3, AX_X, ALU.add))
    do(nc.vector.tensor_scalar(mean, mean, 1.0 / D, None, ALU.mult))
    nc.vector.tensor_tensor(xc3, x3, mean.unsqueeze(2).to_broadcast([P, NB, D]), ALU.subtract).then_inc(sq_ready, 1)
    dve.wait_ge(squared, 1)
    do(nc.vector.tensor_reduce(rstd, square.rearrange("p (b d) -> p b d", d=D), AX_X, ALU.add))
    nc.vector.tensor_scalar(rstd, rstd, 1.0 / D, eps, ALU.mult, ALU.add).then_inc(var_ready, 1)
    dve.wait_ge(rooted, 1)
    do(nc.vector.reciprocal(rstd, rstd))


def scale_rows(k, rows, by):
    rows3 = rows.rearrange("p (b d) -> p b d", d=D)
    return k.nc.vector.tensor_tensor(rows3, rows3, by.unsqueeze(2).to_broadcast([P, NB, D]), ALU.mult)


def norm_to_features(k, x, rows, scratch, load, tag, records=None):
    nc = k.nc
    cut = Carver(k.work)
    mean, rstd = cut(NB), cut(NB)
    stage = [cut(P) for _ in range(2)]
    names = ("loaded", "order", "sq_ready", "squared", "var", "rooted", "ready", "cleared")
    loaded, order, sq_ready, squared, var_ready, rooted, ready, cleared = (k.sem(f"n{tag}_{n}") for n in names)
    staged = [k.sem(f"n{tag}_staged{s}") for s in range(2)]
    turned = [k.sem(f"n{tag}_turned{s}") for s in range(2)]
    kept = [k.sem(f"n{tag}_kept{s}") for s in range(2)]
    with nc.Block() as block:
        if records is not None:
            @block.gpsimd
            def _(pool):
                records.write(pool, RANK_TURNS, NORM_TURNS)

        if load is not None:
            @block.sync
            def _(sp):
                sp.wait_ge(cleared, 1)
                load_nodes(sp, load, x, loaded)

        @block.scalar
        def _(act):
            act.wait_ge(sq_ready, 1)
            nc.scalar.activation(scratch, rows, ACT.Square).then_inc(squared, 1)
            act.wait_ge(var_ready, 1)
            nc.scalar.activation(rstd, rstd, ACT.Sqrt).then_inc(rooted, 1)
            act.wait_ge(ready, 1)

            def relu(j, s):
                if reused(j):
                    act.wait_ge(turned[s], j)
                nc.scalar.activation(stage[s], rows[:, ds((2 * j + s) * P, P)], ACT.Relu).then_inc(staged[s], 1)

            pipeline(act, NB, [(0, relu)])

        @block.tensor
        def _(pe):
            def turn(j, s):
                pe.wait_ge(staged[s], j + 1)
                if reused(j):
                    pe.wait_ge(kept[s], j)
                nc.tensor.transpose(k.bank[s][:, 0:P], stage[s], k.ident[:, :]).then_inc(turned[s], 1)

            pipeline(pe, NB, [(0, turn)])

        @block.vector
        def _(dve):
            do = Order(dve, order)
            if load is not None:
                nc.vector.memset(x[:, (NB - 1) * D:NB * D], 0.0).then_inc(cleared, 1)
                dve.wait_ge(loaded, 32)
            center(k, do, dve, x, rows, scratch, mean, rstd, 1e-5, sq_ready, squared, var_ready, rooted)
            scale_rows(k, rows, rstd).then_inc(ready, 1)

            def keep(j, s):
                dve.wait_ge(turned[s], j + 1)
                nc.vector.tensor_copy(k.hT[:, ds((2 * j + s) * P, P)], k.bank[s][:, 0:P]).then_inc(kept[s], 1)

            pipeline(dve, NB, [(0, keep)])
            do(nc.vector.tensor_scalar(rows, rows, 0.0, None, ALU.max)) if load is None else None


def node_tables(k, gathered_w, local_ws, gather_w, local_w, table, local, bias_rows, att, tag,
                records=None):
    nc = k.nc
    cut = Carver(k.work)
    w = cut(gather_w + local_w)
    bias = [cut(local_w) for _ in bias_rows]
    stage = [cut(P) for _ in range(2)]
    out = [cut(gather_w) for _ in range(2)]
    att_bc = cut(HD) if att is not None else None
    loaded, order, weights_set = k.sem(f"w{tag}_loaded"), k.sem(f"w{tag}_order"), k.sem(f"w{tag}_weights")
    names = ("staged", "done", "copied", "kept", "stored")
    staged, done, copied, kept, stored = ([k.sem(f"w{tag}_{n}{s}") for s in range(2)] for n in names)
    table3 = table.rearrange("(b p) d -> b p d", p=P)
    n_loads = len(gathered_w) + len(local_ws) + len(bias_rows) + (att is not None)
    with nc.Block() as block:
        @block.sync
        def _(sp):
            for at, group in ((0, gathered_w), (gather_w, local_ws)):
                for v in group:
                    sp.dma_start(w[:, at:at + v.shape[1]], v).then_inc(loaded, 16)
                    at += v.shape[1]
            for b, v in zip(bias, bias_rows):
                sp.dma_start(b[:, 0:v.shape[0]], v.partition_broadcast(P)).then_inc(loaded, 16)
            if att is not None:
                sp.dma_start(att_bc, att.rearrange("h d -> (h d)").partition_broadcast(P)).then_inc(loaded, 16)

            def store(j, s):
                sp.wait_ge(copied[s], j + 1)
                sp.dma_start(table3[ds(2 * j + s, 1), :, :].rearrange("o p d -> (o p) d"), out[s]).then_inc(stored[s], 16)

            pipeline(sp, NB, [(0, store)])
            for s in range(2):
                sp.wait_ge(stored[s], 16 * ((NB + 1 - s) // 2))

        if records is not None:
            @block.gpsimd
            def _(pool):
                records.write(pool, NORM_TURNS, TURNS)

        @block.tensor
        def _(pe):
            pe.wait_ge(weights_set, 1)

            def products(j, s):
                pe.wait_ge(staged[s], j + 1)
                if reused(j):
                    pe.wait_ge(copied[s], j)
                    pe.wait_ge(kept[s], j)
                nc.tensor.matmul(k.bank[s][:, 0:gather_w], stage[s], w[:, 0:gather_w], start=True, stop=True)
                nc.tensor.matmul(k.bank[2 + s][:, 0:local_w], stage[s], w[:, gather_w:gather_w + local_w],
                                 start=True, stop=True).then_inc(done[s], 1)

            pipeline(pe, NB, [(0, products)])

        @block.scalar
        def _(act):
            def take(j, s):
                if reused(j):
                    act.wait_ge(done[s], j)
                nc.scalar.copy(stage[s], k.hT[:, ds((2 * j + s) * P, P)]).then_inc(staged[s], 1)

            def copy(j, s):
                act.wait_ge(done[s], j + 1)
                if reused(j):
                    act.wait_ge(stored[s], 16 * j)
                nc.scalar.copy(out[s], k.bank[s][:, 0:gather_w]).then_inc(copied[s], 1)

            pipeline(act, NB, [(1, take), (0, copy)])

        @block.vector
        def _(dve):
            do = Order(dve, order)
            dve.wait_ge(loaded, 16 * n_loads)
            if bias_rows:
                do(nc.vector.tensor_tensor(bias[0][:, 0:HD], bias[0][:, 0:HD], bias[1][:, 0:HD], ALU.add))
            if att is not None:
                for v in (w[:, 0:HE], w[:, HE:2 * HE], bias[0]):
                    do(nc.vector.tensor_tensor(out[0][:, 0:HD], v[:, 0:HD], att_bc, ALU.mult))
                    do(nc.vector.tensor_reduce(v[:, HD:HE], out[0][:, 0:HD].rearrange("p (h d) -> p h d", h=H), AX_X,
                                               ALU.add))
            dve.sem_inc(weights_set, 1)

            def keep(j, s):
                dve.wait_ge(done[s], j + 1)
                to = local[:, ds((2 * j + s) * local_w, local_w)]
                if bias_rows:
                    nc.vector.tensor_tensor(to, k.bank[2 + s][:, 0:local_w], bias[0], ALU.add).then_inc(kept[s], 1)
                else:
                    nc.vector.tensor_copy(to, k.bank[2 + s][:, 0:local_w]).then_inc(kept[s], 1)

            pipeline(dve, NB, [(0, keep)])


def edge_scores(k, att, tag):
    nc = k.nc
    groups = T_DST // GS
    U = 8
    V = 4
    cut = Carver(k.wide)
    xg = [cut(GS * HE) for _ in range(U)]
    z = [cut(GS * HE) for _ in range(V)]
    z3 = [v.rearrange("p (u e) -> p u e", u=GS) for v in z]
    pick = [cut(GS * P) for _ in range(V)]
    lo_bc = [cut(GS * P // 2, BF16) for _ in range(V)]
    att_bc = cut(HD)
    part = [cut(GS * H) for _ in range(V)]
    index = [cut(GS, I32) for _ in range(U)]
    gathered = [k.gather_sem(f"a{tag}_gathered{s}") for s in range(U)]
    index_set, spilled = ([k.sem(f"a{tag}_{n}{s}") for s in range(U)] for n in ("index", "spilled"))
    lo_ready = [k.sem(f"a{tag}_lo{s}") for s in range(V)]
    tiled = [s for s in range(U) if s % 4 < 3]
    names = ("loaded", "order", "picked", "looked", "added", "weighed", "reduced", "scored")
    loaded, order, picked, looked, added, weighed, reduced, scored = (k.sem(f"a{tag}_{n}") for n in names)
    with nc.Block() as block:
        @block.gpsimd
        def _(pool):
            def gather(j, s):
                g = U * j + s
                pool.wait_ge(index_set[s], 16 * j + 16)
                if reused(j):
                    pool.wait_ge(added, GS * g - GS * U + GS)
                    if s in tiled:
                        pool.wait_ge(spilled[s], 16 * j)
                pool.nop(nofuse=True)
                for u in range(GS):
                    pool.indirect_dma_start(xg[s][:, u * HE:(u + 1) * HE], None, k.xl,
                                            bass.IndirectOffsetOnAxis(ap=index[s][:, u:u + 1], axis=0)).then_inc(gathered[s], 16)

            pipeline(pool, groups, [(0, gather)], U)

        @block.sync
        def _(sp):
            sp.dma_start(att_bc, att.rearrange("h d -> (h d)").partition_broadcast(P)).then_inc(loaded, 16)

            def load_keys(j, s):
                g = U * j + s
                if later(g, V):
                    sp.wait_ge(picked, g - V + 1)
                    sp.nop(nofuse=True)
                sp.dma_start(lo_bc[s % V], k.lo_slot[ds(g * (GS * P), GS * P)].partition_broadcast(P)
                             ).then_inc(lo_ready[s % V], 16)

            def load_index(j, s):
                g = U * j + s
                if reused(j):
                    sp.wait_ge(gathered[s], 16 * GS * j)
                    sp.nop(nofuse=True)
                sp.dma_start(index[s], k.gather_col[:, ds(g * GS, GS)]).then_inc(index_set[s], 16)

            def spill(j, s):
                if s not in tiled:
                    return
                sp.wait_ge(gathered[s], 16 * GS * j + 16 * GS)
                sp.dma_start(k.spill[ds((U * j + s) * GS, GS), :, :].rearrange("u p d -> p u d"),
                             xg[s].rearrange("p (u e) -> p u e", u=GS)[:, :, 0:HD]).then_inc(spilled[s], 16)

            pipeline(sp, groups, [(5, load_index), (3, load_keys), (0, spill)], U)
            for s in tiled:
                sp.wait_ge(spilled[s], 16 * (groups // U))

        @block.tensor
        def _(pe):
            def look(j, s):
                g = U * j + s
                word = block_words(k, PE, U // 2 * j + s // 2, 1)[0]
                columns = block_columns(pe, word, range(s % 2 * GS, s % 2 * GS + GS), HE)
                pe.wait_ge(picked, g + 1)
                if later(g, V):
                    pe.wait_ge(added, GS * (g - V) + GS)
                for u, at in enumerate(columns):
                    last = nc.tensor.matmul(k.bank[GS * (s % V) + u][:, 0:HE], pick[s % V][:, u * P:(u + 1) * P],
                                            k.node[:, ds(at, HE)], start=True, stop=True)
                last.then_inc(looked, 1)

            pipeline(pe, groups, [(0, look)], U)

        @block.scalar
        def _(act):
            def reduce(j, s):
                g = U * j + s
                act.wait_ge(weighed, g + 1)
                if later(g, V):
                    act.wait_ge(scored, g - V + 1)
                for u in range(GS):
                    for h in range(H):
                        at = z[s % V][:, u * HE + h * D:u * HE + (h + 1) * D]
                        last = nc.scalar.activation(at, at, ACT.Copy, accum_out=part[s % V][:, u * H + h:u * H + h + 1])
                last.then_inc(reduced, 1)

            pipeline(act, groups, [(0, reduce)], U)

        @block.vector
        def _(dve):
            do = Order(dve, order)
            do(nc.vector.memset(k.wcol[:, T_DST * H:TILES * H], 0.0))
            dve.wait_ge(loaded, 16)
            do(nc.vector.tensor_scalar(att_bc, att_bc, 1.0 - SLOPE, None, ALU.mult))

            def picks(j, s):
                g = U * j + s
                dve.wait_ge(lo_ready[s % V], 16 * (U // V * j + s // V) + 16)
                if later(g, V):
                    dve.wait_ge(looked, g - V + 1)
                nc.vector.tensor_scalar(pick[s % V], lo_bc[s % V], k.part_f[:, 0:1], None, ALU.is_equal).then_inc(picked, 1)

            def add(u):
                def fn(j, s):
                    g = U * j + s
                    if u == 0:
                        dve.wait_ge(gathered[s], 16 * GS * j + 16 * GS)
                        dve.wait_ge(looked, g + 1)
                        if later(g, V):
                            dve.wait_ge(scored, g - V + 1)
                    nc.vector.tensor_tensor(z[s % V][:, u * HE:(u + 1) * HE], k.bank[GS * (s % V) + u][:, 0:HE],
                                            xg[s][:, u * HE:(u + 1) * HE], ALU.add).then_inc(added, 1)
                return fn

            def weigh(j, s):
                g = U * j + s
                dve.wait_ge(added, GS * g + GS)
                zd = z3[s % V][:, :, 0:HD]
                nc.vector.scalar_tensor_tensor(out=zd, in0=zd, scalar=0.0, in1=att_bc.unsqueeze(1).to_broadcast([P, GS, HD]),
                                               op0=ALU.max, op1=ALU.mult).then_inc(weighed, 1)

            def score(j, s):
                g = U * j + s
                dve.wait_ge(reduced, g + 1)
                nc.vector.scalar_tensor_tensor(
                    out=k.wcol[:, ds(g * (GS * H), GS * H)].rearrange("p (u h) -> p u h", u=GS),
                    in0=z3[s % V][:, :, HD:HE], scalar=SLOPE, in1=part[s % V].rearrange("p (u h) -> p u h", u=GS),
                    op0=ALU.mult, op1=ALU.add).then_inc(scored, 1)

            pipeline(dve, groups, [(1, add(0)), (-2, score), (1, add(1)), (3, picks), (0, weigh)], U)


def segment_softmax(k, tag):
    nc = k.nc
    W = SLOTROW
    cut = Carver(k.wide)
    s_row, fwd, bwd = cut(H * W), cut(H * W), cut(H * W)
    whole = cut(1)
    rowkeep = [cut(H) for _ in range(2)]
    ends = [cut(H) for _ in range(2)]
    init = [cut(H) for _ in range(2)]
    keepT = [cut(P, F32, H) for _ in range(2)]
    endT = [cut(P, F32, H) for _ in range(2)]
    carry = [cut(P + 1, F32, H) for _ in range(2)]
    no = [cut(W) for _ in range(2)]
    keep = [k.keep_fwd[:, :], k.keep_bwd[:, :]]
    NBLK = H * TG
    names = ("order", "turned", "in", "ends", "endsT", "carry", "carryT", "shifted", "exp", "weights", "back")
    order, turned, taken, ends_set, endsT, carry_set, carryT, shifted, exped, weights_set, back = (
        k.sem(f"b{tag}_{n}") for n in names)
    by_slot = k.wcol[:, :].rearrange("p (t g h) -> p h g t", g=TG, h=H)
    quads = [range(q, min(q + 4, NBLK)) for q in range(0, NBLK, 4)]
    along = [lambda v: v, lambda v: v[:, ::-1]]
    with nc.Block() as block:
        @block.gpsimd
        def _(pool):
            nc.gpsimd.memset(k.node[:, 0:NB * HD], 0.0)

        @block.tensor
        def _(pe):
            for q, quad in enumerate(quads):
                for n in quad:
                    last = nc.tensor.transpose(k.bank[q][:, (n - quad[0]) * P:(n - quad[0] + 1) * P],
                                               by_slot[:, n // TG, n % TG, :], k.ident[:, :])
                last.then_inc(turned, 1)
            pe.wait_ge(taken, len(quads))
            for r in range(2):
                pe.wait_ge(ends_set, r + 1)
                for d in range(2):
                    nc.tensor.transpose(k.bank[0][0:H, d * P:(d + 1) * P], ends[d], k.ident[:, :])
                    last = nc.tensor.transpose(k.bank[0][0:H, (2 + d) * P:(3 + d) * P], rowkeep[d], k.ident[:, :])
                last.then_inc(endsT, 1)
                pe.wait_ge(carry_set, r + 1)
                for d in range(2):
                    last = nc.tensor.transpose(k.bank[1][:, d * H:(d + 1) * H], carry[d][:, d:d + P], k.ident[0:H, 0:H])
                last.then_inc(carryT, 1)
            pe.wait_ge(weights_set, 1)
            for q, quad in enumerate(quads):
                for n in quad:
                    last = nc.tensor.transpose(k.bank[2 + q][:, (n - quad[0]) * P:(n - quad[0] + 1) * P],
                                               s_row[:, n * P:(n + 1) * P], k.ident[:, :])
                last.then_inc(back, 1)

        @block.scalar
        def _(act):
            act.wait_ge(shifted, 1)
            nc.scalar.activation(s_row, s_row, ACT.Exp).then_inc(exped, 1)

        @block.vector
        def _(dve):
            do = Order(dve, order)
            for q, quad in enumerate(quads):
                dve.wait_ge(turned, q + 1)
                w = len(quad) * P
                nc.vector.tensor_copy(s_row[:, quad[0] * P:quad[0] * P + w], k.bank[q][:, 0:w]).then_inc(taken, 1)
            dve.wait_ge(taken, len(quads))
            for d in range(2):
                do(nc.vector.tensor_scalar(no[d], keep[d], -1.0, BIG, ALU.add, ALU.mult))
                do(nc.vector.tensor_reduce(whole, keep[d], AX_X, ALU.min))
                do(nc.vector.tensor_copy(rowkeep[d], whole.to_broadcast([P, H])))

            def both_ways(r, gate, empty, op0, op1):
                out = (fwd, bwd)
                for d in range(2):
                    for h in range(H):
                        row = slice(h * W, (h + 1) * W)
                        nc_scan = nc.vector.tensor_tensor_scan(along[d](out[d][:, row]), along[d](gate[d]),
                                                               along[d](s_row[:, row]), empty, op0, op1)
                        do(nc_scan)
                        end = h * W + (W - 1 if d == 0 else 0)
                        do(nc.vector.tensor_copy(ends[d][:, h:h + 1], out[d][:, end:end + 1]))
                dve.sem_inc(ends_set, 1)
                dve.wait_ge(endsT, r + 1)
                for d in range(2):
                    do(nc.vector.tensor_copy(endT[d], k.bank[0][0:H, d * P:(d + 1) * P]))
                    do(nc.vector.tensor_copy(keepT[d], k.bank[0][0:H, (2 + d) * P:(3 + d) * P]))
                    if r == 0:
                        do(nc.vector.tensor_scalar(keepT[d], keepT[d], -1.0, BIG, ALU.add, ALU.mult))
                    do(nc.vector.memset(carry[d], empty))
                    do(nc.vector.tensor_tensor_scan(along[d](carry[d][:, 1 - d:1 - d + P]), along[d](keepT[d]),
                                                    along[d](endT[d]), empty, op0, op1))
                dve.sem_inc(carry_set, 1)
                dve.wait_ge(carryT, r + 1)
                for d in range(2):
                    do(nc.vector.tensor_copy(init[d], k.bank[1][:, d * H:(d + 1) * H]))
                    for h in range(H):
                        row = slice(h * W, (h + 1) * W)
                        do(nc.vector.tensor_tensor_scan(along[d](out[d][:, row]), along[d](gate[d]),
                                                        along[d](s_row[:, row]), init[d][:, h:h + 1], op0, op1))

            both_ways(0, no, -BIG, ALU.add, ALU.max)
            do(nc.vector.tensor_tensor(fwd, fwd, bwd, ALU.max))
            nc.vector.tensor_tensor(s_row, s_row, fwd, ALU.subtract).then_inc(shifted, 1)
            dve.wait_ge(exped, 1)
            both_ways(1, keep, 0.0, ALU.mult, ALU.add)
            do(nc.vector.tensor_tensor(bwd, bwd, s_row, ALU.subtract))
            do(nc.vector.tensor_tensor(fwd, fwd, bwd, ALU.add))
            do(nc.vector.reciprocal(fwd, fwd))
            nc.vector.tensor_tensor(s_row, s_row, fwd, ALU.mult).then_inc(weights_set, 1)
            for q, quad in enumerate(quads):
                dve.wait_ge(back, q + 1)
                for n in quad:
                    last = nc.vector.tensor_copy(by_slot[:, n // TG, n % TG, :],
                                                 k.bank[2 + q][:, (n - quad[0]) * P:(n - quad[0] + 1) * P])
            do(last)


def aggregate(k, half, tag):
    nc = k.nc
    groups = T_DST // G
    U = 4
    turns = groups // U
    cut = Carver(k.wide)
    row_w = [HE if s % 2 else HD for s in range(U)]
    xg = [cut(G * w) for w in row_w]
    xw = [cut(G * HD) for _ in range(2)]
    place = [cut(G * P) for _ in range(2)]
    index = [cut(GS, I32) for _ in range(2)]
    rec = [cut(CU, I32, EC).rearrange("p (u f) -> p u f", f=2) for _ in range(2)]
    slot = [cut(CU // 2, I32, EC) for _ in range(2)]
    written = [k.gather_sem(f"g{tag}_written{s}") for s in range(2)]
    gathered = [k.gather_sem(f"g{tag}_gathered{s}") for s in range(2)]
    index_set = [k.sem(f"g{tag}_index{s}") for s in range(2)]
    loaded = [k.sem(f"g{tag}_loaded{s}") for s in range(U)]
    names = ("staged", "placed", "weighed", "summed", "added_part0", "added_part1")
    staged, placed, weighed, summed, *added = (k.sem(f"g{tag}_{n}") for n in names)
    by_scalar = H - 1
    cols = COLS // 2
    scatter_turns = cols // CU

    def rows_in(eng, j, s, u):
        if u == 0:
            eng.wait_ge(loaded[s], 16 * j + 16)
        if u == GS and s % 2:
            eng.wait_ge(gathered[s // 2], 16 * GS * j + 16 * GS)

    with nc.Block() as block:
        @block.gpsimd
        def _(pool):
            def gather(j, n):
                s = 2 * n + 1
                pool.wait_ge(index_set[n], 16 * j + 16)
                if reused(j):
                    pool.wait_ge(weighed, U * j + s - U + 1)
                    pool.wait_ge(placed, U * j + s - U + 1)
                pool.nop(nofuse=True)
                for u in range(GS):
                    at = (GS + u) * HE
                    pool.indirect_dma_start(xg[s][:, at:at + HE], None, k.xl,
                                            bass.IndirectOffsetOnAxis(ap=index[n][:, u:u + 1], axis=0)).then_inc(gathered[n], 16)

            def both(j):
                for n in range(2):
                    gather(j, n)
                    scatter_columns(k, pool, k.pos_s, k.rec_s, rec[n], slot[n], staged, written[n], j, n,
                                    CU // 2, half * cols)

            both(0)
            with pool.Fori(1, scatter_turns) as i:
                both(i)
            with pool.Fori(scatter_turns, turns) as i:
                for n in range(2):
                    gather(i, n)
            for n in range(2):
                pool.wait_ge(written[n], 16 * (CU // 2) * scatter_turns)

        @block.sync
        def _(sp):
            def load(j, s):
                g = U * j + s
                tiles = GS if s % 2 else G
                if later(g, U):
                    sp.wait_ge(weighed, g - U + 1)
                    sp.nop(nofuse=True)
                    sp.wait_ge(placed, g - U + 1)
                    sp.nop(nofuse=True)
                sp.dma_start(xg[s].rearrange("p (u d) -> p u d", u=G)[:, 0:tiles, 0:HD],
                             k.spill[ds(g * G, tiles), :, :].rearrange("u p d -> p u d")).then_inc(loaded[s], 16)
                if s % 2:
                    sp.dma_start(index[s // 2], k.gather_col[:, ds(g * G + GS, GS)]).then_inc(index_set[s // 2], 16)

            pipeline(sp, groups, [(0, load)], U)

        @block.scalar
        def _(act):
            def weigh(j, s):
                g = U * j + s
                rows_in(act, j, s, 0)
                rows_in(act, j, s, GS)
                if later(g, 2):
                    act.wait_ge(summed, g - 1)
                for u in range(G):
                    for h in range(by_scalar):
                        at, to = u * row_w[s] + h * D, u * HD + h * D
                        last = nc.scalar.activation(xw[s % 2][:, to:to + D], xg[s][:, at:at + D], ACT.Copy,
                                                    scale=k.wcol[:, ds((g * G + u) * H + h, 1)])
                last.then_inc(weighed, 1)

            pipeline(act, groups, [(0, weigh)], U)

        @block.tensor
        def _(pe):
            def sums(j, s):
                g = U * j + s
                pe.wait_ge(placed, g + 1)
                if later(g, 2):
                    for part in range(2):
                        pe.wait_ge(added[part], G * g - G)
                pe.wait_ge(weighed, g + 1)
                for u in range(G):
                    last = nc.tensor.matmul(k.bank[G * (s % 2) + u][:, 0:HD], place[s % 2][:, u * P:(u + 1) * P],
                                            xw[s % 2][:, u * HD:(u + 1) * HD], start=True, stop=True)
                last.then_inc(summed, 1)

            pipeline(pe, groups, [(0, sums)], U)

        @block.vector
        def _(dve):
            words, columns, tile, tile_ahead = [], [], [], []

            def find_columns(j, s):
                if s == 0:
                    words[:] = block_words(k, DVE, U * j, U)
                columns[:] = block_columns(dve, words[s], range(G), HD)
                tile[:] = [snapped(dve, (U * j + s) * G)]

            def add(u):
                def fn(j, s):
                    g = U * j + s
                    if u == 0:
                        dve.wait_ge(summed, g + 1)
                    for part, (c0, c1) in enumerate(((0, 2 * D), (2 * D, HD))):
                        if u > 0 or later(g):
                            dve.wait_ge(added[part], tile[0] + u)
                        acc = k.node[:, ds(columns[u] + c0, c1 - c0)]
                        nc.vector.tensor_tensor(acc, acc, k.bank[G * (s % 2) + u][:, c0:c1], ALU.add
                                                ).then_inc(added[part], 1)
                return fn

            def places(u):
                def fn(j, s):
                    g = U * j + s
                    if u == 0:
                        tile_ahead[:] = [snapped(dve, G * g)]
                        if later(g, 2):
                            dve.wait_ge(summed, g - 1)
                    key_rows(k, place[s % 2][:, u * P:(u + 2) * P], tile_ahead[0] + u, 2)
                return fn

            def weigh(u):
                def fn(j, s):
                    rows_in(dve, j, s, u)
                    weight = k.wcol[:, :].rearrange("p (t h) -> p t h", h=H)[:, ds(tile_ahead[0] + u, 2), by_scalar:H]
                    rows = [v.rearrange("p (u d) -> p u d", u=G)[:, u:u + 2, by_scalar * D:HD] for v in (xw[s % 2], xg[s])]
                    last = nc.vector.tensor_tensor(rows[0], rows[1], weight.to_broadcast([P, 2, D]), ALU.mult)
                    if u == 2:
                        last.then_inc(placed, 1)
                return fn

            pipeline(dve, groups, [(0, find_columns), (0, add(0)), (2, places(0)), (0, add(1)), (2, weigh(0)), (0, add(2)),
                                   (2, places(2)), (0, add(3)), (2, weigh(2))], U)


def load_cols(nc, sp, cols, sources, loaded):
    with nc.allow_non_contiguous_dma(reason="one word per partition"):
        for n, v in enumerate(sources):
            sp.dma_start(cols[:, n:n + 1], v.rearrange("(p o) -> p o", o=1)).then_inc(loaded, 16)


def node_layer(k, row_biases, mats, outs, tag):
    nc = k.nc
    cut = Carver(k.work)
    M = len(mats)
    bias = [cut(HD) for _ in row_biases]
    w = cut(M * HD)
    col = cut(M)
    rows = [cut(HD) for _ in range(2)]
    turned_rows = [cut(HD) for _ in range(2)]
    loaded, order = k.sem(f"m{tag}_loaded"), k.sem(f"m{tag}_order")
    names = ("rows", "turned", "copied", "done", "kept")
    rows_set, turned, copied, done, kept = ([k.sem(f"m{tag}_{n}{s}") for s in range(2)] for n in names)
    col_biases = [v for _, v, _ in outs if v is not None]
    n_loads = M + len(row_biases) + len(col_biases)
    with nc.Block() as block:
        @block.sync
        def _(sp):
            for b, v in zip(bias, row_biases):
                sp.dma_start(b, v.partition_broadcast(P)).then_inc(loaded, 16)
            for m, v in enumerate(mats):
                sp.dma_start(w[:, m * HD:(m + 1) * HD].rearrange("p (h n) -> p h n", h=H),
                             v.rearrange("(h p) n -> p h n", p=P)).then_inc(loaded, 16)
            load_cols(nc, sp, col, col_biases, loaded)

        @block.tensor
        def _(pe):
            pe.wait_ge(loaded, 16 * n_loads)

            def turn(j, s):
                pe.wait_ge(rows_set[s], j + 1)
                if reused(j):
                    pe.wait_ge(copied[s], j)
                for h in range(H):
                    last = nc.tensor.transpose(k.bank[s][:, h * P:(h + 1) * P], rows[s][:, h * P:(h + 1) * P], k.ident[:, :])
                last.then_inc(turned[s], 1)

            def products(j, s):
                pe.wait_ge(copied[s], j + 1)
                if reused(j):
                    pe.wait_ge(kept[s], j)
                for m in range(M):
                    for h in range(H):
                        last = nc.tensor.matmul(k.bank[2 + s][:, m * P:(m + 1) * P], w[:, (m * H + h) * P:(m * H + h + 1) * P],
                                                turned_rows[s][:, h * P:(h + 1) * P], start=(h == 0), stop=(h == H - 1))
                last.then_inc(done[s], 1)

            pipeline(pe, NB, [(1, turn), (0, products)])

        @block.scalar
        def _(act):
            def copy(j, s):
                act.wait_ge(turned[s], j + 1)
                if reused(j):
                    act.wait_ge(done[s], j)
                nc.scalar.copy(turned_rows[s], k.bank[s][:, 0:HD]).then_inc(copied[s], 1)

            pipeline(act, NB, [(0, copy)])

        @block.vector
        def _(dve):
            do = Order(dve, order)
            dve.wait_ge(loaded, 16 * n_loads)
            do(nc.vector.tensor_tensor(bias[0], bias[0], bias[1], ALU.add))

            def biased(j, s):
                if reused(j):
                    dve.wait_ge(turned[s], j)
                nc.vector.tensor_tensor(rows[s], k.node[:, ds((2 * j + s) * HD, HD)], bias[0], ALU.add).then_inc(rows_set[s], 1)

            def keep(j, s):
                dve.wait_ge(done[s], j + 1)
                c = 0
                for m, (area, v, adds) in enumerate(outs):
                    to = area[:, ds((2 * j + s) * P, P)]
                    ps = k.bank[2 + s][:, m * P:(m + 1) * P]
                    if adds:
                        last = nc.vector.tensor_tensor(to, to, ps, ALU.add)
                    else:
                        last = nc.vector.tensor_scalar(to, ps, col[:, c:c + 1], None, ALU.add)
                        c += 1
                last.then_inc(kept[s], 1)

            pipeline(dve, NB, [(2, biased), (0, keep)])


def batch_norm(k, y, gamma, beta, scale, shift, tag):
    nc = k.nc
    cut = Carver(k.work[:, 0:400])
    CH = 250
    stats, agg, cols = cut(N // CH * 6), cut(2), cut(2)
    assert N % CH == 0
    loaded, order, rooted, var_set = (k.sem(f"v{tag}_{n}") for n in ("loaded", "order", "rooted", "var"))
    with nc.Block() as block:
        @block.sync
        def _(sp):
            load_cols(nc, sp, cols, (gamma, beta), loaded)

        @block.scalar
        def _(act):
            act.wait_ge(var_set, 1)
            nc.scalar.activation(scale, scale, ACT.Sqrt).then_inc(rooted, 1)

        @block.vector
        def _(dve):
            do = Order(dve, order)
            for c in range(N // CH):
                last = nc.vector.bn_stats(stats[:, 6 * c:6 * c + 6], y[:, c * CH:(c + 1) * CH])
            do(last)
            do(nc.vector.bn_aggr(agg, stats))
            nc.vector.tensor_scalar(scale, agg[:, 1:2], 1e-5, None, ALU.add).then_inc(var_set, 1)
            dve.wait_ge(rooted, 1)
            do(nc.vector.reciprocal(scale, scale))
            dve.wait_ge(loaded, 32)
            do(nc.vector.tensor_tensor(scale, scale, cols[:, 0:1], ALU.mult))
            do(nc.vector.tensor_tensor(shift, agg[:, 0:1], scale, ALU.mult))
            do(nc.vector.tensor_tensor(shift, cols[:, 1:2], shift, ALU.subtract))


def gat_layer(k, io, n, records=None):
    w = {m: io[f"L0_gnn_{m}{n}"] for m in ("Wl", "Wr", "bl", "br", "att")}
    node_tables(k, (w["Wl"],), (w["Wr"],), HE, HE, k.xl, k.node, (w["bl"], w["br"]), w["att"], f"{n}",
                records)
    if records is not None:
        slot_tables(k, k.rec_d, k.block_d, 0, 1, True, "d")
        k.recycle()
    edge_scores(k, w["att"], n)
    segment_softmax(k, n)
    aggregate(k, n - 1, n)


def relu_in_place(k, scale, shift, tag):
    nc = k.nc
    done = k.sem(f"u{tag}_done")
    with nc.Block() as block:
        @block.scalar
        def _(act):
            nc.scalar.activation(k.hT, k.hT, ACT.Relu, bias=shift, scale=scale).then_inc(done, 1)
            act.wait_ge(done, 1)


def residual_rows(k, io, scale, shift):
    nc = k.nc
    cut = Carver(k.work)
    stage = [cut(P) for _ in range(2)]
    xr = k.hT
    loaded, cleared = k.sem("e_loaded"), k.sem("e_cleared")
    staged, turned, kept = ([k.sem(f"e_{n}{s}") for s in range(2)] for n in ("staged", "turned", "kept"))
    with nc.Block() as block:
        @block.sync
        def _(sp):
            sp.wait_ge(cleared, 1)
            load_nodes(sp, io["x"], xr, loaded)

        @block.scalar
        def _(act):
            def relu(j, s):
                if reused(j):
                    act.wait_ge(turned[s], j)
                nc.scalar.activation(stage[s], k.y2[:, ds((2 * j + s) * P, P)], ACT.Relu, bias=shift,
                                     scale=scale).then_inc(staged[s], 1)

            pipeline(act, NB, [(0, relu)])

        @block.tensor
        def _(pe):
            def turn(j, s):
                pe.wait_ge(staged[s], j + 1)
                if reused(j):
                    pe.wait_ge(kept[s], j)
                nc.tensor.transpose(k.bank[s][:, 0:P], stage[s], k.ident[:, :]).then_inc(turned[s], 1)

            pipeline(pe, NB, [(0, turn)])

        @block.vector
        def _(dve):
            nc.vector.memset(xr[:, (NB - 1) * D:NB * D], 0.0).then_inc(cleared, 1)
            dve.wait_ge(loaded, 32)

            def add(j, s):
                at = ds((2 * j + s) * P, P)
                dve.wait_ge(turned[s], j + 1)
                nc.vector.tensor_tensor(k.y2[:, at], k.bank[s][:, 0:P], xr[:, at], ALU.add).then_inc(kept[s], 1)

            pipeline(dve, NB, [(0, add)])


def edge_attention(k, q_area, acc):
    nc = k.nc
    groups = T_SRC // G
    U = 4
    cut = Carver(k.wide)
    kv = [cut(G * KV) for _ in range(U)]
    prod = [cut(G * D) for _ in range(2)]
    pick = [cut(G * P) for _ in range(2)]
    place = [cut(G * P) for _ in range(2)]
    lo_bc = [cut(G * P // 2, BF16) for _ in range(U)]
    att = [cut(G * LH) for _ in range(2)]
    wv = [cut(G * VW) for _ in range(2)]
    w4 = [v.rearrange("p (u w) -> p u w", u=G) for v in wv]
    index = [cut(G, I32) for _ in range(U)]
    gathered = [k.gather_sem(f"f_gathered{s}") for s in range(U)]
    index_set, lo_ready = ([k.sem(f"f_{n}{s}") for s in range(U)] for n in ("index", "lo"))
    names = ("picked", "looked", "mult", "att", "clip", "exp", "weighed", "summed", "added")
    picked, looked, multiplied, att_set, clipped, exped, weighed, summed, added = (k.sem(f"f_{n}") for n in names)
    with nc.Block() as block:
        @block.gpsimd
        def _(pool):
            def gather(j, s):
                g = U * j + s
                pool.wait_ge(index_set[s], 16 * j + 16)
                if later(g, U):
                    pool.wait_ge(weighed, g - U + 1)
                pool.nop(nofuse=True)
                for u in range(G):
                    pool.indirect_dma_start(kv[s][:, u * KV:(u + 1) * KV], None, k.kv,
                                            bass.IndirectOffsetOnAxis(ap=index[s][:, u:u + 1], axis=0)).then_inc(gathered[s], 16)

            pipeline(pool, groups, [(0, gather)], U)

        @block.sync
        def _(sp):
            def load(j, s):
                g = U * j + s
                if reused(j):
                    sp.wait_ge(gathered[s], 16 * G * j)
                    sp.nop(nofuse=True)
                    sp.wait_ge(picked, g - U + 1)
                    sp.nop(nofuse=True)
                sp.dma_start(lo_bc[s], k.lo_slot[ds(g * (G * P), G * P)].partition_broadcast(P)).then_inc(lo_ready[s], 16)
                sp.dma_start(index[s], k.gather_col[:, ds(g * G, G)]).then_inc(index_set[s], 16)

            pipeline(sp, groups, [(0, load)], U)

        @block.tensor
        def _(pe):
            def look(j, s):
                g = U * j + s
                columns = block_columns(pe, block_words(k, PE, g, 1)[0], range(G), D)
                pe.wait_ge(picked, g + 1)
                if later(g, 2):
                    pe.wait_ge(multiplied, g - 1)
                for u, at in enumerate(columns):
                    last = nc.tensor.matmul(k.bank[s % 2][:, u * P:(u + 1) * P], pick[s % 2][:, u * P:(u + 1) * P],
                                            q_area[:, ds(at, D)], start=True, stop=True)
                last.then_inc(looked, 1)

            def sums(j, s):
                g = U * j + s
                pe.wait_ge(weighed, g + 1)
                if later(g):
                    pe.wait_ge(added, G * g)
                for u in range(G):
                    nc.tensor.matmul(k.bank[2 + u][:, 0:VW], place[s % 2][:, u * P:(u + 1) * P],
                                     wv[s % 2][:, u * VW:(u + 1) * VW], start=True, stop=True).then_inc(summed, 1)

            pipeline(pe, groups, [(2, look), (0, sums)], U)

        @block.scalar
        def _(act):
            def weights(j, s):
                g = U * j + s
                act.wait_ge(clipped, g + 1)
                if later(g, 2):
                    act.wait_ge(summed, G * g - G)
                nc.scalar.activation(w4[s % 2][:, :, D:VW], att[s % 2].rearrange("p (u h) -> p u h", u=G),
                                     ACT.Exp).then_inc(exped, 1)

            pipeline(act, groups, [(0, weights)], U)

        @block.vector
        def _(dve):
            def picks(j, s, g):
                dve.wait_ge(lo_ready[s], 16 * j + 16)
                if later(g, 2):
                    dve.wait_ge(looked, g - 1)
                nc.vector.tensor_scalar(pick[s % 2], lo_bc[s], k.part_f[:, 0:1], None, ALU.is_equal).then_inc(picked, 1)

            def multiply(j, s, g):
                dve.wait_ge(gathered[s], 16 * G * j + 16 * G)
                dve.wait_ge(looked, g + 1)
                keys = kv[s].rearrange("p (u d) -> p u d", u=G)[:, :, 0:D]
                if later(g, 2):
                    dve.wait_ge(att_set, g - 1)
                nc.vector.tensor_tensor(prod[s % 2].rearrange("p (u d) -> p u d", u=G), keys,
                                        k.bank[s % 2][:, 0:G * D].rearrange("p (u d) -> p u d", u=G),
                                        ALU.mult).then_inc(multiplied, 1)

            def reduce(j, s, g):
                dve.wait_ge(multiplied, g + 1)
                if later(g, 2):
                    dve.wait_ge(exped, g - 1)
                nc.vector.tensor_reduce(att[s % 2], prod[s % 2].rearrange("p (q d) -> p q d", d=D // LH), AX_X,
                                        ALU.add).then_inc(att_set, 1)

            def clip(j, s, g):
                dve.wait_ge(att_set, g + 1)
                nc.vector.tensor_scalar(att[s % 2], att[s % 2], -10.0, 10.0, ALU.max, ALU.min).then_inc(clipped, 1)

            def places(j, s, g):
                first = snapped(dve, g * G)
                if later(g, 2):
                    dve.wait_ge(summed, first - G)
                key_rows(k, place[s % 2], first, G)

            def weigh(j, s, g):
                dve.wait_ge(exped, g + 1)
                ex = w4[s % 2][:, :, D:VW].unsqueeze(3).to_broadcast([P, G, LH, D // LH])
                v4 = kv[s].rearrange("p (u d) -> p u d", u=G)[:, :, D:KV].rearrange("p u (h d) -> p u h d", h=LH)
                nc.vector.tensor_tensor(w4[s % 2][:, :, 0:D].rearrange("p u (h d) -> p u h d", h=LH), v4, ex,
                                        ALU.mult).then_inc(weighed, 1)

            words, columns, tile = [], [], []

            def find_columns(j, s, g):
                if s == 0:
                    words[:] = block_words(k, DVE, U * j, U)
                columns[:] = block_columns(dve, words[s], range(G), VW)
                tile[:] = [snapped(dve, g * G)]

            def add(u):
                def fn(j, s, g):
                    dve.wait_ge(summed, tile[0] + (u + 1))
                    if u > 0 or later(g):
                        dve.wait_ge(added, tile[0] + u)
                    to = acc[:, ds(columns[u], VW)]
                    nc.vector.tensor_tensor(to, to, k.bank[2 + u][:, 0:VW], ALU.add).then_inc(added, 1)
                return fn

            pipeline(dve, groups, [(2, multiply), (0, find_columns), (0, add(0)), (2, reduce), (0, add(1)),
                                   (1, places), (0, add(2)), (2, clip), (4, picks), (0, add(3)), (1, weigh)], U, True)


def finish(k, io, acc, h, x, scratch, square):
    nc = k.nc
    cut = Carver(k.work)
    mean, rstd, recip = cut(NB), cut(NB), cut(NB * LH)
    gain, bias = cut(D), cut(D)
    names = ("loaded", "order", "sq_ready", "squared", "var", "rooted", "ready", "stored")
    loaded, order, sq_ready, squared, var_ready, rooted, ready, stored = (k.sem(f"z_{n}") for n in names)
    acc3 = acc.rearrange("p (b w) -> p b w", w=VW)
    rows = scratch
    rows3 = rows.rearrange("p (b d) -> p b d", d=D)
    with nc.Block() as block:
        @block.sync
        def _(sp):
            sp.dma_start(gain, io["L1_gnn_ln_scale"].partition_broadcast(P)).then_inc(loaded, 16)
            sp.dma_start(bias, io["L1_gnn_ln_bias"].partition_broadcast(P)).then_inc(loaded, 16)
            sp.wait_ge(ready, 1)
            whole = (NB - 1) * P
            sp.dma_start(io["out"][0:whole, :].rearrange("(b p) d -> p b d", p=P),
                         rows[:, 0:(NB - 1) * D].rearrange("p (b d) -> p b d", d=D)).then_inc(stored, 16)
            sp.dma_start(io["out"][whole:N, :], rows[0:TAIL, (NB - 1) * D:NB * D]).then_inc(stored, 16)
            sp.wait_ge(stored, 32)

        @block.scalar
        def _(act):
            act.wait_ge(sq_ready, 1)
            nc.scalar.activation(square, rows, ACT.Square).then_inc(squared, 1)
            act.wait_ge(var_ready, 1)
            nc.scalar.activation(rstd, rstd, ACT.Sqrt).then_inc(rooted, 1)

        @block.vector
        def _(dve):
            do = Order(dve, order)
            r3 = recip.rearrange("p (b h) -> p b h", h=LH)
            do(nc.vector.tensor_scalar(r3, acc3[:, :, D:VW], 1e-8, None, ALU.add))
            do(nc.vector.reciprocal(recip, recip))
            do(nc.vector.tensor_tensor(rows3.rearrange("p b (h d) -> p b h d", h=LH),
                                       acc3[:, :, 0:D].rearrange("p b (h d) -> p b h d", h=LH),
                                       r3.unsqueeze(3).to_broadcast([P, NB, LH, D // LH]), ALU.mult))
            do(nc.vector.tensor_tensor(rows, rows, h, ALU.add))
            center(k, do, dve, rows, rows, square, mean, rstd, 1e-6, sq_ready, squared, var_ready, rooted)
            do(scale_rows(k, rows, rstd))
            dve.wait_ge(loaded, 32)
            do(nc.vector.tensor_tensor(rows3, rows3, gain.unsqueeze(1).to_broadcast([P, NB, D]), ALU.mult))
            do(nc.vector.tensor_tensor(rows3, rows3, bias.unsqueeze(1).to_broadcast([P, NB, D]), ALU.add))
            nc.vector.tensor_tensor(rows, rows, x, ALU.add).then_inc(ready, 1)


def program(nc, io):
    with ExitStack() as ctx:
        k = Core(nc, ctx)
        g = {n: io[f"L0_gnn_{n}"] for n in ("bl1", "bc1", "g1", "be1", "bl2", "bc2", "g2", "be2", "W1", "b1", "W2", "b2")}
        scale = ctx.enter_context(nc.sbuf_tensor("bn_scale", [P, 1], F32))
        shift = ctx.enter_context(nc.sbuf_tensor("bn_shift", [P, 1], F32))
        constants(k, io)
        records = sort_by_dst(k, io, SortBySrc(k))

        norm_to_features(k, k.y2, k.node[:, 0:NPAD], k.node[:, NPAD:2 * NPAD], io["x"], "0", records)
        gat_layer(k, io, 1, records)
        node_layer(k, (g["bl1"], g["bc1"]), (g["W1"], g["W2"][HD:2 * HD, :]),
                   ((k.hT, g["b1"], False), (k.y2, g["b2"], False)), "1")
        batch_norm(k, k.hT, g["g1"], g["be1"], scale[:, :], shift[:, :], "1")
        relu_in_place(k, scale[:, 0:1], shift[:, 0:1], "1")

        k.recycle()

        gat_layer(k, io, 2)
        node_layer(k, (g["bl2"], g["bc2"]), (g["W2"][0:HD, :],), ((k.y2, None, True),), "2")
        batch_norm(k, k.y2, g["g2"], g["be2"], scale[:, :], shift[:, :], "2")
        residual_rows(k, io, scale[:, 0:1], shift[:, 0:1])

        k.recycle()

        q_area, acc, h = k.node[:, 0:NPAD], k.node[:, NPAD:NPAD + NB * VW], k.node[:, NPAD + NB * VW:2 * NPAD + NB * VW]
        norm_to_features(k, k.y2, h, q_area, None, "3")
        node_tables(k, (io["L1_gnn_kTrans"], io["L1_gnn_vTrans"]), (io["L1_gnn_qTrans"],), KV, D, k.kv, q_area, (), None, "3")
        slot_tables(k, k.rec_s, k.block_s, 1, 0, False, "s", acc)
        edge_attention(k, q_area, acc)
        finish(k, io, acc, h, k.y2, q_area, k.hT)


_INS = ["x", "src", "dst"] + [f"L0_gnn_{n}" for n in (
    "Wl1", "bl1", "Wr1", "br1", "att1", "bc1", "g1", "be1", "Wl2", "bl2", "Wr2", "br2", "att2", "bc2", "g2", "be2",
    "W1", "b1", "W2", "b2")] + [f"L1_gnn_{n}" for n in ("qTrans", "kTrans", "vTrans", "ln_scale", "ln_bias")]


def kernel(**inputs):
    import numpy as np
    import concourse.bacc as bacc
    from concourse.bass_utils import run_bass_kernel_spmd

    nc = bacc.Bacc("TRN2", target_bir_lowering=False, num_devices=1)
    arrays, io = {}, {}
    for name in _INS:
        a = np.ascontiguousarray(inputs[name])
        arrays[f"in_{name}"] = a
        io[name] = nc.dram_tensor(f"in_{name}", a.shape, mybir.dt.from_np(a.dtype), kind="ExternalInput").ap()
    io["out"] = nc.dram_tensor("out_0", (N, D), F32, kind="ExternalOutput").ap()
    program(nc, io)
    r = run_bass_kernel_spmd(nc, [arrays], core_ids=[0])
    return r.results[0]["out_0"]
```
